# Optimizing a Trainium2 kernel written in Bass

```python
import numpy as np
import jax
import jax.numpy as jnp

def _softmax(x, axis=-1):
    return jax.nn.softmax(x, axis=axis)

def _gelu(x):
    return jax.nn.gelu(x, approximate=True)

def _silu(x):
    return jax.nn.silu(x)

def _sigmoid(x):
    return jax.nn.sigmoid(x)

def _layernorm(x, axis=-1, eps=1e-05):
    m = jnp.mean(x, axis=axis, keepdims=True)
    v = jnp.var(x, axis=axis, keepdims=True)
    return (x - m) / jnp.sqrt(v + eps)

def _scatter_add(tgt, idx, src, axis=0):
    return tgt.at[idx].add(src)

def _segment_sum(src, seg, n):
    return jax.ops.segment_sum(src, seg, n)
kernel_name = 'mk_macaron_d1_jaxref_r8_9f22a4'

def setup_inputs(seed: int=0):
    np.random.seed(seed)
    _w = jnp.asarray

    def _L0_attn_setup():
        import jax, jax.numpy as jnp
        import numpy as np
        N_HEAD = 32
        ROPE_BASE = 10000.0

        def _rope_cos_sin(T, n_elem, dtype):
            theta = 1.0 / ROPE_BASE ** (jnp.arange(0, n_elem, 2, dtype=dtype) / n_elem)
            seq_idx = jnp.arange(T, dtype=dtype)
            idx_theta = jnp.outer(seq_idx, theta)
            idx_theta2 = jnp.concatenate([idx_theta, idx_theta], axis=-1)
            return (jnp.cos(idx_theta2), jnp.sin(idx_theta2))

        def _apply_rope(x, cos, sin):
            d2 = x.shape[-1] // 2
            rot = jnp.concatenate([-x[..., d2:], x[..., :d2]], axis=-1)
            return x * cos + rot * sin
        key = jax.random.key(seed)
        k1, k2, k3, k4 = jax.random.split(key, 4)
        B, T, C = (1, 256, 512)
        s_in = 1.0 / np.sqrt(C)
        return {'x': jax.random.normal(k1, (B, T, C), jnp.float32), 'w_attn': jax.random.normal(k2, (3 * C, C), jnp.float32) * s_in, 'w_proj': jax.random.normal(k3, (C, C), jnp.float32) * s_in, 'adapter_wte': jax.random.normal(k4, (10, C), jnp.float32), 'gating': jnp.ones((1,), jnp.float32)}
    _L0_attn_in = _L0_attn_setup()

    def _L0_ffn_setup():
        import jax, jax.numpy as jnp
        import numpy as np
        HIDDEN = 512
        INTER = 1376

        def _ternary_quantize(w):
            scale = jnp.mean(jnp.abs(w))
            return jnp.clip(jnp.round(w / scale), -1.0, 1.0) * scale
        key = jax.random.key(seed)
        kx, kg, ku, kd = jax.random.split(key, 4)
        x = jax.random.normal(kx, (2, 256, HIDDEN), dtype=jnp.float32)
        w_gate = _ternary_quantize(jax.random.normal(kg, (INTER, HIDDEN), dtype=jnp.float32) * 0.02)
        w_up = _ternary_quantize(jax.random.normal(ku, (INTER, HIDDEN), dtype=jnp.float32) * 0.02)
        w_down = _ternary_quantize(jax.random.normal(kd, (HIDDEN, INTER), dtype=jnp.float32) * 0.02)
        return {'x': x, 'w_gate': w_gate, 'w_up': w_up, 'w_down': w_down}
    _L0_ffn_in = _L0_ffn_setup()
    _d = {'L0_attn_x': _L0_attn_in['x'], 'L0_attn_w_attn': _L0_attn_in['w_attn'], 'L0_attn_w_proj': _L0_attn_in['w_proj'], 'L0_attn_adapter_wte': _L0_attn_in['adapter_wte'], 'L0_attn_gating': _L0_attn_in['gating'], 'L0_ffn_w_gate': _L0_ffn_in['w_gate'], 'L0_ffn_w_up': _L0_ffn_in['w_up'], 'L0_ffn_w_down': _L0_ffn_in['w_down']}
    _x0 = _d['L0_attn_x']
    _d['L0_attn_x'] = jax.random.normal(jax.random.fold_in(jax.random.key(seed), 1), (4, 512, 512), dtype=_x0.dtype)
    del _x0
    return _d

def reference(L0_attn_x, L0_attn_w_attn, L0_attn_w_proj, L0_attn_adapter_wte, L0_attn_gating, L0_ffn_w_gate, L0_ffn_w_up, L0_ffn_w_down):

    def _L0_attn_ref(x, w_attn, w_proj, adapter_wte, gating):
        import jax, jax.numpy as jnp
        import numpy as np
        N_HEAD = 32
        ROPE_BASE = 10000.0

        def _rope_cos_sin(T, n_elem, dtype):
            theta = 1.0 / ROPE_BASE ** (jnp.arange(0, n_elem, 2, dtype=dtype) / n_elem)
            seq_idx = jnp.arange(T, dtype=dtype)
            idx_theta = jnp.outer(seq_idx, theta)
            idx_theta2 = jnp.concatenate([idx_theta, idx_theta], axis=-1)
            return (jnp.cos(idx_theta2), jnp.sin(idx_theta2))

        def _apply_rope(x, cos, sin):
            d2 = x.shape[-1] // 2
            rot = jnp.concatenate([-x[..., d2:], x[..., :d2]], axis=-1)
            return x * cos + rot * sin
        B, T, C = x.shape
        H = N_HEAD
        hd = C // H
        qkv = jnp.einsum('btc,oc->bto', x, w_attn)
        q, k, v = jnp.split(qkv, 3, axis=-1)
        q = q.reshape(B, T, H, hd).transpose(0, 2, 1, 3)
        k = k.reshape(B, T, H, hd).transpose(0, 2, 1, 3)
        v = v.reshape(B, T, H, hd).transpose(0, 2, 1, 3)
        cos, sin = _rope_cos_sin(T, hd, x.dtype)
        q = _apply_rope(q, cos, sin)
        k = _apply_rope(k, cos, sin)
        scores = jnp.einsum('bhqd,bhkd->bhqk', q, k) / jnp.sqrt(jnp.asarray(hd, x.dtype))
        causal = jnp.tril(jnp.ones((T, T), bool))
        scores = jnp.where(causal, scores, jnp.asarray(-jnp.inf, x.dtype))
        attn = jax.nn.softmax(scores, axis=-1)
        y = jnp.einsum('bhqk,bhkd->bhqd', attn, v)
        aT = adapter_wte.shape[0]
        prefix = adapter_wte[None]
        aqkv = jnp.einsum('btc,oc->bto', prefix, w_attn)
        _, ak, av = jnp.split(aqkv, 3, axis=-1)
        ak = ak.reshape(1, aT, H, hd).transpose(0, 2, 1, 3)
        av = av.reshape(1, aT, H, hd).transpose(0, 2, 1, 3)
        ascores = jnp.einsum('bhqd,xhkd->bhqk', q, ak) / jnp.sqrt(jnp.asarray(C, x.dtype))
        ascores = gating[0] * jax.nn.softmax(ascores.astype(jnp.float32), axis=-1).astype(q.dtype)
        y = y + jnp.einsum('bhqk,xhkd->bhqd', ascores, av)
        y = y.transpose(0, 2, 1, 3).reshape(B, T, C)
        return jnp.einsum('btc,oc->bto', y, w_proj)

    def _L0_ffn_ref(x, w_gate, w_up, w_down):
        import jax, jax.numpy as jnp
        import numpy as np
        HIDDEN = 512
        INTER = 1376

        def _ternary_quantize(w):
            scale = jnp.mean(jnp.abs(w))
            return jnp.clip(jnp.round(w / scale), -1.0, 1.0) * scale
        xf = x.astype(jnp.float32) / 128.0
        gate = jnp.einsum('bsh,ih->bsi', xf, w_gate)
        up = jnp.einsum('bsh,ih->bsi', xf, w_up)
        inter = jax.nn.silu(gate) * up
        inter_q = jnp.trunc(jnp.clip(inter * 128.0, -128.0, 127.0)).astype(jnp.int8)
        down = jnp.einsum('bsi,hi->bsh', inter_q.astype(jnp.float32), w_down)
        out = jnp.trunc(jnp.clip(down * 128.0, -128.0, 127.0)).astype(jnp.int8)
        return out
    x = L0_attn_x
    x = x + 0.5 * _L0_ffn_ref(_layernorm(x, axis=-1), L0_ffn_w_gate, L0_ffn_w_up, L0_ffn_w_down)
    x = x + _L0_attn_ref(_layernorm(x, axis=-1), L0_attn_w_attn, L0_attn_w_proj, L0_attn_adapter_wte, L0_attn_gating)
    x = x + 0.5 * _L0_ffn_ref(_layernorm(x, axis=-1), L0_ffn_w_gate, L0_ffn_w_up, L0_ffn_w_down)
    return x

_drawn_inputs = setup_inputs


def setup_inputs(seed=0):
    import zlib

    import numpy as np

    out = dict(_drawn_inputs(seed))
    spreads = {}
    factors = {}
    for name, (base, spread) in spreads.items():
        noise = np.random.default_rng([zlib.crc32(name.encode()), seed]).standard_normal(out[name].shape)
        drawn = base * np.exp(spread * noise) if base else spread * noise
        out[name] = jnp.asarray(drawn.astype(out[name].dtype))
    for name, factor in factors.items():
        out[name] = (out[name] * factor).astype(out[name].dtype)
    return out
```

```python
from contextlib import ExitStack

import numpy as np

import concourse.bass as bass
from concourse import mybir

F32 = mybir.dt.float32
F32R = mybir.dt.float32r
BF16 = mybir.dt.bfloat16
I32 = mybir.dt.int32
ALU = mybir.AluOpType
ACT = mybir.ActivationFunctionType
AX = mybir.AxisListType.X

P = 128
C = 512
T = 512
NB = 4
NT = T // P
NK = C // P
INTER = 1376
NJ = -(-INTER // P)
H, HD = 32, 16
G = 8
GH = H // G
NA = 10
EPS = 1e-5
ROUND = 1.5 * 2.0 ** 23
RSQRT_SEED = 1597463007.0
HI, LO = 0, 1


def wait(eng, sem, value):
    if not isinstance(value, int) or value > 0:
        eng.wait_ge(sem, value)


def over_blocks(eng, body, last=True):
    body(0, True, False)
    with eng.Fori(1, NB - 1 if last else NB) as b:
        body(b, False, False)
    if last:
        body(NB - 1, False, True)


def rows(j):
    return min(P, INTER - j * P)


def layernorm(eng, x, st, sem):
    counter, before = sem
    n = 0

    def step(ins):
        nonlocal n
        ins.then_inc(counter, 1)
        n += 1

    def chained():
        eng.wait_ge(counter, before + n)

    stats, mean, var, rstd, a, d = (st[k] for k in ("stats", "mean", "var", "rstd", "a", "d"))
    for t in range(NT):
        step(eng.bn_stats(stats[:, t, :], x[:, t, :]))
    chained()
    step(eng.tensor_tensor(mean[:, :], stats[:, :, 1], stats[:, :, 4], ALU.add))
    step(eng.tensor_tensor(d[:, :], stats[:, :, 1], stats[:, :, 4], ALU.subtract))
    step(eng.tensor_tensor(var[:, :], stats[:, :, 2], stats[:, :, 5], ALU.add))
    chained()
    step(eng.tensor_scalar(mean[:, :], mean[:, :], 0.5, None, ALU.mult))
    step(eng.scalar_tensor_tensor(out=d[:, :], in0=d[:, :], scalar=0.25, in1=d[:, :], op0=ALU.mult, op1=ALU.mult))
    step(eng.tensor_scalar(var[:, :], var[:, :], 1.0 / C, EPS, ALU.mult, ALU.add))
    chained()
    step(eng.tensor_tensor(var[:, :], var[:, :], d[:, :], ALU.add))
    chained()
    step(eng.tensor_scalar(rstd[:, :].bitcast(I32), var[:, :].bitcast(I32), -0.5, RSQRT_SEED, ALU.mult, ALU.add))
    for _ in range(3):
        chained()
        step(eng.tensor_tensor(a[:, :], rstd[:, :], rstd[:, :], ALU.mult))
        chained()
        step(eng.scalar_tensor_tensor(out=a[:, :], in0=a[:, :], scalar=-0.5, in1=var[:, :], op0=ALU.mult, op1=ALU.mult))
        chained()
        step(eng.scalar_tensor_tensor(out=rstd[:, :], in0=a[:, :], scalar=1.5, in1=rstd[:, :], op0=ALU.add, op1=ALU.mult))
    chained()
    assert n == LN_STEPS


LN_STEPS = NT + 7 + 1 + 9


def ffn_phase(nc, tag, x_src, x_dst, wgT, wuT, wdT, ident_dram):
    with ExitStack() as ctx:
        def sb(name, shape, dt=F32):
            return ctx.enter_context(nc.sbuf_tensor(f"{tag}_{name}", shape, dt))

        def sem(name):
            return ctx.enter_context(nc.semaphore(f"{tag}_{name}"))

        w_gu = sb("w_gu", [P, 2, 2, NK, INTER], F32R)
        w_dn = sb("w_dn", [P, 2, NJ, C], F32R)
        raw_gu = sb("raw_gu", [P, 2, 2, NK, P])
        raw_dn = sb("raw_dn", [P, 2, C])
        xa = sb("xa", [P, NT, C])
        xT = sb("xT", [P, 2, NK, T], F32R)
        inter = sb("inter", [P, NJ, T], F32R)
        silu = sb("silu", [P, 2, T])
        clipped = sb("clipped", [P, T])
        rounded = sb("rounded", [P, T])
        over = sb("over", [P, T])
        under = sb("under", [P, T])
        res = sb("res", [P, 2, C])
        ident = sb("ident", [P, P])
        ln = {k: sb(k, [P, NT]) for k in ("mean", "var", "rstd", "a", "d")}
        ln["stats"] = sb("stats", [P, NT, 6])
        ps = ctx.enter_context(nc.psum_tensor(f"{tag}_ps", [P, 8, 512], F32))
        GATE, UP, DOWN, TR = 0, 2, 4, 6

        s_ident, s_x = sem("ident"), sem("x_loaded")
        s_raw_gu, s_raw_dn, s_res_in, s_store = (
            [sem(f"{name}{i}") for i in range(2)] for name in ("raw_gu_loaded", "raw_dn_loaded", "res_loaded", "stored"))
        s_w_hi, s_w_lo, s_dn_hi, s_dn_lo = map(sem, ("w_hi", "w_lo", "dn_hi", "dn_lo"))
        s_ln, s_norm, s_tr, s_hi, s_lo = map(sem, ("ln_steps", "normalised", "transposed", "xT_hi", "xT_lo"))
        s_gate, s_up, s_silu, s_prod = map(sem, ("gate", "up", "silu_done", "product"))
        s_clip, s_round, s_over, s_under, s_floor, s_trunc = map(
            sem, ("clip", "round", "over_s", "under_s", "floor", "trunc"))
        s_down, s_down_read, s_res = map(sem, ("down", "down_read", "res_done"))

        src = x_src.rearrange("(b t p) c -> p b t c", p=P, t=NT)
        dst = x_dst.rearrange("(b t p) c -> p b t c", p=P, t=NT)
        gT = wgT.rearrange("(k p) i -> p k i", p=P)
        uT = wuT.rearrange("(k p) i -> p k i", p=P)
        TILES = NJ + NT

        block = ctx.enter_context(nc.Block())

        def at(b):
            return bass.ds(b, 1)

        @block.sync
        def _(sp):
            def load_x(b):
                wait(sp, s_tr, b * NK)
                sp.dma_start(xa[:, :, :], src[:, at(b), :, :]).then_inc(s_x, 16)

            def load_raw(j):
                m = rows(j)
                wait(sp, s_w_lo, j - 1)
                for i, w in enumerate((gT, uT)):
                    sp.dma_start(raw_gu[:, j % 2, i, :, 0:m], w[:, :, j * P:j * P + m]).then_inc(s_raw_gu[j % 2], 16)
                wait(sp, s_dn_lo, j - 1)
                sp.dma_start(raw_dn[0:m, j % 2, :], wdT[j * P:j * P + m, :]).then_inc(s_raw_dn[j % 2], 16)

            sp.dma_start(ident[:, :], ident_dram).then_inc(s_ident, 16)

            def body(b, first, last):
                if first:
                    load_x(0)
                    for j in range(NJ):
                        load_raw(j)
                        if j == 2:
                            load_x(1)
                elif not last:
                    load_x(b + 1)
                for t in range(2):
                    wait(sp, s_store[t], b * (NT // 2) * 16)
                    sp.dma_start(res[:, t, :], src[:, at(b), t, :]).then_inc(s_res_in[t], 16)
                for t in range(NT):
                    i, used = t % 2, b * (NT // 2) + t // 2 + 1
                    sp.wait_ge(s_res, b * NT + t + 1)
                    sp.dma_start(dst[:, at(b), t, :], res[:, i, :]).then_inc(s_store[i], 16)
                    if t + 2 < NT:
                        sp.wait_ge(s_store[i], used * 16)
                        sp.dma_start(res[:, i, :], src[:, at(b), t + 2, :]).then_inc(s_res_in[i], 16)

            over_blocks(sp, body)
            for i in range(2):
                sp.wait_ge(s_store[i], NB * (NT // 2) * 16)

        @block.tensor
        def _(pe):
            def transpose_x(b, k):
                wait(pe, s_lo, b * NK + k - 1)
                pe.wait_ge(s_norm, (b + 1) * NT)
                for t in range(NT):
                    last = pe.transpose(ps[:, TR + k % 2, t * P:(t + 1) * P], xa[:, t, k * P:(k + 1) * P], ident[:, :])
                last.then_inc(s_tr, 1)

            def gate_up(b, j):
                n = b * NJ + j
                m = rows(j)
                pe.wait_ge(s_w_lo, j + 1)
                for which, bank, free, done in ((0, GATE, s_silu, s_gate), (1, UP, s_prod, s_up)):
                    if which == 0:
                        wait(pe, free, n - 1)
                    else:
                        wait(pe, free, n - 1)
                    out = ps[0:m, bank + j % 2, :]
                    for k in range(NK):
                        cols = slice(j * P, j * P + m)
                        pe.matmul(out, w_gu[:, HI, which, k, cols], xT[:, HI, k, :], start=(k == 0), stop=False)
                        pe.matmul(out, w_gu[:, HI, which, k, cols], xT[:, LO, k, :], start=False, stop=False)
                        mm = pe.matmul(out, w_gu[:, LO, which, k, cols], xT[:, HI, k, :], start=False, stop=(k == NK - 1))
                    mm.then_inc(done, 1)

            def down(b, t):
                n = b * NT + t
                wait(pe, s_down_read, n - 1)
                out = ps[:, DOWN + t % 2, :]
                for j in range(NJ):
                    m = rows(j)
                    if t == 0 and j >= NJ - 3:
                        pe.wait_ge(s_trunc, b * TILES + j + 1)
                    for part in (HI, LO):
                        mm = pe.matmul(out, inter[0:m, j, t * P:(t + 1) * P], w_dn[0:m, part, j, :],
                                       start=(j == 0 and part == HI), stop=(j == NJ - 1 and part == LO))
                mm.then_inc(s_down, 1)

            pe.wait_ge(s_ident, 16)
            for k in range(NK):
                transpose_x(0, k)

            def body(b, first, last):
                pe.wait_ge(s_lo, (b + 1) * NK)
                for j in range(NJ):
                    gate_up(b, j)
                if first:
                    pe.wait_ge(s_dn_lo, NJ)
                    pe.wait_ge(s_dn_hi, NJ)
                pe.wait_ge(s_trunc, b * TILES + NJ - 3)
                for t in range(NT):
                    if not last:
                        transpose_x(b + 1, t)
                    down(b, t)

            over_blocks(pe, body)

        @block.scalar
        def _(act):
            def cut_hi(b, k):
                act.wait_ge(s_tr, b * NK + k + 1)
                act.activation(xT[:, HI, k, :], ps[:, TR + k % 2, :], ACT.Copy).then_inc(s_hi, 1)

            def cut_weights(j):
                m = rows(j)
                act.wait_ge(s_raw_gu[j % 2], 32 * (j // 2 + 1))
                act.activation(w_gu[:, HI, :, :, j * P:j * P + m], raw_gu[:, j % 2, :, :, 0:m], ACT.Copy).then_inc(s_w_hi, 1)
                act.wait_ge(s_raw_dn[j % 2], 16 * (j // 2 + 1))
                act.activation(w_dn[0:m, HI, j, :], raw_dn[0:m, j % 2, :], ACT.Copy).then_inc(s_dn_hi, 1)

            cut_weights(0)
            for k in range(NK):
                cut_hi(0, k)
            cut_weights(1)

            def body(b, first, last):
                for j in range(NJ):
                    n = b * NJ + j
                    m = rows(j)
                    act.wait_ge(s_gate, n + 1)
                    wait(act, s_prod, n - 1)
                    act.activation(silu[0:m, j % 2, :], ps[0:m, GATE + j % 2, :], ACT.Silu, scale=1.0 / 128).then_inc(s_silu, 1)
                    if first and j + 2 < NJ:
                        cut_weights(j + 2)
                if not last:
                    for k in range(NK):
                        cut_hi(b + 1, k)

            over_blocks(act, body)

        @block.gpsimd
        def _(pool):
            for j in range(NJ):
                m = rows(j)
                pool.wait_ge(s_dn_hi, j + 1)
                pool.tensor_tensor(w_dn[0:m, LO, j, :], raw_dn[0:m, j % 2, :], w_dn[0:m, HI, j, :].bitcast(F32),
                                   ALU.subtract).then_inc(s_dn_lo, 1)

        @block.vector
        def _(dve):
            def cut_lo(b, k):
                dve.wait_ge(s_hi, b * NK + k + 1)
                dve.tensor_tensor(xT[:, LO, k, :], ps[:, TR + k % 2, :], xT[:, HI, k, :].bitcast(F32),
                                  ALU.subtract).then_inc(s_lo, 1)

            def cut_weights(j):
                m = rows(j)
                dve.wait_ge(s_w_hi, j + 1)
                for i in range(2):
                    ins = dve.tensor_tensor(w_gu[:, LO, i, :, j * P:j * P + m], raw_gu[:, j % 2, i, :, 0:m],
                                            w_gu[:, HI, i, :, j * P:j * P + m].bitcast(F32), ALU.subtract)
                ins.then_inc(s_w_lo, 1)

            def normalise(b):
                dve.wait_ge(s_x, (b + 1) * 16)
                layernorm(dve, xa, ln, (s_ln, b * LN_STEPS))
                for t in range(NT):
                    dve.tensor_scalar(xa[:, t, :], xa[:, t, :], ln["mean"][:, t:t + 1], ln["rstd"][:, t:t + 1],
                                      ALU.subtract, ALU.mult).then_inc(s_norm, 1)

            def truncate(out, m, n):
                c, r = clipped[0:m, :], rounded[0:m, :]
                dve.wait_ge(s_clip, n + 1)
                dve.tensor_scalar(r, c, ROUND, -ROUND, ALU.add, ALU.add).then_inc(s_round, 1)
                dve.wait_ge(s_round, n + 1)
                dve.scalar_tensor_tensor(out=over[0:m, :], in0=c, scalar=0.0, in1=r,
                                         op0=ALU.max, op1=ALU.is_lt).then_inc(s_over, 1)
                dve.scalar_tensor_tensor(out=under[0:m, :], in0=c, scalar=0.0, in1=r,
                                         op0=ALU.min, op1=ALU.is_gt).then_inc(s_under, 1)
                dve.wait_ge(s_over, n + 1)
                dve.tensor_tensor(r, r, over[0:m, :], ALU.subtract).then_inc(s_floor, 1)
                dve.wait_ge(s_under, n + 1)
                dve.wait_ge(s_floor, n + 1)
                dve.tensor_tensor(out, r, under[0:m, :], ALU.add).then_inc(s_trunc, 1)

            def quantise_inner(b, j):
                n, m = b * TILES + j, rows(j)
                dve.wait_ge(s_silu, b * NJ + j + 1)
                dve.wait_ge(s_up, b * NJ + j + 1)
                dve.tensor_tensor(clipped[0:m, :], silu[0:m, j % 2, :], ps[0:m, UP + j % 2, :], ALU.mult).then_inc(s_prod, 1)
                dve.wait_ge(s_prod, b * NJ + j + 1)
                dve.tensor_scalar(clipped[0:m, :], clipped[0:m, :], -128.0, 127.0, ALU.max, ALU.min).then_inc(s_clip, 1)
                truncate(inter[0:m, j, :], m, n)

            def finish(b, t):
                n = b * TILES + NJ + t
                dve.wait_ge(s_down, b * NT + t + 1)
                dve.tensor_scalar(clipped[:, :], ps[:, DOWN + t % 2, :], 128.0, 127.0, ALU.mult, ALU.min).then_inc(s_down_read, 1)
                dve.wait_ge(s_down_read, b * NT + t + 1)
                dve.tensor_scalar(clipped[:, :], clipped[:, :], -128.0, None, ALU.max).then_inc(s_clip, 1)
                truncate(over[:, :], P, n)
                dve.wait_ge(s_trunc, n + 1)
                dve.wait_ge(s_res_in[t % 2], (b * (NT // 2) + t // 2 + 1) * 16)
                dve.scalar_tensor_tensor(out=res[:, t % 2, :], in0=over[:, :], scalar=0.5, in1=res[:, t % 2, :],
                                         op0=ALU.mult, op1=ALU.add).then_inc(s_res, 1)

            normalise(0)
            cut_weights(0)
            for k in range(NK):
                cut_lo(0, k)
            cut_weights(1)

            def body(b, first, last):
                for j in range(NJ):
                    quantise_inner(b, j)
                    if first and j + 2 < NJ:
                        cut_weights(j + 2)
                    if j == 6 and not last:
                        normalise(b + 1)
                for t in range(NT):
                    if not last:
                        cut_lo(b + 1, t)
                    if t:
                        finish(b, t - 1)
                finish(b, NT - 1)

            over_blocks(dve, body)


UNITS = [(0, 0, 4), (1, 0, 2), (1, 2, 2)] + [(t, h, 1) for t in (2, 3) for h in range(GH)]
KEY_UNITS = [(NT - 1 - t, h, n) for t, h, n in sorted(UNITS, key=lambda u: (-u[0], u[1]))]
NU = len(UNITS)
PART_Q = (0, 0, 1, 0, 2, 1)
PART_K = (0, 1, 0, 2, 0, 1)
NS = len(PART_Q)
KROWS = NS * HD
SLOTS = 4


def attention_steps():
    steps = [("norm",)] + [("xt", k) for k in range(NK)] + [("qkv", t) for t in range(NT)]

    def cut(c):
        return [("tr", c, 0), ("tr", c, 1), ("cut", c, 0), ("cut", c, 1)]

    def maxima(g):
        return [("max", g, u) for u in range(NU)] + [("neg", g)]

    steps += cut(0) + [("stack", 0), ("stack", 1), ("ascore", 0)]
    steps += cut(1) + [("stack", 2), ("stack", 3)] + maxima(0) + [("amix", 0), ("mrow", 0), ("ascore", 1)]
    steps += maxima(1) + [("aout", 0), ("mrow", 1), ("amix", 1)]
    for g in range(G):
        for u in range(NU):
            c = (g + 3) // 2
            new = g % 2 == 1 and c < NK
            steps.append(("prob", g, u))
            if g + 2 < G:
                steps.append(("max", g + 2, u))
            if u == 1 and g:
                steps += [("pv", g - 1, 2), ("pv", g - 1, 3)]
            if u == 2:
                if g and g + 1 < G and g > 0:
                    steps.append(("mrow", g + 1))
                if new:
                    steps += [("tr", c, 0), ("tr", c, 1)]
                if g == 1:
                    steps.append(("aout", 1))
            if u == 3:
                if g:
                    steps.append(("oT", g - 1))
                if new:
                    steps += [("cut", c, 0), ("cut", c, 1)]
            if u == 4 and g and g + 3 < G:
                steps.append(("stack", g + 3))
            if u == 5:
                steps.append(("pv", g, 0))
                if new:
                    steps.append(("ascore", c))
                if g % 2 == 0 and 2 <= g // 2 + 1 < NK:
                    steps.append(("amix", g // 2 + 1))
            if u == 8:
                if g % 2 == 0 and 2 <= g // 2 + 1 < NK:
                    steps.append(("aout", g // 2 + 1))
            if u == 9:
                steps.append(("pv", g, 1))
        if g + 2 < G:
            steps.append(("neg", g + 2))
    steps += [("pv", G - 1, 2), ("pv", G - 1, 3), ("oT", G - 1)]
    steps += [("yt", k) for k in range(NK)] + [("proj", t) for t in range(NT)]
    return steps


SHARED = ("xt", "tr", "ascore", "amix", "aout", "mrow", "oT", "yt")


def attention_phase(nc, x_src, x_dst, wqkvT, wpT, wte, gating, consts):
    with ExitStack() as ctx:
        def sb(name, shape, dt=F32):
            return ctx.enter_context(nc.sbuf_tensor(f"at_{name}", shape, dt))

        def sem(name):
            return ctx.enter_context(nc.semaphore(f"at_{name}"))

        w = sb("w", [P, 2, NK, 3 * C], F32R)
        wp = sb("wp", [P, 2, NK, C], F32R)
        xT = sb("xT", [P, 2, NK, T], F32R)
        xa = sb("xa", [P, NT, C])
        y = xa
        res = sb("res", [P, 2, C])
        qk = sb("qk", [P, NT, 2 * C])
        v = sb("v", [P, NT, H, 32])
        parts = sb("parts", [P, 2, 3, T], BF16)
        rest = sb("rest", [P, 2, T])
        q_stack = sb("q_stack", [KROWS + 3, SLOTS, GH, T], BF16)
        k_stack = sb("k_stack", [KROWS + 3, SLOTS, GH, T], BF16)
        probs = sb("probs", [P, 10 * T])
        o_cols = sb("o_cols", [P, T])
        o_part = sb("o_part", [P, NT, GH, HD])
        rsum = sb("rsum", [P, NT, GH])
        a_prob = sb("a_prob", [P, NT * 8, NA])
        a_max = sb("a_max", [P, NT * 8])
        a_sum = sb("a_sum", [P, NT * 8])
        a_T = sb("a_T", [8 * NA, T])
        ak = sb("ak", [P, 3, NK, 8 * NA], BF16)
        av = sb("av", [8 * NA, C])
        aw = sb("aw", [P, 2, NK, 8 * NA], F32R)
        cos = sb("cos", [P, NT, 64])
        sin = sb("sin", [P, NT, 64])
        ident = sb("ident", [P, P])
        ident_b = sb("ident_b", [P, P], BF16)
        neg_mask = sb("neg_mask", [P, P], BF16)
        ak_mask = sb("ak_mask", [P, 8])
        av_mask = sb("av_mask", [8 * NA, P])
        gate = sb("gate", [P, 1])
        top = sb("top", [P, NT, GH])
        top_rest = sb("top_rest", [P, NT, GH])
        top_parts = sb("top_parts", [P, NT, 3, GH], BF16)
        top_rows = sb("top_rows", [3 * GH, 2, T], BF16)
        ln = {k: sb(k, [P, NT]) for k in ("mean", "var", "rstd", "a", "d")}
        ln["stats"] = sb("stats", [P, NT, 6])
        ps = ctx.enter_context(nc.psum_tensor("at_ps", [P, 8, 512], F32))
        SMAX, SPROB, OUT, SH = 0, 2, 5, 6

        starts = [GH * sum(T - P * m for m in range(i)) for i in range(NT)]
        prob = [probs[:, starts[i]:starts[i] + GH * (T - P * i)].rearrange("p (h q) -> p h q", h=GH) for i in range(NT)]
        rope_a = [probs[:, 2048 * i:2048 * i + 1024] for i in range(2)]
        rope_b = [probs[:, 2048 * i + 1024:2048 * i + 2048] for i in range(2)]
        raw_w = [probs[:, 1536 * k:1536 * k + 1536] for k in range(3)] + [qk[:, 0:2, :].rearrange("p t c -> p (t c)")[:, 0:1536]]
        raw_wp = qk[:, 2:4, :].rearrange("p t c -> p (t c)").rearrange("p (k c) -> p k c", k=NK)
        raw_aw = rest[:, 0, 0:NK * 8 * NA].rearrange("p (k a) -> p k a", k=NK)
        ak_full = a_prob
        ak_rest = xa[:, 0, 0:NK * 8 * NA]

        s_const, s_raw, s_masks = sem("const_loaded"), sem("raw_loaded"), sem("masks")
        s_w_hi, s_w_lo, s_wp_hi, s_wp_lo, s_aw_hi, s_aw_lo = map(sem, ("w_hi", "w_lo", "wp_hi", "wp_lo", "aw_hi", "aw_lo"))
        s_ak_mm, s_av_mm, s_ak, s_av = map(sem, ("ak_mm", "av_mm", "ak_steps", "ident_cast"))
        s_x, s_ln, s_norm = map(sem, ("x_loaded", "ln_steps", "normalised"))
        s_xt, s_xhi = map(sem, ("x_transposed", "x_hi"))
        s_qk, s_v, s_vcopy = map(sem, ("qk_mm", "v_mm", "v_copied"))
        s_rope, s_turned = sem("rope_terms"), sem("rope_summed")
        s_tr, s_hi, s_mid, s_parts = map(sem, ("qk_transposed", "part_hi", "part_mid", "parts_ready"))
        s_stack = [sem(f"stacked{i}") for i in range(SLOTS)]
        s_smm, s_max = sem("scores_for_max"), sem("unit_max")
        s_top, s_topT = map(sem, ("top_steps", "top_transposed"))
        s_toprow_in = [sem(f"top_row_in{i}") for i in range(2)]
        s_pmm, s_exp, s_causal, s_pv, s_out, s_ocopy = map(
            sem, ("scores_for_exp", "exp_done", "causal", "pv_tile", "pv_group", "out_copied"))
        s_oT, s_rsum, s_opart, s_y = map(sem, ("out_transposed", "row_sum", "out_part", "y_added"))
        s_amm, s_amax, s_aexp, s_asum, s_ascale, s_anorm = map(
            sem, ("a_scores", "a_max_done", "a_exp", "a_sum_done", "a_scale", "a_norm"))
        s_aT, s_aout = map(sem, ("a_transposed", "a_out"))
        s_yt, s_yhi = map(sem, ("y_transposed", "y_hi"))
        s_proj, s_res = sem("proj"), sem("res_done")
        s_res_in, s_store = ([sem(f"{name}{i}") for i in range(2)] for name in ("res_loaded", "stored"))
        s_pool_passed, s_sp_passed = sem("pool_passed"), sem("sp_passed")
        s_free = [sem(f"shared_bank_free{i}") for i in range(2)]

        src = x_src.rearrange("(b t p) c -> p b t c", p=P, t=NT)
        dst = x_dst.rearrange("(b t p) c -> p b t c", p=P, t=NT)
        steps = attention_steps()
        uses = {s: i for i, s in enumerate([s for s in steps if s[0] in SHARED])}
        assert len(uses) % 2 == 0 and len(uses) == sum(s[0] in SHARED for s in steps)
        PER_BANK = len(uses) // 2
        SETUP_USES = 1

        def shared(step):
            return ps[:, SH + uses[step] % 2, :]

        def free(step):
            return s_free[uses[step] % 2]

        def read(b, step):
            return free(step), b * PER_BANK + uses[step] // 2 + 1 + SETUP_USES

        def over_batches(eng, body):
            body(0)
            with eng.Fori(1, NB) as b:
                body(b)

        def at(b):
            return bass.ds(b, 1)

        def key_unit(u):
            i, h, n = KEY_UNITS[u]
            return i, h, n, T - P * i, SPROB + u % 3

        block = ctx.enter_context(nc.Block())

        @block.sync
        def _(sp):
            for k in range(NK):
                sp.dma_start(raw_w[k], wqkvT[k * P:(k + 1) * P, :]).then_inc(s_raw, 16)
                sp.wait_ge(s_raw, 16 * (k + 1))
            sp.dma_start(raw_aw, wte.rearrange("(k p) a -> p k a", p=P)).then_inc(s_raw, 16)
            sp.wait_ge(s_raw, 16 * (NK + 1))
            sp.dma_start(raw_wp, wpT.rearrange("(k p) c -> p k c", p=P)).then_inc(s_raw, 16)
            for tile, name in ((ident, "ident"), (ak_mask, "ak_mask"), (av_mask, "av_mask")):
                sp.dma_start(tile[:, :], consts[name]).then_inc(s_const, 16)
            for tile, name in ((cos, "cos"), (sin, "sin")):
                sp.dma_start(tile[:, :, :], consts[name].rearrange("(t p) c -> p t c", p=P)).then_inc(s_const, 16)
            sp.dma_start(gate[:, :], gating.partition_broadcast(P)).then_inc(s_const, 16)
            sp.wait_ge(s_ak, 4)

            def body(b):
                for step in steps:
                    kind, *a = step
                    if kind == "norm":
                        wait(sp, s_yt, b * NK)
                        sp.dma_start(xa[:, :, :], src[:, at(b), :, :]).then_inc(s_x, 16)
                    if kind == "stack":
                        g, = a
                        c, half, slot = g // 2, g % 2, g % SLOTS
                        n = b * G + g
                        done = b * (G * NU) + (g - SLOTS + 1) * NU
                        sp.wait_ge(s_parts, 2 * (b * NK + c + 1))
                        sp.sem_inc(s_sp_passed, 1)
                        wait(sp, s_pmm, done)
                        own = slice(half * 64, half * 64 + 64)
                        for r in range(NS):
                            to = slice(r * HD, (r + 1) * HD)
                            sp.dma_start(q_stack[to, slot, :, :], parts[own, 0, PART_Q[r], :]).then_inc(s_stack[slot], 16)
                            sp.dma_start(k_stack[to, slot, :, :], parts[own, 1, PART_K[r], :]).then_inc(s_stack[slot], 16)
                    if kind == "mrow":
                        g, = a
                        sp.wait_ge(*read(b, step))
                        sp.dma_start(q_stack[KROWS:KROWS + 3, g % SLOTS, :, :], top_rows[:, g % 2, :]).then_inc(s_toprow_in[g % 2], 16)
                    if kind == "proj":
                        t, = a
                        i, used = t % 2, b * (NT // 2) + t // 2
                        if t < 2:
                            wait(sp, s_store[i], used * 16)
                            sp.dma_start(res[:, i, :], src[:, at(b), t, :]).then_inc(s_res_in[i], 16)
                for t in range(NT):
                    i, used = t % 2, b * (NT // 2) + t // 2 + 1
                    sp.wait_ge(s_res, b * NT + t + 1)
                    sp.dma_start(dst[:, at(b), t, :], res[:, i, :]).then_inc(s_store[i], 16)
                    if t + 2 < NT:
                        sp.wait_ge(s_store[i], used * 16)
                        sp.dma_start(res[:, i, :], src[:, at(b), t + 2, :]).then_inc(s_res_in[i], 16)

            over_batches(sp, body)
            for i in range(2):
                sp.wait_ge(s_store[i], NB * (NT // 2) * 16)

        @block.tensor
        def _(pe):
            def three(out, lhsT, rhs, start, stop):
                pe.matmul(out, lhsT(HI), rhs(HI), start=start, stop=False)
                pe.matmul(out, lhsT(HI), rhs(LO), start=False, stop=False)
                return pe.matmul(out, lhsT(LO), rhs(HI), start=False, stop=stop)

            pe.wait_ge(s_w_lo, NK)
            pe.wait_ge(s_aw_lo, 1)
            for c in range(NK):
                for k in range(NK):
                    mm = three(ps[:, SH, c * NA:(c + 1) * NA], lambda part: w[:, part, k, C + c * P:C + (c + 1) * P],
                               lambda part: aw[:, part, k, 0:NA], k == 0, k == NK - 1)
            mm.then_inc(s_ak_mm, 1)
            for k in range(NK):
                mm = three(ps[0:8 * NA, SH + 1, :], lambda part: aw[:, part, k, :],
                           lambda part: w[:, part, k, 2 * C:3 * C], k == 0, k == NK - 1)
            mm.then_inc(s_av_mm, 1)
            pe.wait_ge(s_const, 6 * 16)
            pe.wait_ge(s_masks, 5)
            pe.wait_ge(s_ak, 4)
            pe.wait_ge(s_av, 1)

            def body(b):
                def take(step):
                    pe.wait_ge(free(step), b * PER_BANK + uses[step] // 2 + SETUP_USES)
                    return shared(step)

                for step in steps:
                    kind, *a = step
                    if kind == "xt":
                        k, = a
                        out = take(step)
                        pe.wait_ge(s_norm, (b + 1) * NT)
                        for t in range(NT):
                            mm = pe.transpose(out[:, t * P:(t + 1) * P], xa[:, t, k * P:(k + 1) * P], ident[:, :])
                        mm.then_inc(s_xt, 1)
                    if kind == "qkv":
                        t, = a
                        if t == 0:
                            for k in (NK - 2, NK - 1):
                                pe.wait_ge(*read(b, ("xt", k)))
                            wait(pe, s_res, b * NT)
                            wait(pe, s_exp, b * G * NU)
                            wait(pe, s_ocopy, b * G)
                        if t >= 2:
                            pe.wait_ge(s_rope, (b * NT + t - 1) * 3)
                            pe.wait_ge(s_vcopy, b * NT + t - 1)
                        for part, bank in ((0, 2 * (t % 2)), (1, 2 * (t % 2) + 1), (2, 4 + t % 2)):
                            for k in range(NK):
                                mm = three(ps[:, bank, :], lambda x: xT[:, x, k, t * P:(t + 1) * P],
                                           lambda x: w[:, x, k, part * C:(part + 1) * C], k == 0, k == NK - 1)
                            if part:
                                mm.then_inc(s_qk if part == 1 else s_v, 1)
                    if kind == "tr":
                        c, which = a
                        out = take(step)
                        pe.wait_ge(s_turned, (b + 1) * NT)
                        for t in range(NT):
                            at_ = which * C + c * P
                            mm = pe.transpose(out[:, t * P:(t + 1) * P], qk[:, t, at_:at_ + P], ident[:, :])
                        mm.then_inc(s_tr, 1)
                    if kind == "ascore":
                        c, = a
                        out = take(step)
                        pe.wait_ge(s_parts, 2 * (b * NK + c + 1))
                        for t in range(NT):
                            for r in range(NS):
                                mm = pe.matmul(out[:, t * 8 * NA:(t + 1) * 8 * NA], parts[:, 0, PART_Q[r], t * P:(t + 1) * P],
                                               ak[:, PART_K[r], c, :], start=(r == 0), stop=(r == NS - 1))
                        mm.then_inc(s_amm, 1)
                    if kind == "amix":
                        c, = a
                        out = take(step)
                        pe.wait_ge(s_anorm, b * NK + c + 1)
                        for t in range(NT):
                            mm = pe.transpose(out[0:8 * NA, t * P:(t + 1) * P],
                                              a_prob[:, 8 * t:8 * t + 8, :].rearrange("p h a -> p (h a)"), ident[:, :])
                        mm.then_inc(s_aT, 1)
                    if kind == "aout":
                        c, = a
                        out = take(step)
                        pe.wait_ge(*read(b, ("amix", c)))
                        for t in range(NT):
                            mm = pe.matmul(out[:, t * P:(t + 1) * P], a_T[:, t * P:(t + 1) * P], av[:, c * P:(c + 1) * P],
                                           start=True, stop=True)
                        mm.then_inc(s_aout, 1)
                    if kind == "max":
                        g, u = a
                        t, h0, nh = UNITS[u]
                        n, slot = b * G + g, g % SLOTS
                        bank = SMAX + (g * NU + u) % 2
                        if g == 0 and u == 0:
                            pe.wait_ge(s_rope, (b + 1) * NT * 3)
                        wait(pe, s_max, n * NU + u - 1)
                        if u == 0:
                            pe.wait_ge(s_stack[slot], (b * (G // SLOTS) + g // SLOTS + 1) * 2 * NS * 16)
                        m = P * (t + 1)
                        for h in range(h0, h0 + nh):
                            out = ps[:, bank, (h - h0) * m:(h - h0 + 1) * m]
                            pe.matmul(out, q_stack[0:KROWS, slot, h, t * P:(t + 1) * P], k_stack[0:KROWS, slot, h, 0:m],
                                      start=True, stop=False)
                            mm = pe.matmul(out[:, t * P:m], ident_b[:, :], neg_mask[:, :], start=False, stop=True)
                        mm.then_inc(s_smm, 1)
                    if kind == "mrow":
                        g, = a
                        out = take(step)
                        pe.wait_ge(s_top, (b * G + g + 1) * 4)
                        rows_ps = out[0:3 * GH, 0:T // 2].bitcast(BF16)
                        for t in range(NT):
                            mm = pe.transpose(rows_ps[:, t * P:(t + 1) * P],
                                              top_parts[:, t, :, :].rearrange("p s h -> p (s h)"), ident_b[:, :])
                        mm.then_inc(s_topT, 1)
                    if kind == "prob":
                        g, u = a
                        i, h0, nh, m, bank = key_unit(u)
                        n, slot = b * G + g, g % SLOTS
                        if g == 0 and u == 0:
                            pe.wait_ge(s_rope, (b + 1) * NT * 3)
                            pe.wait_ge(s_vcopy, (b + 1) * NT)
                        wait(pe, s_exp, n * NU + (u - 2 if u >= 3 else (-1, 0, -2)[u]))
                        if u == 0:
                            pe.wait_ge(s_toprow_in[g % 2], (b * (G // 2) + g // 2 + 1) * 16)
                        for h in range(h0, h0 + nh):
                            mm = pe.matmul(ps[:, bank, (h - h0) * m:(h - h0 + 1) * m],
                                           k_stack[:, slot, h, i * P:(i + 1) * P], q_stack[:, slot, h, i * P:T],
                                           start=True, stop=True)
                        mm.then_inc(s_pmm, 1)
                    if kind == "pv":
                        g, i = a
                        n = b * G + g
                        pe.wait_ge(s_causal, n * NT + i + 1)
                        if i == 0:
                            wait(pe, s_ocopy, n)
                            if g == 0:
                                pe.wait_ge(s_vcopy, (b + 1) * NT)
                        for h in range(GH):
                            mm = pe.matmul(ps[32 * h:32 * h + 32, OUT, i * P:T], v[:, i, g * GH + h, :], prob[i][:, h, :],
                                           start=(i == 0), stop=(i == NT - 1))
                        mm.then_inc(s_pv, 1)
                    if kind == "oT":
                        g, = a
                        out = take(step)
                        pe.wait_ge(s_ocopy, b * G + g + 1)
                        for t in range(NT):
                            mm = pe.transpose(out[:, t * P:(t + 1) * P], o_cols[:, t * P:(t + 1) * P], ident[:, :])
                        mm.then_inc(s_oT, 1)
                    if kind == "yt":
                        k, = a
                        out = take(step)
                        pe.wait_ge(s_y, b * G + 2 * k + 2)
                        for t in range(NT):
                            mm = pe.transpose(out[:, t * P:(t + 1) * P], y[:, t, k * P:(k + 1) * P], ident[:, :])
                        mm.then_inc(s_yt, 1)
                    if kind == "proj":
                        t, = a
                        if t == 0:
                            for k in (NK - 2, NK - 1):
                                pe.wait_ge(*read(b, ("yt", k)))
                            pe.wait_ge(s_max, (b + 1) * G * NU)
                        if t >= 2:
                            pe.wait_ge(s_res, b * NT + t - 1)
                        for k in range(NK):
                            mm = three(ps[:, SMAX + t % 2, :], lambda x: xT[:, x, k, t * P:(t + 1) * P],
                                       lambda x: wp[:, x, k, :], k == 0, k == NK - 1)
                        mm.then_inc(s_proj, 1)

            over_batches(pe, body)

        @block.scalar
        def _(act):
            for k in range(NK):
                act.wait_ge(s_raw, 16 * (k + 1))
                act.activation(w[:, HI, k, :], raw_w[k], ACT.Copy).then_inc(s_w_hi, 1)
            act.wait_ge(s_raw, 16 * (NK + 1))
            act.activation(aw[:, HI, :, :], raw_aw, ACT.Copy).then_inc(s_aw_hi, 1)
            act.wait_ge(s_raw, 16 * (NK + 2))
            act.activation(wp[:, HI, :, :], raw_wp, ACT.Copy).then_inc(s_wp_hi, 1)

            def body(b):
                for step in steps:
                    kind, *a = step
                    if kind == "xt":
                        k, = a
                        act.wait_ge(s_xt, b * NK + k + 1)
                        act.activation(xT[:, HI, k, :], shared(step), ACT.Copy).then_inc(s_xhi, 1)
                    if kind == "qkv":
                        t, = a
                        act.wait_ge(s_v, b * NT + t + 1)
                        act.activation(v[:, t, :, 0:HD], ps[:, 4 + t % 2, :].rearrange("p (h d) -> p h d", h=H), ACT.Copy).then_inc(s_vcopy, 1)
                    if kind == "tr":
                        c, which = a
                        n = 2 * (b * NK + c) + which
                        act.wait_ge(s_tr, n + 1)
                        if which == 0:
                            if c:
                                for g in (2 * c - 2, 2 * c - 1):
                                    act.wait_ge(s_stack[g % SLOTS], (b * (G // SLOTS) + g // SLOTS + 1) * 2 * NS * 16)
                            else:
                                for g in (G - 2, G - 1):
                                    wait(act, s_stack[g % SLOTS], b * (G // SLOTS) * 2 * NS * 16)
                            wait(act, s_amm, b * NK + c)
                        act.activation(parts[:, which, 0, :], shared(step), ACT.Copy).then_inc(s_hi, 1)
                    if kind == "cut":
                        c, which = a
                        n = 2 * (b * NK + c) + which
                        act.wait_ge(*read(b, ("tr", c, which)))
                        act.activation(parts[:, which, 1, :], rest[:, which, :], ACT.Copy).then_inc(s_mid, 1)
                    if kind == "amix":
                        c, = a
                        act.wait_ge(s_aT, b * NK + c + 1)
                        act.activation(a_T[:, :], shared(step)[0:8 * NA, :], ACT.Copy).then_inc(free(step), 1)
                    if kind == "ascore":
                        c, = a
                        act.wait_ge(*read(b, step))
                        act.activation(a_prob[:, :, :], a_prob[:, :, :], ACT.Exp, scale=float(1.0 / np.sqrt(np.float32(C)))).then_inc(s_aexp, 1)
                    if kind == "aout":
                        c, = a
                        act.wait_ge(s_aout, b * NK + c + 1)
                        act.activation(y[:, :, c * P:(c + 1) * P], shared(step).rearrange("p (t c) -> p t c", t=NT), ACT.Copy).then_inc(free(step), 1)
                    if kind == "mrow":
                        g, = a
                        n = b * G + g
                        act.wait_ge(s_topT, n + 1)
                        wait(act, s_toprow_in[g % 2], (b * (G // 2) + g // 2) * 16)
                        act.activation(top_rows[:, g % 2, :], shared(step)[0:3 * GH, 0:T // 2].bitcast(BF16), ACT.Copy).then_inc(free(step), 1)
                    if kind == "prob":
                        g, u = a
                        i, h0, nh, m, bank = key_unit(u)
                        n = b * G + g
                        act.wait_ge(s_pmm, n * NU + u + 1)
                        wait(act, s_pv, (n - 1) * NT + i + 1)
                        act.activation(prob[i][:, h0:h0 + nh, :], ps[:, bank, 0:nh * m].rearrange("p (h q) -> p h q", h=nh),
                                       ACT.Exp, scale=HD ** -0.5).then_inc(s_exp, 1)
                    if kind == "pv" and a[1] == NT - 1:
                        g = a[0]
                        n = b * G + g
                        act.wait_ge(s_pv, (n + 1) * NT)
                        wait(act, s_oT, n)
                        act.activation(o_cols[:, :], ps[:, OUT, :], ACT.Copy).then_inc(s_ocopy, 1)
                    if kind == "yt":
                        k, = a
                        act.wait_ge(s_yt, b * NK + k + 1)
                        act.activation(xT[:, HI, k, :], shared(step), ACT.Copy).then_inc(s_yhi, 1)

            over_batches(act, body)

        @block.gpsimd
        def _(pool):
            pool.memset(v[:, :, :, HD:32], 0.0).then_inc(s_masks, 1)
            pool.wait_ge(s_masks, 1)
            pool.memset(v[:, :, :, HD:HD + 1], 1.0).then_inc(s_masks, 1)
            pool.wait_ge(s_masks, 2)
            pool.memset(k_stack[KROWS:KROWS + 3, :, :, :], 1.0).then_inc(s_masks, 1)
            pool.wait_ge(s_masks, 3)
            pool.memset(neg_mask[:, :], 0.0).then_inc(s_masks, 1)
            pool.wait_ge(s_masks, 4)
            pool.affine_select(neg_mask[:, :], neg_mask[:, :], pattern=[[-1, P]], compare_op=ALU.is_ge,
                               fill=-3e38, base=0, channel_multiplier=1).then_inc(s_masks, 1)
            pool.wait_ge(s_wp_hi, 1)
            pool.tensor_tensor(wp[:, LO, :, :], raw_wp, wp[:, HI, :, :].bitcast(F32), ALU.subtract).then_inc(s_wp_lo, 1)

            def body(b):
                for step in steps:
                    kind, *a = step
                    if kind == "qkv":
                        t, = a
                        if t == 0:
                            pool.wait_ge(s_wp_lo, 1)
                        pool.wait_ge(s_rope, (b * NT + t + 1) * 3)
                        pool.tensor_tensor(qk[:, t, :], rope_a[t % 2], rope_b[t % 2], ALU.add).then_inc(s_turned, 1)
                    if kind == "prob":
                        g, u = a
                        i = KEY_UNITS[u][0]
                        if u == NU - 1 or KEY_UNITS[u + 1][0] != i:
                            n = b * G + g
                            pool.wait_ge(s_exp, n * NU + u + 1)
                            pool.sem_inc(s_pool_passed, 1)
                            own = prob[i][:, :, 0:P]
                            pool.affine_select(own, own, pattern=[[0, GH], [1, P]], compare_op=ALU.is_ge, fill=0.0,
                                               base=0, channel_multiplier=-1).then_inc(s_causal, 1)

            over_batches(pool, body)

        @block.vector
        def _(dve):
            for k in range(NK):
                dve.wait_ge(s_w_hi, k + 1)
                dve.tensor_tensor(w[:, LO, k, :], raw_w[k], w[:, HI, k, :].bitcast(F32), ALU.subtract).then_inc(s_w_lo, 1)
            dve.wait_ge(s_aw_hi, 1)
            dve.tensor_tensor(aw[:, LO, :, :], raw_aw, aw[:, HI, :, :].bitcast(F32), ALU.subtract).then_inc(s_aw_lo, 1)
            dve.wait_ge(s_const, 6 * 16)
            dve.tensor_copy(ident_b[:, :], ident[:, :]).then_inc(s_av, 1)
            dve.wait_ge(s_ak_mm, 1)
            for c in range(NK):
                ins = dve.tensor_tensor(
                    ak_full[:, 8 * c:8 * c + 8, :],
                    ps[:, SH, c * NA:(c + 1) * NA].rearrange("p (o a) -> p o a", o=1).broadcast_to([P, 8, NA]),
                    ak_mask[:, :].rearrange("p (h o) -> p h o", o=1).broadcast_to([P, 8, NA]), ALU.mult)
            ins.then_inc(s_free[0], 1)
            dve.wait_ge(s_free[0], 1)
            flat = ak_full[:, :, :].rearrange("p h a -> p (h a)")

            def ak_part(i):
                return ak[:, i, :, :].rearrange("p c a -> p (c a)")

            dve.tensor_copy(ak_part(0), flat).then_inc(s_ak, 1)
            dve.wait_ge(s_ak, 1)
            dve.tensor_tensor(ak_rest, flat, ak_part(0), ALU.subtract).then_inc(s_ak, 1)
            dve.wait_ge(s_ak, 2)
            dve.tensor_copy(ak_part(1), ak_rest).then_inc(s_ak, 1)
            dve.wait_ge(s_ak, 3)
            dve.tensor_tensor(ak_part(2), ak_rest, ak_part(1), ALU.subtract).then_inc(s_ak, 1)
            dve.wait_ge(s_av_mm, 1)
            dve.tensor_tensor(av[:, :].rearrange("p (c d) -> p c d", c=NK), ps[0:8 * NA, SH + 1, :].rearrange("p (c d) -> p c d", c=NK),
                              av_mask[:, :].rearrange("p (o d) -> p o d", o=1).broadcast_to([8 * NA, NK, P]),
                              ALU.mult).then_inc(s_free[1], 1)
            dve.wait_ge(s_ak, 4)
            dve.wait_ge(s_free[1], 1)

            def body(b):
                for step in steps:
                    kind, *a = step
                    if kind == "norm":
                        dve.wait_ge(s_x, (b + 1) * 16)
                        layernorm(dve, xa, ln, (s_ln, b * LN_STEPS))
                        for t in range(NT):
                            dve.tensor_scalar(xa[:, t, :], xa[:, t, :], ln["mean"][:, t:t + 1], ln["rstd"][:, t:t + 1],
                                              ALU.subtract, ALU.mult).then_inc(s_norm, 1)
                    if kind == "xt":
                        k, = a
                        dve.wait_ge(s_xhi, b * NK + k + 1)
                        dve.tensor_tensor(xT[:, LO, k, :], shared(step), xT[:, HI, k, :].bitcast(F32),
                                          ALU.subtract).then_inc(free(step), 1)
                    if kind == "qkv":
                        t, = a
                        n = b * NT + t
                        dve.wait_ge(s_qk, n + 1)
                        wait(dve, s_turned, n - 1)
                        both = ps[:, 2 * (t % 2):2 * (t % 2) + 2, :].rearrange("p w (g c) -> p (w g) c", c=64)
                        ra, rb = (x[t % 2].rearrange("p (g c) -> p g c", c=64) for x in (rope_a, rope_b))

                        def table(x, lo, hi):
                            return x[:, t, lo:hi].rearrange("p (o c) -> p o c", o=1).broadcast_to([P, 2 * G, hi - lo])

                        dve.tensor_tensor(ra, both, table(cos, 0, 64), ALU.mult).then_inc(s_rope, 1)
                        dve.tensor_tensor(rb[:, :, 0:32], both[:, :, 32:64], table(sin, 0, 32), ALU.mult).then_inc(s_rope, 1)
                        dve.tensor_tensor(rb[:, :, 32:64], both[:, :, 0:32], table(sin, 32, 64), ALU.mult).then_inc(s_rope, 1)
                    if kind == "tr":
                        c, which = a
                        n = 2 * (b * NK + c) + which
                        dve.wait_ge(s_hi, n + 1)
                        dve.tensor_tensor(rest[:, which, :], shared(step), parts[:, which, 0, :], ALU.subtract).then_inc(free(step), 1)
                    if kind == "cut":
                        c, which = a
                        n = 2 * (b * NK + c) + which
                        dve.wait_ge(s_mid, n + 1)
                        dve.tensor_tensor(parts[:, which, 2, :], rest[:, which, :], parts[:, which, 1, :], ALU.subtract).then_inc(s_parts, 1)
                    if kind == "max":
                        g, u = a
                        t, h0, nh = UNITS[u]
                        n, m = b * G + g, P * (t + 1)
                        bank = SMAX + (g * NU + u) % 2
                        dve.wait_ge(s_smm, n * NU + u + 1)
                        dve.tensor_reduce(top[:, t, h0:h0 + nh], ps[:, bank, 0:nh * m].rearrange("p (h k) -> p h k", h=nh),
                                          AX, ALU.max).then_inc(s_max, 1)
                    if kind == "neg":
                        g, = a
                        n = b * G + g
                        dve.wait_ge(s_max, (n + 1) * NU)
                        wait(dve, s_topT, n)
                        hi, mid, lo = (top_parts[:, :, i, :] for i in range(3))
                        dve.tensor_scalar(hi, top[:, :, :], -1.0, None, ALU.mult).then_inc(s_top, 1)
                        dve.wait_ge(s_top, 4 * n + 1)
                        dve.scalar_tensor_tensor(out=top_rest[:, :, :], in0=top[:, :, :], scalar=-1.0, in1=hi,
                                                 op0=ALU.mult, op1=ALU.subtract).then_inc(s_top, 1)
                        dve.wait_ge(s_top, 4 * n + 2)
                        dve.tensor_copy(mid, top_rest[:, :, :]).then_inc(s_top, 1)
                        dve.wait_ge(s_top, 4 * n + 3)
                        dve.tensor_tensor(lo, top_rest[:, :, :], mid, ALU.subtract).then_inc(s_top, 1)
                    if kind == "ascore":
                        c, = a
                        n = b * NK + c
                        s = shared(step)[:, 0:NT * 8 * NA].rearrange("p (h a) -> p h a", a=NA)

                        def wide(x):
                            return x[:, :].rearrange("p (h o) -> p h o", o=1).broadcast_to([P, NT * 8, NA])

                        dve.wait_ge(s_amm, n + 1)
                        wait(dve, s_aT, n)
                        dve.tensor_reduce(a_max[:, :], s, AX, ALU.max).then_inc(s_amax, 1)
                        dve.wait_ge(s_amax, n + 1)
                        dve.tensor_tensor(a_prob[:, :, :], s, wide(a_max), ALU.subtract).then_inc(free(step), 1)
                        dve.wait_ge(s_aexp, n + 1)
                        dve.tensor_reduce(a_sum[:, :], a_prob[:, :, :], AX, ALU.add).then_inc(s_asum, 1)
                        dve.wait_ge(s_asum, n + 1)
                        dve.reciprocal(a_sum[:, :], a_sum[:, :]).then_inc(s_ascale, 1)
                        dve.wait_ge(s_ascale, 2 * n + 1)
                        dve.tensor_scalar(a_sum[:, :], a_sum[:, :], gate[:, 0:1], None, ALU.mult).then_inc(s_ascale, 1)
                        dve.wait_ge(s_ascale, 2 * n + 2)
                        dve.tensor_tensor(a_prob[:, :, :], a_prob[:, :, :], wide(a_sum), ALU.mult).then_inc(s_anorm, 1)
                    if kind == "oT":
                        g, = a
                        n = b * G + g
                        s = shared(step).rearrange("p (t h c) -> p t h c", t=NT, h=GH)
                        dve.wait_ge(s_oT, n + 1)
                        dve.reciprocal(rsum[:, :, :], s[:, :, :, HD]).then_inc(s_rsum, 1)
                        dve.wait_ge(s_rsum, n + 1)
                        dve.tensor_tensor(o_part[:, :, :, :], s[:, :, :, 0:HD],
                                          rsum[:, :, :].rearrange("p t (h o) -> p t h o", o=1).broadcast_to([P, NT, GH, HD]),
                                          ALU.mult).then_inc(free(step), 1)
                        dve.wait_ge(*read(b, step))
                        own = y[:, :, g * GH * HD:(g + 1) * GH * HD]
                        dve.wait_ge(*read(b, ("aout", g // 2)))
                        dve.tensor_tensor(own, own, o_part[:, :, :, :].rearrange("p t h d -> p t (h d)"), ALU.add).then_inc(s_y, 1)
                    if kind == "yt":
                        k, = a
                        dve.wait_ge(s_yhi, b * NK + k + 1)
                        dve.tensor_tensor(xT[:, LO, k, :], shared(step), xT[:, HI, k, :].bitcast(F32),
                                          ALU.subtract).then_inc(free(step), 1)
                    if kind == "proj":
                        t, = a
                        n = b * NT + t
                        dve.wait_ge(s_proj, n + 1)
                        dve.wait_ge(s_res_in[t % 2], (b * (NT // 2) + t // 2 + 1) * 16)
                        dve.tensor_tensor(res[:, t % 2, :], ps[:, SMAX + t % 2, :], res[:, t % 2, :], ALU.add).then_inc(s_res, 1)

            over_batches(dve, body)


def macaron(nc, x, w_qkvT, w_projT, wte, gating, w_gateT, w_upT, w_downT, cos, sin, ident, ak_mask, av_mask, out):
    h1 = nc.dram_tensor("h1", [NB * T, C], F32).ap()
    h2 = nc.dram_tensor("h2", [NB * T, C], F32).ap()
    consts = {"cos": cos, "sin": sin, "ident": ident, "ak_mask": ak_mask, "av_mask": av_mask}
    ffn_phase(nc, "f1", x, h1, w_gateT, w_upT, w_downT, ident)
    attention_phase(nc, h1, h2, w_qkvT, w_projT, wte, gating, consts)
    ffn_phase(nc, "f2", h2, out, w_gateT, w_upT, w_downT, ident)


def shape_constants():
    theta = np.float32(1.0) / np.power(np.float32(10000.0), np.arange(0, HD, 2, dtype=np.float32) / np.float32(HD))
    angle = np.outer(np.arange(T, dtype=np.float32), theta.astype(np.float32)).astype(np.float32)
    cos, sin = np.cos(angle), np.sin(angle)
    head_of_row = np.arange(P) // 64 * GH + np.arange(P) % GH
    head_of_pair = np.arange(8 * NA) // NA
    return {
        "cos": np.repeat(np.concatenate([cos, cos], 1), GH, axis=1),
        "sin": np.repeat(np.concatenate([-sin, sin], 1), GH, axis=1),
        "ident": np.eye(P, dtype=np.float32),
        "ak_mask": (head_of_row[:, None] == np.arange(8)).astype(np.float32),
        "av_mask": (head_of_pair[:, None] == np.arange(P) // HD).astype(np.float32),
    }


_NAMES = ["x", "w_qkvT", "w_projT", "wte", "gating", "w_gateT", "w_upT", "w_downT", "cos", "sin", "ident", "ak_mask", "av_mask"]


def lay_out(x, w_attn, w_proj, adapter_wte, gating, w_gate, w_up, w_down):
    qk = w_attn[:2 * C].reshape(2, G, GH, HD, C).transpose(0, 1, 3, 2, 4).reshape(2 * C, C)
    arrays = {
        "x": x.reshape(NB * T, C), "w_qkvT": np.concatenate([qk, w_attn[2 * C:]]).T, "w_projT": w_proj.T,
        "wte": np.tile(adapter_wte.T, (1, 8)), "gating": gating, "w_gateT": w_gate.T, "w_upT": w_up.T, "w_downT": w_down.T,
    }
    arrays.update(shape_constants())
    return {name: np.ascontiguousarray(arrays[name]) for name in _NAMES}


def kernel(L0_attn_x, L0_attn_w_attn, L0_attn_w_proj, L0_attn_adapter_wte, L0_attn_gating,
           L0_ffn_w_gate, L0_ffn_w_up, L0_ffn_w_down):
    import concourse.bacc as _bacc
    from concourse import mybir as _mybir
    from concourse.bass_utils import run_bass_kernel_spmd as _run

    arrays = lay_out(*(np.asarray(a) for a in (
        L0_attn_x, L0_attn_w_attn, L0_attn_w_proj, L0_attn_adapter_wte, L0_attn_gating,
        L0_ffn_w_gate, L0_ffn_w_up, L0_ffn_w_down)))
    nc = _bacc.Bacc("TRN2", target_bir_lowering=False, num_devices=1)
    args = [nc.dram_tensor(f"in_{n}", arrays[n].shape, _mybir.dt.from_np(arrays[n].dtype), kind="ExternalInput").ap()
            for n in _NAMES]
    out = nc.dram_tensor("out_y", [NB * T, C], _mybir.dt.float32, kind="ExternalOutput").ap()
    macaron(nc, *args, out)
    r = _run(nc, [{f"in_{n}": arrays[n] for n in _NAMES}], core_ids=[0])
    return r.results[0]["out_y"].reshape(NB, T, C)
```

```python
from contextlib import ExitStack

import numpy as np

import concourse.bass as bass
from concourse import mybir

F32 = mybir.dt.float32
F32R = mybir.dt.float32r
BF16 = mybir.dt.bfloat16
I32 = mybir.dt.int32
ALU = mybir.AluOpType
ACT = mybir.ActivationFunctionType
AX = mybir.AxisListType.X

P = 128
C = 512
T = 512
NB = 4
NT = T // P
NK = C // P
INTER = 1376
NJ = -(-INTER // P)
H, HD = 32, 16
G = 8
GH = H // G
NA = 10
EPS = 1e-5
ROUND = 1.5 * 2.0 ** 23
RSQRT_SEED = 1597463007.0
HI, LO = 0, 1


def wait(eng, sem, value):
    if not isinstance(value, int) or value > 0:
        eng.wait_ge(sem, value)


def over_blocks(eng, body, last=True):
    body(0, True, False)
    with eng.Fori(1, NB - 1 if last else NB) as b:
        body(b, False, False)
    if last:
        body(NB - 1, False, True)


def rows(j):
    return min(P, INTER - j * P)


def row_statistics(eng, x, st, t):
    return eng.bn_stats(st["stats"][:, t, :], x[:, t, :])


def inverse_deviation(eng, st, counter, before):
    n = 0

    def step(ins):
        nonlocal n
        ins.then_inc(counter, 1)
        n += 1

    def chained():
        eng.wait_ge(counter, before + n)

    stats, mean, var, rstd, a, d = (st[k] for k in ("stats", "mean", "var", "rstd", "a", "d"))
    chained()
    step(eng.tensor_tensor(mean[:, :], stats[:, :, 1], stats[:, :, 4], ALU.add))
    step(eng.tensor_tensor(d[:, :], stats[:, :, 1], stats[:, :, 4], ALU.subtract))
    step(eng.tensor_tensor(var[:, :], stats[:, :, 2], stats[:, :, 5], ALU.add))
    chained()
    step(eng.tensor_scalar(mean[:, :], mean[:, :], 0.5, None, ALU.mult))
    step(eng.scalar_tensor_tensor(out=d[:, :], in0=d[:, :], scalar=0.25, in1=d[:, :], op0=ALU.mult, op1=ALU.mult))
    step(eng.tensor_scalar(var[:, :], var[:, :], 1.0 / C, EPS, ALU.mult, ALU.add))
    chained()
    step(eng.tensor_tensor(var[:, :], var[:, :], d[:, :], ALU.add))
    chained()
    step(eng.tensor_scalar(rstd[:, :].bitcast(I32), var[:, :].bitcast(I32), -0.5, RSQRT_SEED, ALU.mult, ALU.add))
    for _ in range(3):
        chained()
        step(eng.tensor_tensor(a[:, :], rstd[:, :], rstd[:, :], ALU.mult))
        chained()
        step(eng.scalar_tensor_tensor(out=a[:, :], in0=a[:, :], scalar=-0.5, in1=var[:, :], op0=ALU.mult, op1=ALU.mult))
        chained()
        step(eng.scalar_tensor_tensor(out=rstd[:, :], in0=a[:, :], scalar=1.5, in1=rstd[:, :], op0=ALU.add, op1=ALU.mult))
    assert n == LN_STEPS


LN_STEPS = 7 + 1 + 9


def normalise_tile(eng, x, st, t):
    return eng.tensor_scalar(x[:, t, :], x[:, t, :], st["mean"][:, t:t + 1], st["rstd"][:, t:t + 1], ALU.subtract, ALU.mult)


class Shared:

    def __init__(self, nc, ctx):
        def sb(name, shape, dt=F32):
            return ctx.enter_context(nc.sbuf_tensor(f"all_{name}", shape, dt))

        def sem(name):
            return ctx.enter_context(nc.semaphore(f"all_{name}"))

        def over(*tensors):
            with ExitStack() as here:
                return [here.enter_context(nc.sbuf_tensor(f"all_{name}", shape, dt)) for name, shape, dt in tensors]

        self.w_gu, = over(("w_gu", [P, 2, 2, NK, INTER], F32R))
        w_qkv = ("w_qkv", [P, 2, NK, 3 * C], F32R)
        w_proj = ("w_proj", [P, 2, NK, C], F32R)
        with nc.sbuf_tensor("all_" + w_qkv[0], *w_qkv[1:]) as self.w_qkv:
            self.raw_late, = over(("raw_qkv_late", [P, 2, 3 * C], F32))
            with nc.sbuf_tensor("all_" + w_proj[0], *w_proj[1:]) as self.w_proj:
                self.qk, self.parts = over(("qk", [P, NT, 2 * C], F32), ("parts", [P, 2, 3, T], BF16))
                self.last_yT, = over(("last_yT", [P, 2, NK, T], F32R))
        sb("weights_space", [P, 4 * NK * INTER])
        self.staging = sb("staging", [P, 6 * C])
        self.xa = sb("xa", [P, NT, C])
        self.xT = sb("xT", [P, 2, NK, T], F32R)
        self.res = sb("res", [P, 2, C])
        self.ident = sb("ident", [P, P])
        self.ln = {k: sb(k, [P, NT]) for k in ("mean", "var", "rstd", "a", "d")}
        self.ln["stats"] = sb("stats", [P, NT, 6])
        self.s_x, self.s_ln, self.s_norm, self.s_tr, self.s_hi = map(
            sem, ("x_loaded", "ln_steps", "normalised", "x_transposed", "xT_hi"))
        self.s_store = [sem(f"stored{i}") for i in range(2)]
        self.s_w = [sem(f"qkv_w{k}_loaded") for k in range(NK)]
        self.s_w_hi, self.s_w_lo = sem("qkv_w_hi"), sem("qkv_w_lo")

    def raw_gate_up(self):
        return self.staging[:, 0:4 * C].rearrange("p (i w k m) -> p i w k m", i=2, w=2, k=NK)

    def raw_down(self):
        return self.staging[:, 4 * C:6 * C].rearrange("p (i c) -> p i c", i=2)

    def raw_qkv(self, k):
        if k < 2:
            return self.staging[:, 3 * C * k:3 * C * (k + 1)]
        return self.raw_late[:, k - 2, :]


def load_raw_gate_up(eng, raw_gu, gT, uT, j, counters):
    m = rows(j)
    for i, w in enumerate((gT, uT)):
        eng.dma_start(raw_gu[:, j % 2, i, :, 0:m], w[:, :, j * P:j * P + m]).then_inc(counters[j % 2], 16)


def load_raw_down(eng, raw_dn, wdT, j, counters):
    eng.dma_start(raw_dn[0:rows(j), j % 2, :], wdT[j * P:j * P + rows(j), :]).then_inc(counters[j % 2], 16)


def ffn_phase(nc, sh, tag, base, x_src, x_dst, wgT, wuT, wdT, ident_dram, wqkvT=None):
    leads = wqkvT is not None
    with ExitStack() as ctx:
        def sb(name, shape, dt=F32):
            return ctx.enter_context(nc.sbuf_tensor(f"{tag}_{name}", shape, dt))

        def sem(name):
            return ctx.enter_context(nc.semaphore(f"{tag}_{name}"))

        w_gu, raw_gu, raw_dn = sh.w_gu, sh.raw_gate_up(), sh.raw_down()
        xa, xT, res, ident, ln = sh.xa, sh.xT, sh.res, sh.ident, sh.ln
        w_dn = sb("w_dn", [P, 2, NJ, C], F32R)
        inter = sb("inter", [P, NJ, T], F32R)
        silu = sb("silu", [P, 2, T])
        clipped = sb("clipped", [P, T])
        rounded = sb("rounded", [P, T])
        over = sb("over", [P, T])
        under = sb("under", [P, T])
        ps = ctx.enter_context(nc.psum_tensor(f"{tag}_ps", [P, 8, 512], F32))
        GATE, UP, DOWN, TR = 0, 2, 4, 6

        s_ident, s_x, s_store = sem("ident"), sh.s_x, sh.s_store
        s_raw_gu, s_raw_dn, s_res_in = (
            [sem(f"{name}{i}") for i in range(2)] for name in ("raw_gu_loaded", "raw_dn_loaded", "res_loaded"))
        s_x_first = [sem(f"first_x_loaded{t}") for t in range(NT)]
        s_w_hi, s_gate_lo, s_up_lo, s_dn_hi, s_dn_lo = map(sem, ("w_hi", "gate_lo", "up_lo", "dn_hi", "dn_lo"))
        s_ln, s_norm, s_tr, s_hi, s_lo = sh.s_ln, sh.s_norm, sh.s_tr, sh.s_hi, sem("xT_lo")
        s_gate, s_up, s_silu, s_prod = map(sem, ("gate", "up", "silu_done", "product"))
        s_clip, s_round, s_over, s_under, s_floor, s_trunc = map(
            sem, ("clip", "round", "over_s", "under_s", "floor", "trunc"))
        s_down, s_down_read, s_res = map(sem, ("down", "down_read", "res_done"))

        src = x_src.rearrange("(b t p) c -> p b t c", p=P, t=NT)
        dst = x_dst.rearrange("(b t p) c -> p b t c", p=P, t=NT)
        gT = wgT.rearrange("(k p) i -> p k i", p=P)
        uT = wuT.rearrange("(k p) i -> p k i", p=P)
        TILES = NJ + NT
        FOUND = 0 if leads else 1
        STORED = base * (NT // 2) * 16

        def lo_done(b, k):
            return (b - FOUND) * NK + k + 1

        block = ctx.enter_context(nc.Block())

        def at(b):
            return bass.ds(b, 1)

        @block.sync
        def _(sp):
            def load_x(b):
                wait(sp, s_tr, (base + b) * NK)
                sp.dma_start(xa[:, :, :], src[:, at(b), :, :]).then_inc(s_x, 16)

            def load_raw(j):
                wait(sp, s_gate_lo, j - 1)
                wait(sp, s_up_lo, j - 1)
                load_raw_gate_up(sp, raw_gu, gT, uT, j, s_raw_gu)
                wait(sp, s_dn_lo, j - 1)
                load_raw_down(sp, raw_dn, wdT, j, s_raw_dn)

            def load_next_phase():
                sp.wait_ge(s_tr, NB * NK)
                for i in range(2):
                    sp.wait_ge(s_store[i], (NT // 2) * 16)
                sp.dma_start(xa[:, :, :], dst[:, 0, :, :]).then_inc(s_x, 16)
                for cut in (s_gate_lo, s_up_lo, s_dn_lo):
                    sp.wait_ge(cut, NJ)
                for k in range(2):
                    sp.dma_start(sh.raw_qkv(k), wqkvT[k * P:(k + 1) * P, :]).then_inc(sh.s_w[k], 16)

            def load_next_weights():
                sp.wait_ge(s_gate, NB * NJ)
                sp.wait_ge(s_up, NB * NJ)
                for k in range(2, NK):
                    sp.dma_start(sh.raw_qkv(k), wqkvT[k * P:(k + 1) * P, :]).then_inc(sh.s_w[k], 16)

            if leads:
                for t in range(0, NT, 2):
                    sp.dma_start(xa[:, t, :], src[:, 0, t, :]).then_inc(s_x_first[t], 16)
                load_raw(0)
                sp.dma_start(ident[:, :], ident_dram).then_inc(s_ident, 16)
                load_raw(1)

            def body(b, first, last):
                if first:
                    for j in range(2, NJ):
                        load_raw(j)
                        if j == 2:
                            load_x(1)
                elif not last:
                    load_x(b + 1)
                elif leads:
                    load_next_phase()
                for t in range(2):
                    wait(sp, s_store[t], STORED + b * (NT // 2) * 16)
                    sp.dma_start(res[:, t, :], src[:, at(b), t, :]).then_inc(s_res_in[t], 16)
                if last and leads:
                    load_next_weights()
                for t in range(NT):
                    i, used = t % 2, b * (NT // 2) + t // 2 + 1
                    sp.wait_ge(s_res, b * NT + t + 1)
                    sp.dma_start(dst[:, at(b), t, :], res[:, i, :]).then_inc(s_store[i], 16)
                    if t + 2 < NT:
                        sp.wait_ge(s_store[i], STORED + used * 16)
                        sp.dma_start(res[:, i, :], src[:, at(b), t + 2, :]).then_inc(s_res_in[i], 16)

            over_blocks(sp, body)
            if not leads:
                for i in range(2):
                    sp.wait_ge(s_store[i], STORED + NB * (NT // 2) * 16)

        @block.tensor
        def _(pe):
            def transpose_x(b, k):
                wait(pe, s_lo, lo_done(b, k - 2))
                pe.wait_ge(s_norm, (base + b + 1) * NT)
                for t in range(NT):
                    last = pe.transpose(ps[:, TR + k % 2, t * P:(t + 1) * P], xa[:, t, k * P:(k + 1) * P], ident[:, :])
                last.then_inc(s_tr, 1)

            def gate_up(b, j):
                n = b * NJ + j
                m = rows(j)
                for which, bank, free, done, cut in ((0, GATE, s_silu, s_gate, s_gate_lo), (1, UP, s_prod, s_up, s_up_lo)):
                    wait(pe, free, n - 1)
                    pe.wait_ge(cut, j + 1)
                    out = ps[0:m, bank + j % 2, :]
                    for k in range(NK):
                        cols = slice(j * P, j * P + m)
                        pe.matmul(out, w_gu[:, HI, which, k, cols], xT[:, HI, k, :], start=(k == 0), stop=False)
                        pe.matmul(out, w_gu[:, HI, which, k, cols], xT[:, LO, k, :], start=False, stop=False)
                        mm = pe.matmul(out, w_gu[:, LO, which, k, cols], xT[:, HI, k, :], start=False, stop=(k == NK - 1))
                    mm.then_inc(done, 1)

            def down(b, t, first):
                n = b * NT + t
                wait(pe, s_down_read, n - 1)
                out = ps[:, DOWN + t % 2, :]
                for j in range(NJ):
                    m = rows(j)
                    if t == 0 and j >= NJ - 3:
                        pe.wait_ge(s_trunc, b * TILES + j + 1)
                    if first and t == 0 and j == NJ - 1:
                        pe.wait_ge(s_dn_lo, NJ)
                    for part in (HI, LO):
                        mm = pe.matmul(out, inter[0:m, j, t * P:(t + 1) * P], w_dn[0:m, part, j, :],
                                       start=(j == 0 and part == HI), stop=(j == NJ - 1 and part == LO))
                mm.then_inc(s_down, 1)

            if leads:
                pe.wait_ge(s_ident, 16)
                for k in range(NK):
                    transpose_x(0, k)

            def body(b, first, last):
                wait(pe, s_lo, lo_done(b, NK - 1))
                for j in range(NJ):
                    gate_up(b, j)
                if first:
                    pe.wait_ge(s_dn_lo, NJ - 1)
                pe.wait_ge(s_trunc, b * TILES + NJ - 3)
                for t in range(NT):
                    if leads or not last:
                        transpose_x(b + 1, t)
                    down(b, t, first)

            over_blocks(pe, body)

        @block.scalar
        def _(act):
            def cut_hi(b, k):
                act.wait_ge(s_tr, (base + b) * NK + k + 1)
                act.activation(xT[:, HI, k, :], ps[:, TR + k % 2, :], ACT.Copy).then_inc(s_hi, 1)

            def cut_weights(j):
                m = rows(j)
                wait(act, s_raw_gu[j % 2], 32 * (j // 2 + 1 - FOUND))
                act.activation(w_gu[:, HI, :, :, j * P:j * P + m], raw_gu[:, j % 2, :, :, 0:m], ACT.Copy).then_inc(s_w_hi, 1)
                wait(act, s_raw_dn[j % 2], 16 * (j // 2 + 1 - FOUND))
                act.activation(w_dn[0:m, HI, j, :], raw_dn[0:m, j % 2, :], ACT.Copy).then_inc(s_dn_hi, 1)

            if leads:
                for t in range(1, NT, 2):
                    act.dma_start(xa[:, t, :], src[:, 0, t, :]).then_inc(s_x_first[t], 16)
            cut_weights(0)
            if leads:
                for k in range(NK):
                    cut_hi(0, k)
            cut_weights(1)

            def body(b, first, last):
                for j in range(NJ):
                    n = b * NJ + j
                    m = rows(j)
                    act.wait_ge(s_gate, n + 1)
                    wait(act, s_prod, n - 1)
                    act.activation(silu[0:m, j % 2, :], ps[0:m, GATE + j % 2, :], ACT.Silu, scale=1.0 / 128).then_inc(s_silu, 1)
                    if first and j + 2 < NJ:
                        cut_weights(j + 2)
                for k in range(NK):
                    if leads or not last:
                        cut_hi(b + 1, k)
                    if leads and last:
                        if k == 0:
                            act.wait_ge(s_up, NB * NJ)
                        act.wait_ge(sh.s_w[k], 16)
                        act.activation(sh.w_qkv[:, HI, k, :], sh.raw_qkv(k), ACT.Copy).then_inc(sh.s_w_hi, 1)

            over_blocks(act, body)

        @block.gpsimd
        def _(pool):
            def cut_weights(j):
                m = rows(j)
                pool.wait_ge(s_w_hi, j + 1)
                pool.tensor_tensor(w_gu[:, LO, 1, :, j * P:j * P + m], raw_gu[:, j % 2, 1, :, 0:m],
                                   w_gu[:, HI, 1, :, j * P:j * P + m].bitcast(F32), ALU.subtract).then_inc(s_up_lo, 1)
                pool.wait_ge(s_dn_hi, j + 1)
                pool.tensor_tensor(w_dn[0:m, LO, j, :], raw_dn[0:m, j % 2, :], w_dn[0:m, HI, j, :].bitcast(F32),
                                   ALU.subtract).then_inc(s_dn_lo, 1)

            for j in range(NJ):
                cut_weights(j)
            if leads:
                for k in range(NK):
                    pool.wait_ge(sh.s_w_hi, k + 1)
                    pool.tensor_tensor(sh.w_qkv[:, LO, k, :], sh.raw_qkv(k), sh.w_qkv[:, HI, k, :].bitcast(F32),
                                       ALU.subtract).then_inc(sh.s_w_lo, 1)

        @block.vector
        def _(dve):
            def cut_lo(b, k):
                dve.wait_ge(s_hi, (base + b) * NK + k + 1)
                dve.tensor_tensor(xT[:, LO, k, :], ps[:, TR + k % 2, :], xT[:, HI, k, :].bitcast(F32),
                                  ALU.subtract).then_inc(s_lo, 1)

            def cut_weights(j):
                m = rows(j)
                dve.wait_ge(s_w_hi, j + 1)
                dve.tensor_tensor(w_gu[:, LO, 0, :, j * P:j * P + m], raw_gu[:, j % 2, 0, :, 0:m],
                                  w_gu[:, HI, 0, :, j * P:j * P + m].bitcast(F32), ALU.subtract).then_inc(s_gate_lo, 1)

            def statistics(b, t):
                if isinstance(b, int) and b == 0:
                    dve.wait_ge(s_x_first[t], 16)
                else:
                    dve.wait_ge(s_x, (base + b) * 16)
                row_statistics(dve, xa, ln, t).then_inc(s_ln, 1)

            def normalise(b, t):
                if t == 0:
                    before = (base + b) * (NT + LN_STEPS) + NT
                    inverse_deviation(dve, ln, s_ln, before)
                    dve.wait_ge(s_ln, before + LN_STEPS)
                normalise_tile(dve, xa, ln, t).then_inc(s_norm, 1)

            def truncate(out, m, n):
                c, r = clipped[0:m, :], rounded[0:m, :]
                dve.wait_ge(s_clip, n + 1)
                dve.tensor_scalar(r, c, ROUND, -ROUND, ALU.add, ALU.add).then_inc(s_round, 1)
                dve.wait_ge(s_round, n + 1)
                dve.scalar_tensor_tensor(out=over[0:m, :], in0=c, scalar=0.0, in1=r,
                                         op0=ALU.max, op1=ALU.is_lt).then_inc(s_over, 1)
                dve.scalar_tensor_tensor(out=under[0:m, :], in0=c, scalar=0.0, in1=r,
                                         op0=ALU.min, op1=ALU.is_gt).then_inc(s_under, 1)
                dve.wait_ge(s_over, n + 1)
                dve.tensor_tensor(r, r, over[0:m, :], ALU.subtract).then_inc(s_floor, 1)
                dve.wait_ge(s_under, n + 1)
                dve.wait_ge(s_floor, n + 1)
                dve.tensor_tensor(out, r, under[0:m, :], ALU.add).then_inc(s_trunc, 1)

            def quantise_inner(b, j):
                n, m = b * TILES + j, rows(j)
                dve.wait_ge(s_silu, b * NJ + j + 1)
                dve.wait_ge(s_up, b * NJ + j + 1)
                dve.tensor_tensor(clipped[0:m, :], silu[0:m, j % 2, :], ps[0:m, UP + j % 2, :], ALU.mult).then_inc(s_prod, 1)
                dve.wait_ge(s_prod, b * NJ + j + 1)
                dve.tensor_scalar(clipped[0:m, :], clipped[0:m, :], -128.0, 127.0, ALU.max, ALU.min).then_inc(s_clip, 1)
                truncate(inter[0:m, j, :], m, n)

            def finish(b, t):
                n = b * TILES + NJ + t
                dve.wait_ge(s_down, b * NT + t + 1)
                dve.tensor_scalar(clipped[:, :], ps[:, DOWN + t % 2, :], 128.0, 127.0, ALU.mult, ALU.min).then_inc(s_down_read, 1)
                dve.wait_ge(s_down_read, b * NT + t + 1)
                dve.tensor_scalar(clipped[:, :], clipped[:, :], -128.0, None, ALU.max).then_inc(s_clip, 1)
                truncate(over[:, :], P, n)
                dve.wait_ge(s_trunc, n + 1)
                dve.wait_ge(s_res_in[t % 2], (b * (NT // 2) + t // 2 + 1) * 16)
                dve.scalar_tensor_tensor(out=res[:, t % 2, :], in0=over[:, :], scalar=0.5, in1=res[:, t % 2, :],
                                         op0=ALU.mult, op1=ALU.add).then_inc(s_res, 1)

            if leads:
                for t in range(NT):
                    statistics(0, t)
                for t in range(NT):
                    normalise(0, t)
            cut_weights(0)
            if leads:
                for k in range(NK):
                    cut_lo(0, k)
            cut_weights(1)

            def body(b, first, last):
                for j in range(NJ):
                    if first and j + 2 < NJ:
                        cut_weights(j + 2)
                    quantise_inner(b, j)
                    start = 2 if first else 1
                    ahead = leads or not last
                    if ahead and start <= j < start + NT:
                        statistics(b + 1, j - start)
                    if ahead and start + NT <= j < start + 2 * NT:
                        normalise(b + 1, j - start - NT)
                for t in range(NT):
                    if leads or not last:
                        cut_lo(b + 1, t)
                    if t:
                        finish(b, t - 1)
                finish(b, NT - 1)

            over_blocks(dve, body)


UNITS = [(0, 0, 4), (1, 0, 2), (1, 2, 2)] + [(t, h, 1) for t in (2, 3) for h in range(GH)]
KEY_UNITS = [(NT - 1 - t, h, n) for t, h, n in sorted(UNITS, key=lambda u: (-u[0], u[1]))]
NU = len(UNITS)
PART_Q = (0, 0, 1, 0, 2, 1)
PART_K = (0, 1, 0, 2, 0, 1)
NS = len(PART_Q)
KROWS = NS * HD
SLOTS = 4


def step_lists():
    def maxima(d, g, us):
        return [(d, "max", g, u) for u in us]

    def cut(d, c):
        return [(d, kind, c, which) for kind in ("rest", "mid", "low") for which in range(2)]

    def bridge(d, done):
        out = [(d, "v", 0), (d, "tr", 0, 0), (d, "tr", 0, 1), (d, "v", 1)] + cut(d, 0)
        out += [(d, "stack", 0), *done["oT"], (d, "v", 2), (d, "stack", 1), (d, "ascore", 0), *done["onorm"], (d, "v", 3), (d, "anorm", 0)]
        out += done["yt"]
        out += [(d, "tr", 1, 0), (d, "tr", 1, 1)] + maxima(d, 0, range(0, 3)) + cut(d, 1)[:4] + done["proj"][0]
        out += maxima(d, 0, range(3, 7)) + cut(d, 1)[4:] + [(d, "stack", 2)] + done["proj"][1] + maxima(d, 0, range(7, NU))
        out += [(d, "neg", 0)] + maxima(d, 1, range(0, 2)) + done["proj"][2] + maxima(d, 1, range(2, 4)) + [(d, "mrow", 0)]
        out += maxima(d, 1, range(4, 8)) + done["proj"][3] + maxima(d, 1, range(8, NU)) + [(d, "neg", 1), (d, "amix", 0), (d, "mrow", 1)]
        return out + [(d, "stack", 3)]

    nothing = {"oT": [], "onorm": [], "yt": [], "proj": [[]] * NT}
    finish = {
        "oT": [(0, "oT", G - 1)], "onorm": [(0, "onorm", G - 1)], "yt": [(0, "yt", k) for k in range(NK)],
        "proj": [[(0, "proj", t), (0, "out", t)] for t in range(NT)],
    }
    setup = []
    for i in range(NT):
        setup += [(0, "qk", i), (0, "rope", i)]
        if i == 0:
            setup += [(0, "ak"), (0, "av")]
    setup += bridge(0, nothing)

    extra = {
        (0, 1): [(0, "aout", 0)], (0, 3): [(0, "ascore", 1)], (0, 4): [(0, "anorm", 1)],
        (0, 5): [(0, "tr", 2, 0), (0, "tr", 2, 1)], (0, 6): cut(0, 2)[:2], (0, 7): cut(0, 2)[2:4], (0, 8): cut(0, 2)[4:] + [(0, "amix", 1)],
        (1, 0): [(0, "stack", 4)], (1, 2): [(0, "aout", 1)], (1, 4): [(0, "ascore", 2)], (1, 6): [(0, "anorm", 2)], (1, 9): [(0, "amix", 2)],
        (2, 0): [(0, "stack", 5)], (2, 3): [(0, "aout", 2)], (2, 8): [(0, "tr", 3, 0), (0, "tr", 3, 1)], (2, 9): cut(0, 3)[:2],
        (2, 10): cut(0, 3)[2:4], (3, 0): cut(0, 3)[4:] + [(0, "stack", 6)],
        (3, 4): [(0, "ascore", 3)], (3, 6): [(0, "anorm", 3)], (4, 0): [(0, "stack", 7)], (4, 3): [(0, "amix", 3)], (4, 6): [(0, "aout", 3)],
    }
    ahead = {
        (0, 0): [(1, "load")], (4, 2): [(1, "stats", 0)], (4, 4): [(1, "stats", 1)], (4, 7): [(1, "stats", 2)], (4, 9): [(1, "stats", 3)],
        (4, 10): [(1, "rstd")], (5, 0): [(1, "normal", 0)], (5, 1): [(1, "normal", 1)], (5, 2): [(1, "normal", 2)], (5, 3): [(1, "normal", 3)],
        (5, 5): [(1, "xt", 0)], (5, 7): [(1, "xt", 1)], (5, 9): [(1, "xt", 2)], (6, 0): [(1, "xt", 3)],
        (6, 3): [(1, "qk", 0)], (6, 4): [(1, "rope", 0)], (6, 8): [(1, "qk", 1)], (6, 9): [(1, "rope", 1)],
        (7, 3): [(1, "qk", 2)], (7, 4): [(1, "rope", 2)], (7, 8): [(1, "qk", 3)], (7, 9): [(1, "rope", 3)],
    }

    def batch(last):
        out = []
        for g in range(G):
            for u in range(NU):
                out.append((0, "prob", g, u))
                if g + 2 < G:
                    out.append((0, "max", g + 2, u))
                if u == 1 and g:
                    out += [(0, "pv", g - 1, 2), (0, "pv", g - 1, 3)]
                if u == 2 and g and g + 1 < G:
                    out.append((0, "mrow", g + 1))
                if u == 4 and g:
                    out.append((0, "oT", g - 1))
                if u == 5:
                    out += [(0, "onorm", g - 1)] * (g > 0) + [(0, "pv", g, 0)]
                if u == 9:
                    out.append((0, "pv", g, 1))
                out += extra.get((g, u), [])
                out += [step for step in ahead.get((g, u), []) if not last or step[1] not in ("qk", "rope")]
            if g + 2 < G:
                out.append((0, "neg", g + 2))
        out += [(0, "pv", G - 1, 2), (0, "pv", G - 1, 3)]
        if not last:
            return out + bridge(1, finish)
        out += finish["oT"] + finish["onorm"] + finish["yt"]
        return out + sum(finish["proj"], [])

    return setup, batch(False), batch(True)


SHARED = ("xt", "ak", "av", "tr", "ascore", "amix", "aout", "mrow", "oT", "yt")


def attention_phase(nc, sh, base, x_src, x_dst, wpT, wte, gating, consts, ffn_weights):
    with ExitStack() as ctx:
        def sb(name, shape, dt=F32):
            return ctx.enter_context(nc.sbuf_tensor(f"at_{name}", shape, dt))

        def sem(name):
            return ctx.enter_context(nc.semaphore(f"at_{name}"))

        w, wp, qk, parts, last_yT = sh.w_qkv, sh.w_proj, sh.qk, sh.parts, sh.last_yT
        xa, xT, res, ident, ln = sh.xa, sh.xT, sh.res, sh.ident, sh.ln
        y = sh.staging[:, 0:4 * C].rearrange("p (t c) -> p t c", t=NT)
        rest = sh.staging[:, 4 * C:6 * C].rearrange("p (w t) -> p w t", w=2)
        v = sb("v", [P, NT, H, HD + 1])
        q_stack = sb("q_stack", [KROWS + 3, SLOTS, GH, T], BF16)
        k_stack = sb("k_stack", [KROWS + 3, SLOTS, GH, T], BF16)
        probs = sb("probs", [P, 10 * T])
        o_cols = sb("o_cols", [P, T])
        o_part = sb("o_part", [P, NT, GH, HD])
        rsum = sb("rsum", [P, NT, GH])
        a_prob = sb("a_prob", [P, NT * 8, NA])
        a_max = sb("a_max", [P, NT * 8])
        a_sum = sb("a_sum", [P, NT * 8])
        a_T = sb("a_T", [8 * NA, T])
        ak = sb("ak", [P, 3, NK, 8 * NA], BF16)
        av = sb("av", [8 * NA, C])
        aw = sb("aw", [P, 2, NK, 8 * NA], F32R)
        cos = sb("cos", [P, NT, 64])
        sin = sb("sin", [P, NT, 64])
        ident_b = sb("ident_b", [P, P], BF16)
        neg_mask = sb("neg_mask", [P, P], BF16)
        ak_mask = sb("ak_mask", [P, 8])
        gate = sb("gate", [P, 1])
        top = sb("top", [P, NT, GH])
        top_rest = sb("top_rest", [P, NT, GH])
        top_parts = sb("top_parts", [P, NT, 3, GH], BF16)
        top_rows = sb("top_rows", [3 * GH, 2, T], BF16)
        ps = ctx.enter_context(nc.psum_tensor("at_ps", [P, 8, 512], F32))
        SMAX, SPROB, OUT, SH = 0, 2, 5, 6
        PROJ_BANKS = (SPROB + 2, SPROB, SPROB + 1, SPROB + 2)

        starts = [GH * sum(T - P * m for m in range(i)) for i in range(NT)]
        prob = [probs[:, starts[i]:starts[i] + GH * (T - P * i)].rearrange("p (h q) -> p h q", h=GH) for i in range(NT)]
        rope_b = res[:, :, :].rearrange("p i c -> p (i c)")
        raw_wp = probs[:, 0:NK * C].rearrange("p (k c) -> p k c", k=NK)
        raw_aw = rest[:, 0, 0:NK * 8 * NA].rearrange("p (k a) -> p k a", k=NK)
        ak_full = a_prob
        ak_rest = y[:, 0, 0:NK * 8 * NA]
        av_mask = y[0:8 * NA, 1, 0:P]

        s_const, s_masks = sem("const_loaded"), sem("masks")
        s_raw_aw, s_raw_wp = sem("raw_aw_loaded"), sem("raw_wp_loaded")
        s_wp_hi, s_wp_lo, s_aw_hi, s_aw_lo = map(sem, ("wp_hi", "wp_lo", "aw_hi", "aw_lo"))
        s_ak_mm, s_av_mm, s_ak, s_cast, s_zeroed = map(sem, ("ak_mm", "av_mm", "ak_steps", "ident_cast", "out_zeroed"))
        s_x, s_ln, s_norm, s_xt, s_xhi = sh.s_x, sh.s_ln, sh.s_norm, sh.s_tr, sh.s_hi
        s_qk, s_v, s_vcopy = map(sem, ("qk_mm", "v_mm", "v_copied"))
        s_rope, s_turned = sem("rope_terms"), sem("rope_summed")
        s_tr, s_hi, s_mid, s_parts = map(sem, ("qk_transposed", "part_hi", "part_mid", "parts_ready"))
        s_stack = [sem(f"stacked{i}") for i in range(SLOTS)]
        s_smm, s_max = sem("scores_for_max"), sem("unit_max")
        s_top, s_topT = map(sem, ("top_steps", "top_transposed"))
        s_toprow_in = [sem(f"top_row_in{i}") for i in range(2)]
        s_pmm, s_exp, s_causal, s_pv, s_out, s_ocopy = map(
            sem, ("scores_for_exp", "exp_done", "causal", "pv_tile", "pv_group", "out_copied"))
        s_oT, s_rsum, s_opart, s_y = map(sem, ("out_transposed", "row_sum", "out_part", "y_added"))
        s_amm, s_amax, s_aexp, s_asum, s_ascale, s_anorm = map(
            sem, ("a_scores", "a_max_done", "a_exp", "a_sum_done", "a_scale", "a_norm"))
        s_aT, s_aout = map(sem, ("a_transposed", "a_out"))
        s_yt, s_yhi = map(sem, ("y_transposed", "y_hi"))
        s_proj, s_res = sem("proj"), sem("res_done")
        s_res_in, s_store = [sem(f"res_loaded{i}") for i in range(2)], sh.s_store
        s_staged = sem("next_weights_staged")
        STORED = base * (NT // 2) * 16
        s_pool_passed, s_sp_passed = sem("pool_passed"), sem("sp_passed")
        s_free = [sem(f"shared_bank_free{i}") for i in range(2)]

        src = x_src.rearrange("(b t p) c -> p b t c", p=P, t=NT)
        dst = x_dst.rearrange("(b t p) c -> p b t c", p=P, t=NT)
        gT, uT = (x.rearrange("(k p) i -> p k i", p=P) for x in ffn_weights[:2])
        wdT = ffn_weights[2]
        setup, middle, end = step_lists()
        order = {id(x): [s for s in x if s[1] in SHARED] for x in (setup, middle, end)}
        assert all(len(order[id(x)]) % 2 == 0 for x in (setup, middle))
        BEFORE, PER_BANK = len(order[id(setup)]) // 2, len(order[id(middle)]) // 2

        def uses_before(b, steps, step):
            start = 0 if steps is setup else BEFORE + b * PER_BANK
            return start + order[id(steps)].index(step) // 2

        def shared(steps, step):
            return ps[:, SH + order[id(steps)].index(step) % 2, :]

        def free(steps, step):
            return s_free[order[id(steps)].index(step) % 2]

        def read(b, steps, step):
            return free(steps, step), uses_before(b, steps, step) + 1

        def read_in_last(b, step):
            later = len(order[id(middle)]) - 1 - order[id(middle)].index((1, *step[1:]))
            assert order[id(setup)][-later - 1] == step
            return s_free[(later + 1) % 2], BEFORE + b * PER_BANK - later // 2

        def over_batches(eng, body):
            body(0, setup)
            body(0, middle)
            with eng.Fori(1, NB - 1) as b:
                body(b, middle)
            body(NB - 1, end)

        def at(b):
            return bass.ds(b, 1)

        def key_unit(u):
            i, h, n = KEY_UNITS[u]
            return i, h, n, T - P * i, SPROB + u % 3

        def yT(steps):
            return last_yT if steps is end else xT

        block = ctx.enter_context(nc.Block())

        @block.sync
        def _(sp):
            sp.dma_start(raw_aw, wte.rearrange("(k p) a -> p k a", p=P)).then_inc(s_raw_aw, 16)
            for tile, name in ((cos, "cos"), (sin, "sin")):
                sp.dma_start(tile[:, :, :], consts[name].rearrange("(t p) c -> p t c", p=P)).then_inc(s_const, 16)
            sp.dma_start(ak_mask[:, :], consts["ak_mask"]).then_inc(s_const, 16)
            sp.dma_start(av_mask, consts["av_mask"]).then_inc(s_const, 16)
            sp.dma_start(raw_wp, wpT.rearrange("(k p) c -> p k c", p=P)).then_inc(s_raw_wp, 16)
            sp.dma_start(gate[:, :], gating.partition_broadcast(P)).then_inc(s_const, 16)

            def body(b0, steps):
                for step in steps:
                    ahead, kind, *a = step
                    b = b0 + ahead
                    if kind == "load":
                        sp.wait_ge(s_xt, (base + b) * NK)
                        if steps is end:
                            sp.dma_start(xa[:, :, :], dst[:, 0, :, :]).then_inc(s_x, 16)
                        else:
                            for i in range(2):
                                sp.wait_ge(s_store[i], STORED)
                            sp.dma_start(xa[:, :, :], src[:, at(b), :, :]).then_inc(s_x, 16)
                    if kind == "stack":
                        g, = a
                        c, half, slot = g // 2, g % 2, g % SLOTS
                        done = b * (G * NU) + (g - SLOTS + 1) * NU
                        sp.wait_ge(s_parts, 2 * (b * NK + c + 1))
                        sp.sem_inc(s_sp_passed, 1)
                        wait(sp, s_pmm, done)
                        own = slice(half * 64, half * 64 + 64)
                        for r in range(NS):
                            to = slice(r * HD, (r + 1) * HD)
                            sp.dma_start(q_stack[to, slot, :, :], parts[own, 0, PART_Q[r], :]).then_inc(s_stack[slot], 16)
                            sp.dma_start(k_stack[to, slot, :, :], parts[own, 1, PART_K[r], :]).then_inc(s_stack[slot], 16)
                    if kind == "yt" and a[0] == 0:
                        sp.wait_ge(s_turned, NB * NT if steps is end else (b + 2) * NT)
                        for i in range(2):
                            wait(sp, s_store[i], STORED + b * (NT // 2) * 16)
                        for i in range(2):
                            sp.dma_start(res[:, i, :], src[:, at(b), i, :]).then_inc(s_res_in[i], 16)
                    if kind == "out":
                        t, = a
                        i, used = t % 2, b * (NT // 2) + t // 2 + 1
                        if steps is end and t == 0:
                            sp.wait_ge(s_yt, NB * NK)
                            sp.wait_ge(s_y, NB * G)
                            for j in range(2):
                                load_raw_gate_up(sp, sh.raw_gate_up(), gT, uT, j, [s_staged] * 2)
                                load_raw_down(sp, sh.raw_down(), wdT, j, [s_staged] * 2)
                        sp.wait_ge(s_res, b * NT + t + 1)
                        sp.dma_start(dst[:, at(b), t, :], res[:, i, :]).then_inc(s_store[i], 16)
                        if t + 2 < NT:
                            sp.wait_ge(s_store[i], STORED + used * 16)
                            sp.dma_start(res[:, i, :], src[:, at(b), t + 2, :]).then_inc(s_res_in[i], 16)

            over_batches(sp, body)
            sp.wait_ge(s_staged, 2 * 3 * 16)

        @block.tensor
        def _(pe):
            def three(out, lhsT, rhs, start, stop):
                pe.matmul(out, lhsT(HI), rhs(HI), start=start, stop=False)
                pe.matmul(out, lhsT(HI), rhs(LO), start=False, stop=False)
                return pe.matmul(out, lhsT(LO), rhs(HI), start=False, stop=stop)

            def body(b0, steps):
                def take(step):
                    wait(pe, free(steps, step), uses_before(b0, steps, step))
                    return shared(steps, step)

                for step in steps:
                    ahead, kind, *a = step
                    b = b0 + ahead
                    if kind == "xt":
                        k, = a
                        out = take(step)
                        pe.wait_ge(s_norm, (base + b + 1) * NT)
                        for t in range(NT):
                            mm = pe.transpose(out[:, t * P:(t + 1) * P], xa[:, t, k * P:(k + 1) * P], ident[:, :])
                        mm.then_inc(s_xt, 1)
                    if kind == "ak":
                        out = take(step)
                        pe.wait_ge(s_aw_lo, 1)
                        for c in range(NK):
                            for k in range(NK):
                                mm = three(out[:, c * NA:(c + 1) * NA], lambda part: w[:, part, k, C + c * P:C + (c + 1) * P],
                                           lambda part: aw[:, part, k, 0:NA], k == 0, k == NK - 1)
                        mm.then_inc(s_ak_mm, 1)
                    if kind == "av":
                        out = take(step)
                        for k in range(NK):
                            mm = three(out[0:8 * NA, :], lambda part: aw[:, part, k, :],
                                       lambda part: w[:, part, k, 2 * C:3 * C], k == 0, k == NK - 1)
                        mm.then_inc(s_av_mm, 1)
                    if kind == "qk":
                        t, = a
                        if t == 0:
                            if steps is not setup:
                                for k in (NK - 2, NK - 1):
                                    pe.wait_ge(*read(b0, steps, (ahead, "xt", k)))
                            wait(pe, s_max, b * G * NU)
                        else:
                            pe.wait_ge(s_rope, (b * NT + t) * 3)
                        for part in range(2):
                            for k in range(NK):
                                mm = three(ps[:, SMAX + part, :], lambda x: xT[:, x, k, t * P:(t + 1) * P],
                                           lambda x: w[:, x, k, part * C:(part + 1) * C], k == 0, k == NK - 1)
                        mm.then_inc(s_qk, 1)
                    if kind == "v":
                        t, = a
                        if t == 0:
                            wait(pe, s_exp, b * G * NU)
                        if t >= 2:
                            pe.wait_ge(s_vcopy, b * NT + t - 1)
                        for k in range(NK):
                            mm = three(ps[:, SPROB + t % 2, :], lambda x: xT[:, x, k, t * P:(t + 1) * P],
                                       lambda x: w[:, x, k, 2 * C:3 * C], k == 0, k == NK - 1)
                        mm.then_inc(s_v, 1)
                    if kind == "tr":
                        c, which = a
                        out = take(step)
                        pe.wait_ge(s_turned, (b + 1) * NT)
                        for t in range(NT):
                            at_ = which * C + c * P
                            mm = pe.transpose(out[:, t * P:(t + 1) * P], qk[:, t, at_:at_ + P], ident[:, :])
                        mm.then_inc(s_tr, 1)
                    if kind == "ascore":
                        c, = a
                        out = take(step)
                        if steps is setup:
                            pe.wait_ge(s_ak, 4)
                        pe.wait_ge(s_parts, 2 * (b * NK + c + 1))
                        for t in range(NT):
                            for r in range(NS):
                                mm = pe.matmul(out[:, t * 8 * NA:(t + 1) * 8 * NA], parts[:, 0, PART_Q[r], t * P:(t + 1) * P],
                                               ak[:, PART_K[r], c, :], start=(r == 0), stop=(r == NS - 1))
                        mm.then_inc(s_amm, 1)
                    if kind == "amix":
                        c, = a
                        out = take(step)
                        pe.wait_ge(s_anorm, b * NK + c + 1)
                        for t in range(NT):
                            mm = pe.transpose(out[0:8 * NA, t * P:(t + 1) * P],
                                              a_prob[:, 8 * t:8 * t + 8, :].rearrange("p h a -> p (h a)"), ident[:, :])
                        mm.then_inc(s_aT, 1)
                    if kind == "aout":
                        c, = a
                        out = take(step)
                        if c == 0:
                            pe.wait_ge(*read_in_last(b, (0, "amix", 0)))
                        else:
                            pe.wait_ge(*read(b0, steps, (ahead, "amix", c)))
                        for t in range(NT):
                            mm = pe.matmul(out[:, t * P:(t + 1) * P], a_T[:, t * P:(t + 1) * P], av[:, c * P:(c + 1) * P],
                                           start=True, stop=True)
                        mm.then_inc(s_aout, 1)
                    if kind == "max":
                        g, u = a
                        t, h0, nh = UNITS[u]
                        n, slot = b * G + g, g % SLOTS
                        bank = SMAX + (g * NU + u) % 2
                        if steps is setup and g == 0 and u == 0:
                            pe.wait_ge(s_masks, 4)
                            pe.wait_ge(s_cast, 1)
                        if g == 0 and u == 0:
                            pe.wait_ge(s_rope, (b + 1) * NT * 3)
                        wait(pe, s_max, n * NU + u - 1)
                        if u == 0:
                            pe.wait_ge(s_stack[slot], (b * (G // SLOTS) + g // SLOTS + 1) * 2 * NS * 16)
                        m = P * (t + 1)
                        for h in range(h0, h0 + nh):
                            out = ps[:, bank, (h - h0) * m:(h - h0 + 1) * m]
                            pe.matmul(out, q_stack[0:KROWS, slot, h, t * P:(t + 1) * P], k_stack[0:KROWS, slot, h, 0:m],
                                      start=True, stop=False)
                            mm = pe.matmul(out[:, t * P:m], ident_b[:, :], neg_mask[:, :], start=False, stop=True)
                        mm.then_inc(s_smm, 1)
                    if kind == "mrow":
                        g, = a
                        out = take(step)
                        pe.wait_ge(s_top, (b * G + g + 1) * 4)
                        rows_ps = out[0:3 * GH, 0:T // 2].bitcast(BF16)
                        for t in range(NT):
                            mm = pe.transpose(rows_ps[:, t * P:(t + 1) * P],
                                              top_parts[:, t, :, :].rearrange("p s h -> p (s h)"), ident_b[:, :])
                        mm.then_inc(s_topT, 1)
                    if kind == "prob":
                        g, u = a
                        i, h0, nh, m, bank = key_unit(u)
                        n, slot = b * G + g, g % SLOTS
                        if g == 0 and u == 0:
                            pe.wait_ge(s_vcopy, (b + 1) * NT)
                            wait(pe, s_res, b * NT)
                        wait(pe, s_exp, n * NU + (u - 2 if u >= 3 else (-1, 0, -2)[u]))
                        if u == 0:
                            pe.wait_ge(s_toprow_in[g % 2], (b * (G // 2) + g // 2 + 1) * 16)
                        for h in range(h0, h0 + nh):
                            mm = pe.matmul(ps[:, bank, (h - h0) * m:(h - h0 + 1) * m],
                                           k_stack[:, slot, h, i * P:(i + 1) * P], q_stack[:, slot, h, i * P:T],
                                           start=True, stop=True)
                        mm.then_inc(s_pmm, 1)
                    if kind == "pv":
                        g, i = a
                        n = b * G + g
                        pe.wait_ge(s_causal, n * NT + i + 1)
                        if i == 0:
                            wait(pe, s_ocopy, n)
                            if isinstance(b, int) and b == 0 and g == 0:
                                pe.wait_ge(s_zeroed, 1)
                        for h in range(GH):
                            mm = pe.matmul(ps[32 * h:32 * h + HD + 1, OUT, i * P:T], v[:, i, g * GH + h, :], prob[i][:, h, :],
                                           start=(i == 0), stop=(i == NT - 1))
                        mm.then_inc(s_pv, 1)
                    if kind == "oT":
                        g, = a
                        out = take(step)
                        pe.wait_ge(s_ocopy, b * G + g + 1)
                        for t in range(NT):
                            mm = pe.transpose(out[:, t * P:(t + 1) * P], o_cols[:, t * P:(t + 1) * P], ident[:, :])
                        mm.then_inc(s_oT, 1)
                    if kind == "yt":
                        k, = a
                        out = take(step)
                        pe.wait_ge(s_y, b * G + 2 * k + 2)
                        for t in range(NT):
                            mm = pe.transpose(out[:, t * P:(t + 1) * P], y[:, t, k * P:(k + 1) * P], ident[:, :])
                        mm.then_inc(s_yt, 1)
                    if kind == "proj":
                        t, = a
                        if isinstance(b, int) and b == 0 and t == 0:
                            pe.wait_ge(s_wp_lo, 1)
                        if t == 0:
                            for k in (NK - 2, NK - 1):
                                pe.wait_ge(*read(b0, steps, (0, "yt", k)))
                            if steps is end:
                                pe.wait_ge(s_exp, NB * G * NU)
                        if t == 1 and steps is not end:
                            pe.wait_ge(s_vcopy, (b + 2) * NT)
                        if t == NT - 1:
                            pe.wait_ge(s_res, b * NT + 1)
                        for k in range(NK):
                            mm = three(ps[:, PROJ_BANKS[t], :], lambda x: yT(steps)[:, x, k, t * P:(t + 1) * P],
                                       lambda x: wp[:, x, k, :], k == 0, k == NK - 1)
                        mm.then_inc(s_proj, 1)

            over_batches(pe, body)

        @block.scalar
        def _(act):
            act.wait_ge(s_raw_aw, 16)
            act.activation(aw[:, HI, :, :], raw_aw, ACT.Copy).then_inc(s_aw_hi, 1)

            def body(b0, steps):
                for step in steps:
                    ahead, kind, *a = step
                    b = b0 + ahead
                    if kind == "xt":
                        k, = a
                        act.wait_ge(s_xt, (base + b) * NK + k + 1)
                        act.activation(xT[:, HI, k, :], shared(steps, step), ACT.Copy).then_inc(s_xhi, 1)
                    if kind == "ak":
                        act.wait_ge(s_raw_wp, 16)
                        act.activation(wp[:, HI, :, :], raw_wp, ACT.Copy).then_inc(s_wp_hi, 1)
                    if kind == "v":
                        t, = a
                        act.wait_ge(s_v, b * NT + t + 1)
                        act.activation(v[:, t, :, 0:HD], ps[:, SPROB + t % 2, :].rearrange("p (h d) -> p h d", h=H), ACT.Copy).then_inc(s_vcopy, 1)
                    if kind == "tr":
                        c, which = a
                        n = 2 * (b * NK + c) + which
                        act.wait_ge(s_tr, n + 1)
                        if which == 0:
                            last_b, last = (b, 2 * c) if c else (b - 1, G)
                            for g in (last - 2, last - 1):
                                wait(act, s_stack[g % SLOTS], (last_b * (G // SLOTS) + g // SLOTS + 1) * 2 * NS * 16)
                            wait(act, s_amm, b * NK + c)
                        act.activation(parts[:, which, 0, :], shared(steps, step), ACT.Copy).then_inc(s_hi, 1)
                    if kind == "mid":
                        c, which = a
                        act.wait_ge(*read(b0, steps, (ahead, "tr", c, which)))
                        act.activation(parts[:, which, 1, :], rest[:, which, :], ACT.Copy).then_inc(s_mid, 1)
                    if kind == "amix":
                        c, = a
                        act.wait_ge(s_aT, b * NK + c + 1)
                        act.activation(a_T[:, :], shared(steps, step)[0:8 * NA, :], ACT.Copy).then_inc(free(steps, step), 1)
                    if kind == "ascore":
                        c, = a
                        act.wait_ge(*read(b0, steps, step))
                        act.activation(a_prob[:, :, :], a_prob[:, :, :], ACT.Exp, scale=float(1.0 / np.sqrt(np.float32(C)))).then_inc(s_aexp, 1)
                    if kind == "aout":
                        c, = a
                        act.wait_ge(s_aout, b * NK + c + 1)
                        act.activation(y[:, :, c * P:(c + 1) * P], shared(steps, step).rearrange("p (t c) -> p t c", t=NT), ACT.Copy).then_inc(free(steps, step), 1)
                    if kind == "mrow":
                        g, = a
                        n = b * G + g
                        act.wait_ge(s_topT, n + 1)
                        wait(act, s_toprow_in[g % 2], (b * (G // 2) + g // 2) * 16)
                        act.activation(top_rows[:, g % 2, :], shared(steps, step)[0:3 * GH, 0:T // 2].bitcast(BF16), ACT.Copy).then_inc(free(steps, step), 1)
                        act.wait_ge(*read(b0, steps, step))
                        act.dma_start(q_stack[KROWS:KROWS + 3, g % SLOTS, :, :], top_rows[:, g % 2, :]).then_inc(s_toprow_in[g % 2], 16)
                    if kind == "prob":
                        g, u = a
                        i, h0, nh, m, bank = key_unit(u)
                        n = b * G + g
                        if isinstance(b, int) and b == 0 and g == 0 and u == 0:
                            act.wait_ge(s_wp_lo, 1)
                        act.wait_ge(s_pmm, n * NU + u + 1)
                        wait(act, s_pv, (n - 1) * NT + i + 1)
                        act.activation(prob[i][:, h0:h0 + nh, :], ps[:, bank, 0:nh * m].rearrange("p (h q) -> p h q", h=nh),
                                       ACT.Exp, scale=HD ** -0.5).then_inc(s_exp, 1)
                    if kind == "pv" and a[1] == NT - 1:
                        g = a[0]
                        n = b * G + g
                        act.wait_ge(s_pv, (n + 1) * NT)
                        wait(act, s_oT, n)
                        act.activation(o_cols[:, :], ps[:, OUT, :], ACT.Copy).then_inc(s_ocopy, 1)
                    if kind == "yt":
                        k, = a
                        act.wait_ge(s_yt, b * NK + k + 1)
                        act.activation(yT(steps)[:, HI, k, :], shared(steps, step), ACT.Copy).then_inc(s_yhi, 1)

            over_batches(act, body)

        @block.gpsimd
        def _(pool):
            pool.memset(v[:, :, :, HD:HD + 1], 1.0).then_inc(s_masks, 1)
            pool.wait_ge(s_masks, 1)
            pool.memset(k_stack[KROWS:KROWS + 3, :, :, :], 1.0).then_inc(s_masks, 1)
            pool.wait_ge(s_masks, 2)
            pool.memset(neg_mask[:, :], 0.0).then_inc(s_masks, 1)
            pool.wait_ge(s_masks, 3)
            pool.affine_select(neg_mask[:, :], neg_mask[:, :], pattern=[[-1, P]], compare_op=ALU.is_ge,
                               fill=-3e38, base=0, channel_multiplier=1).then_inc(s_masks, 1)
            pool.wait_ge(s_aw_hi, 1)
            pool.tensor_tensor(aw[:, LO, :, :], raw_aw, aw[:, HI, :, :].bitcast(F32), ALU.subtract).then_inc(s_aw_lo, 1)
            pool.wait_ge(s_wp_hi, 1)
            pool.tensor_tensor(wp[:, LO, :, :], raw_wp, wp[:, HI, :, :].bitcast(F32), ALU.subtract).then_inc(s_wp_lo, 1)

            def body(b0, steps):
                for step in steps:
                    ahead, kind, *a = step
                    b = b0 + ahead
                    if kind == "rope":
                        t, = a
                        pool.wait_ge(s_rope, (b * NT + t + 1) * 3)
                        pool.tensor_tensor(qk[:, t, :], qk[:, t, :], rope_b, ALU.add).then_inc(s_turned, 1)
                    if kind == "prob":
                        g, u = a
                        i = KEY_UNITS[u][0]
                        if u == NU - 1 or KEY_UNITS[u + 1][0] != i:
                            n = b * G + g
                            pool.wait_ge(s_exp, n * NU + u + 1)
                            pool.sem_inc(s_pool_passed, 1)
                            own = prob[i][:, :, 0:P]
                            pool.affine_select(own, own, pattern=[[0, GH], [1, P]], compare_op=ALU.is_ge, fill=0.0,
                                               base=0, channel_multiplier=-1).then_inc(s_causal, 1)

            over_batches(pool, body)

        @block.vector
        def _(dve):
            dve.memset(ps[:, OUT, :], 0.0).then_inc(s_zeroed, 1)

            def wide(x):
                return x[:, :].rearrange("p (h o) -> p h o", o=1).broadcast_to([P, NT * 8, NA])

            def adapter_keys(out):
                dve.wait_ge(s_ak_mm, 1)
                for c in range(NK):
                    ins = dve.tensor_tensor(
                        ak_full[:, 8 * c:8 * c + 8, :],
                        out[:, c * NA:(c + 1) * NA].rearrange("p (o a) -> p o a", o=1).broadcast_to([P, 8, NA]),
                        ak_mask[:, :].rearrange("p (h o) -> p h o", o=1).broadcast_to([P, 8, NA]), ALU.mult)
                return ins

            def cut_adapter_keys():
                flat = ak_full[:, :, :].rearrange("p h a -> p (h a)")

                def ak_part(i):
                    return ak[:, i, :, :].rearrange("p c a -> p (c a)")

                dve.tensor_copy(ak_part(0), flat).then_inc(s_ak, 1)
                dve.wait_ge(s_ak, 1)
                dve.tensor_tensor(ak_rest, flat, ak_part(0), ALU.subtract).then_inc(s_ak, 1)
                dve.wait_ge(s_ak, 2)
                dve.tensor_copy(ak_part(1), ak_rest).then_inc(s_ak, 1)
                dve.wait_ge(s_ak, 3)
                dve.tensor_tensor(ak_part(2), ak_rest, ak_part(1), ALU.subtract).then_inc(s_ak, 1)

            def body(b0, steps):
                for step in steps:
                    ahead, kind, *a = step
                    b = b0 + ahead
                    if kind == "stats":
                        if a[0] == 0:
                            dve.wait_ge(s_x, (base + b) * 16)
                        row_statistics(dve, xa, ln, a[0]).then_inc(s_ln, 1)
                    if kind == "rstd":
                        inverse_deviation(dve, ln, s_ln, (base + b) * (NT + LN_STEPS) + NT)
                    if kind == "normal":
                        dve.wait_ge(s_ln, (base + b + 1) * (NT + LN_STEPS))
                        normalise_tile(dve, xa, ln, a[0]).then_inc(s_norm, 1)
                    if kind == "ak":
                        dve.wait_ge(s_const, 5 * 16)
                        adapter_keys(shared(steps, step)).then_inc(free(steps, step), 1)
                        dve.wait_ge(*read(b0, steps, step))
                        cut_adapter_keys()
                    if kind == "av":
                        dve.tensor_copy(ident_b[:, :], ident[:, :]).then_inc(s_cast, 1)
                        dve.wait_ge(s_av_mm, 1)
                        dve.tensor_tensor(av[:, :].rearrange("p (c d) -> p c d", c=NK), shared(steps, step)[0:8 * NA, :].rearrange("p (c d) -> p c d", c=NK),
                                          av_mask.rearrange("p (o d) -> p o d", o=1).broadcast_to([8 * NA, NK, P]),
                                          ALU.mult).then_inc(free(steps, step), 1)
                    if kind == "xt":
                        k, = a
                        dve.wait_ge(s_xhi, (base + b) * NK + k + 1)
                        dve.tensor_tensor(xT[:, LO, k, :], shared(steps, step), xT[:, HI, k, :].bitcast(F32),
                                          ALU.subtract).then_inc(free(steps, step), 1)
                    if kind == "rope":
                        t, = a
                        n = b * NT + t
                        dve.wait_ge(s_qk, n + 1)
                        if t == 0:
                            for i in range(2):
                                dve.wait_ge(s_store[i], STORED + (0 if steps is setup else (b - 1) * (NT // 2) * 16))
                        if steps is setup:
                            dve.wait_ge(s_const, 5 * 16)
                        wait(dve, s_turned, n)
                        both = ps[:, SMAX:SMAX + 2, :].rearrange("p w (g c) -> p (w g) c", c=64)
                        ra, rb = (x.rearrange("p (g c) -> p g c", c=64) for x in (qk[:, t, :], rope_b))

                        def table(x, lo, hi):
                            return x[:, t, lo:hi].rearrange("p (o c) -> p o c", o=1).broadcast_to([P, 2 * G, hi - lo])

                        dve.tensor_tensor(ra, both, table(cos, 0, 64), ALU.mult).then_inc(s_rope, 1)
                        dve.tensor_tensor(rb[:, :, 0:32], both[:, :, 32:64], table(sin, 0, 32), ALU.mult).then_inc(s_rope, 1)
                        dve.tensor_tensor(rb[:, :, 32:64], both[:, :, 0:32], table(sin, 32, 64), ALU.mult).then_inc(s_rope, 1)
                    if kind == "rest":
                        c, which = a
                        n = 2 * (b * NK + c) + which
                        tr = (ahead, "tr", c, which)
                        dve.wait_ge(s_hi, n + 1)
                        dve.tensor_tensor(rest[:, which, :], shared(steps, tr), parts[:, which, 0, :], ALU.subtract).then_inc(free(steps, tr), 1)
                    if kind == "low":
                        c, which = a
                        n = 2 * (b * NK + c) + which
                        dve.wait_ge(s_mid, n + 1)
                        dve.tensor_tensor(parts[:, which, 2, :], rest[:, which, :], parts[:, which, 1, :], ALU.subtract).then_inc(s_parts, 1)
                    if kind == "max":
                        g, u = a
                        t, h0, nh = UNITS[u]
                        n, m = b * G + g, P * (t + 1)
                        bank = SMAX + (g * NU + u) % 2
                        dve.wait_ge(s_smm, n * NU + u + 1)
                        dve.tensor_reduce(top[:, t, h0:h0 + nh], ps[:, bank, 0:nh * m].rearrange("p (h k) -> p h k", h=nh),
                                          AX, ALU.max).then_inc(s_max, 1)
                    if kind == "neg":
                        g, = a
                        n = b * G + g
                        dve.wait_ge(s_max, (n + 1) * NU)
                        wait(dve, s_topT, n)
                        hi, mid, lo = (top_parts[:, :, i, :] for i in range(3))
                        dve.tensor_scalar(hi, top[:, :, :], -1.0, None, ALU.mult).then_inc(s_top, 1)
                        dve.wait_ge(s_top, 4 * n + 1)
                        dve.scalar_tensor_tensor(out=top_rest[:, :, :], in0=top[:, :, :], scalar=-1.0, in1=hi,
                                                 op0=ALU.mult, op1=ALU.subtract).then_inc(s_top, 1)
                        dve.wait_ge(s_top, 4 * n + 2)
                        dve.tensor_copy(mid, top_rest[:, :, :]).then_inc(s_top, 1)
                        dve.wait_ge(s_top, 4 * n + 3)
                        dve.tensor_tensor(lo, top_rest[:, :, :], mid, ALU.subtract).then_inc(s_top, 1)
                    if kind == "ascore":
                        c, = a
                        n = b * NK + c
                        s = shared(steps, step)[:, 0:NT * 8 * NA].rearrange("p (h a) -> p h a", a=NA)

                        dve.wait_ge(s_amm, n + 1)
                        wait(dve, s_aT, n)
                        dve.tensor_reduce(a_max[:, :], s, AX, ALU.max).then_inc(s_amax, 1)
                        dve.wait_ge(s_amax, n + 1)
                        dve.tensor_tensor(a_prob[:, :, :], s, wide(a_max), ALU.subtract).then_inc(free(steps, step), 1)
                    if kind == "anorm":
                        n = b * NK + a[0]
                        dve.wait_ge(s_aexp, n + 1)
                        dve.tensor_reduce(a_sum[:, :], a_prob[:, :, :], AX, ALU.add).then_inc(s_asum, 1)
                        dve.wait_ge(s_asum, n + 1)
                        dve.reciprocal(a_sum[:, :], a_sum[:, :]).then_inc(s_ascale, 1)
                        dve.wait_ge(s_ascale, 2 * n + 1)
                        dve.tensor_scalar(a_sum[:, :], a_sum[:, :], gate[:, 0:1], None, ALU.mult).then_inc(s_ascale, 1)
                        dve.wait_ge(s_ascale, 2 * n + 2)
                        dve.tensor_tensor(a_prob[:, :, :], a_prob[:, :, :], wide(a_sum), ALU.mult).then_inc(s_anorm, 1)
                    if kind == "onorm":
                        g, = a
                        n = b * G + g
                        oT = (ahead, "oT", g)
                        s = shared(steps, oT).rearrange("p (t h c) -> p t h c", t=NT, h=GH)
                        dve.wait_ge(s_oT, n + 1)
                        dve.reciprocal(rsum[:, :, :], s[:, :, :, HD]).then_inc(s_rsum, 1)
                        dve.wait_ge(s_rsum, n + 1)
                        dve.tensor_tensor(o_part[:, :, :, :], s[:, :, :, 0:HD],
                                          rsum[:, :, :].rearrange("p t (h o) -> p t h o", o=1).broadcast_to([P, NT, GH, HD]),
                                          ALU.mult).then_inc(free(steps, oT), 1)
                        dve.wait_ge(*read(b0, steps, oT))
                        own = y[:, :, g * GH * HD:(g + 1) * GH * HD]
                        dve.wait_ge(*read(b0, steps, (ahead, "aout", g // 2)))
                        dve.tensor_tensor(own, own, o_part[:, :, :, :].rearrange("p t h d -> p t (h d)"), ALU.add).then_inc(s_y, 1)
                    if kind == "yt":
                        k, = a
                        dve.wait_ge(s_yhi, b * NK + k + 1)
                        dve.tensor_tensor(yT(steps)[:, LO, k, :], shared(steps, step), yT(steps)[:, HI, k, :].bitcast(F32),
                                          ALU.subtract).then_inc(free(steps, step), 1)
                    if kind == "proj":
                        t, = a
                        n = b * NT + t
                        dve.wait_ge(s_proj, n + 1)
                        dve.wait_ge(s_res_in[t % 2], (b * (NT // 2) + t // 2 + 1) * 16)
                        dve.tensor_tensor(res[:, t % 2, :], ps[:, PROJ_BANKS[t], :], res[:, t % 2, :], ALU.add).then_inc(s_res, 1)

            over_batches(dve, body)


def macaron(nc, x, w_qkvT, w_projT, wte, gating, w_gateT, w_upT, w_downT, cos, sin, ident, ak_mask, av_mask, out):
    h1 = nc.dram_tensor("h1", [NB * T, C], F32).ap()
    h2 = nc.dram_tensor("h2", [NB * T, C], F32).ap()
    consts = {"cos": cos, "sin": sin, "ak_mask": ak_mask, "av_mask": av_mask}
    ffn_weights = (w_gateT, w_upT, w_downT)
    with ExitStack() as ctx:
        sh = Shared(nc, ctx)
        ffn_phase(nc, sh, "f1", 0, x, h1, *ffn_weights, ident, wqkvT=w_qkvT)
        attention_phase(nc, sh, NB, h1, h2, w_projT, wte, gating, consts, ffn_weights)
        ffn_phase(nc, sh, "f2", 2 * NB, h2, out, *ffn_weights, ident)


def shape_constants():
    theta = np.float32(1.0) / np.power(np.float32(10000.0), np.arange(0, HD, 2, dtype=np.float32) / np.float32(HD))
    angle = np.outer(np.arange(T, dtype=np.float32), theta.astype(np.float32)).astype(np.float32)
    cos, sin = np.cos(angle), np.sin(angle)
    head_of_row = np.arange(P) // 64 * GH + np.arange(P) % GH
    head_of_pair = np.arange(8 * NA) // NA
    return {
        "cos": np.repeat(np.concatenate([cos, cos], 1), GH, axis=1),
        "sin": np.repeat(np.concatenate([-sin, sin], 1), GH, axis=1),
        "ident": np.eye(P, dtype=np.float32),
        "ak_mask": (head_of_row[:, None] == np.arange(8)).astype(np.float32),
        "av_mask": (head_of_pair[:, None] == np.arange(P) // HD).astype(np.float32),
    }


_NAMES = ["x", "w_qkvT", "w_projT", "wte", "gating", "w_gateT", "w_upT", "w_downT", "cos", "sin", "ident", "ak_mask", "av_mask"]


def lay_out(x, w_attn, w_proj, adapter_wte, gating, w_gate, w_up, w_down):
    qk = w_attn[:2 * C].reshape(2, G, GH, HD, C).transpose(0, 1, 3, 2, 4).reshape(2 * C, C)
    arrays = {
        "x": x.reshape(NB * T, C), "w_qkvT": np.concatenate([qk, w_attn[2 * C:]]).T, "w_projT": w_proj.T,
        "wte": np.tile(adapter_wte.T, (1, 8)), "gating": gating, "w_gateT": w_gate.T, "w_upT": w_up.T, "w_downT": w_down.T,
    }
    arrays.update(shape_constants())
    return {name: np.ascontiguousarray(arrays[name]) for name in _NAMES}


def kernel(L0_attn_x, L0_attn_w_attn, L0_attn_w_proj, L0_attn_adapter_wte, L0_attn_gating,
           L0_ffn_w_gate, L0_ffn_w_up, L0_ffn_w_down):
    import concourse.bacc as _bacc
    from concourse import mybir as _mybir
    from concourse.bass_utils import run_bass_kernel_spmd as _run

    arrays = lay_out(*(np.asarray(a) for a in (
        L0_attn_x, L0_attn_w_attn, L0_attn_w_proj, L0_attn_adapter_wte, L0_attn_gating,
        L0_ffn_w_gate, L0_ffn_w_up, L0_ffn_w_down)))
    nc = _bacc.Bacc("TRN2", target_bir_lowering=False, num_devices=1)
    args = [nc.dram_tensor(f"in_{n}", arrays[n].shape, _mybir.dt.from_np(arrays[n].dtype), kind="ExternalInput").ap()
            for n in _NAMES]
    out = nc.dram_tensor("out_y", [NB * T, C], _mybir.dt.float32, kind="ExternalOutput").ap()
    macaron(nc, *args, out)
    r = _run(nc, [{f"in_{n}": arrays[n] for n in _NAMES}], core_ids=[0])
    return r.results[0]["out_y"].reshape(NB, T, C)
```

```python
from contextlib import ExitStack

import numpy as np

import concourse.bass as bass
from concourse import mybir

F32 = mybir.dt.float32
F32R = mybir.dt.float32r
BF16 = mybir.dt.bfloat16
I32 = mybir.dt.int32
ALU = mybir.AluOpType
ACT = mybir.ActivationFunctionType
AX = mybir.AxisListType.X

P = 128
C = 512
T = 512
NB = 4
NT = T // P
NK = C // P
INTER = 1376
NJ = -(-INTER // P)
H, HD = 32, 16
G = 8
GH = H // G
NA = 10
EPS = 1e-5
ROUND = 1.5 * 2.0 ** 23
RSQRT_SEED = 1597463007.0
HI, LO = 0, 1


def wait(eng, sem, value):
    if not isinstance(value, int) or value > 0:
        eng.wait_ge(sem, value)


def over_blocks(eng, body, last=True):
    body(0, True, False)
    with eng.Fori(1, NB - 1 if last else NB) as b:
        body(b, False, False)
    if last:
        body(NB - 1, False, True)


def rows(j):
    return min(P, INTER - j * P)


def row_statistics(eng, x, st, t):
    return eng.bn_stats(st["stats"][:, t, :], x[:, t, :])


def inverse_deviation(eng, st, counter, before, pieces=range(4)):
    n = LN_GUESS + 3 * (pieces[0] - 1) if pieces[0] else 0

    def step(ins):
        nonlocal n
        ins.then_inc(counter, 1)
        n += 1

    def chained():
        eng.wait_ge(counter, before + n)

    stats, mean, var, rstd, a, d = (st[k] for k in ("stats", "mean", "var", "rstd", "a", "d"))
    if pieces[0] == 0:
        chained()
        step(eng.tensor_tensor(mean[:, :], stats[:, :, 1], stats[:, :, 4], ALU.add))
        step(eng.tensor_tensor(d[:, :], stats[:, :, 1], stats[:, :, 4], ALU.subtract))
        step(eng.tensor_tensor(var[:, :], stats[:, :, 2], stats[:, :, 5], ALU.add))
        chained()
        step(eng.tensor_scalar(mean[:, :], mean[:, :], 0.5, None, ALU.mult))
        step(eng.scalar_tensor_tensor(out=d[:, :], in0=d[:, :], scalar=0.25, in1=d[:, :], op0=ALU.mult, op1=ALU.mult))
        step(eng.tensor_scalar(var[:, :], var[:, :], 1.0 / C, EPS, ALU.mult, ALU.add))
        chained()
        step(eng.tensor_tensor(var[:, :], var[:, :], d[:, :], ALU.add))
        chained()
        step(eng.tensor_scalar(rstd[:, :].bitcast(I32), var[:, :].bitcast(I32), -0.5, RSQRT_SEED, ALU.mult, ALU.add))
    for _ in range(sum(i > 0 for i in pieces)):
        chained()
        step(eng.tensor_tensor(a[:, :], rstd[:, :], rstd[:, :], ALU.mult))
        chained()
        step(eng.scalar_tensor_tensor(out=a[:, :], in0=a[:, :], scalar=-0.5, in1=var[:, :], op0=ALU.mult, op1=ALU.mult))
        chained()
        step(eng.scalar_tensor_tensor(out=rstd[:, :], in0=a[:, :], scalar=1.5, in1=rstd[:, :], op0=ALU.add, op1=ALU.mult))
    assert n == LN_GUESS + 3 * pieces[-1]


LN_GUESS = 8
LN_STEPS = LN_GUESS + 3 * 3


def normalise_tile(eng, x, st, t):
    return eng.tensor_scalar(x[:, t, :], x[:, t, :], st["mean"][:, t:t + 1], st["rstd"][:, t:t + 1], ALU.subtract, ALU.mult)


class Shared:

    def __init__(self, nc, ctx):
        def sb(name, shape, dt=F32):
            return ctx.enter_context(nc.sbuf_tensor(f"all_{name}", shape, dt))

        def sem(name):
            return ctx.enter_context(nc.semaphore(f"all_{name}"))

        def over(*tensors):
            with ExitStack() as here:
                return [here.enter_context(nc.sbuf_tensor(f"all_{name}", shape, dt)) for name, shape, dt in tensors]

        self.w_gu, = over(("w_gu", [P, 2, 2, NK, INTER], F32R))
        w_qkv = ("w_qkv", [P, 2, NK, 3 * C], F32R)
        w_proj = ("w_proj", [P, 2, NK, C], F32R)
        with nc.sbuf_tensor("all_" + w_qkv[0], *w_qkv[1:]) as self.w_qkv:
            self.raw_late, = over(("raw_qkv_late", [P, 2, 3 * C], F32))
            with nc.sbuf_tensor("all_" + w_proj[0], *w_proj[1:]) as self.w_proj:
                self.qk, self.parts = over(("qk", [P, NT, 2 * C], F32), ("parts", [P, 2, 3, T], BF16))
                self.last_yT, = over(("last_yT", [P, 2, NK, T], F32R))
        sb("weights_space", [P, 4 * NK * INTER])
        self.staging = sb("staging", [P, 6 * C])
        self.xa = sb("xa", [P, NT, C])
        self.xT = sb("xT", [P, 2, NK, T], F32R)
        self.res = sb("res", [P, 2, C])
        self.ident = sb("ident", [P, P])
        self.ln = {k: sb(k, [P, NT]) for k in ("mean", "var", "rstd", "a", "d")}
        self.ln["stats"] = sb("stats", [P, NT, 6])
        self.s_x, self.s_ln, self.s_norm, self.s_tr, self.s_hi = map(
            sem, ("x_loaded", "ln_steps", "normalised", "x_transposed", "xT_hi"))
        self.s_store = [sem(f"stored{i}") for i in range(2)]
        self.s_w = [sem(f"qkv_w{k}_loaded") for k in range(NK)]
        self.s_w_hi, self.s_w_lo = sem("qkv_w_hi"), sem("qkv_w_lo")

    def raw_gate_up(self):
        return self.staging[:, 0:4 * C].rearrange("p (i w k m) -> p i w k m", i=2, w=2, k=NK)

    def raw_down(self):
        return self.staging[:, 4 * C:6 * C].rearrange("p (i c) -> p i c", i=2)

    def raw_qkv(self, k):
        if k < 2:
            return self.staging[:, 3 * C * k:3 * C * (k + 1)]
        return self.raw_late[:, k - 2, :]


def load_raw_gate_up(eng, raw_gu, gT, uT, j, counters):
    m = rows(j)
    for i, w in enumerate((gT, uT)):
        eng.dma_start(raw_gu[:, j % 2, i, :, 0:m], w[:, :, j * P:j * P + m]).then_inc(counters[j % 2], 16)


def load_raw_down(eng, raw_dn, wdT, j, counters):
    eng.dma_start(raw_dn[0:rows(j), j % 2, :], wdT[j * P:j * P + rows(j), :]).then_inc(counters[j % 2], 16)


def ffn_phase(nc, sh, tag, base, x_src, x_dst, wgT, wuT, wdT, ident_dram, wqkvT=None):
    leads = wqkvT is not None
    with ExitStack() as ctx:
        def sb(name, shape, dt=F32):
            return ctx.enter_context(nc.sbuf_tensor(f"{tag}_{name}", shape, dt))

        def sem(name):
            return ctx.enter_context(nc.semaphore(f"{tag}_{name}"))

        w_gu, raw_gu, raw_dn = sh.w_gu, sh.raw_gate_up(), sh.raw_down()
        xa, xT, res, ident, ln = sh.xa, sh.xT, sh.res, sh.ident, sh.ln
        w_dn = sb("w_dn", [P, 2, NJ, C], F32R)
        inter = sb("inter", [P, NJ, T], F32R)
        silu = sb("silu", [P, 2, T])
        clipped = sb("clipped", [P, T])
        rounded = sb("rounded", [P, T])
        over = sb("over", [P, T])
        under = sb("under", [P, T])
        ps = ctx.enter_context(nc.psum_tensor(f"{tag}_ps", [P, 8, 512], F32))
        GATE, UP, DOWN, TR = 0, 2, 4, 6

        s_ident, s_x, s_store = sem("ident"), sh.s_x, sh.s_store
        s_raw_gu, s_raw_dn, s_res_in = (
            [sem(f"{name}{i}") for i in range(2)] for name in ("raw_gu_loaded", "raw_dn_loaded", "res_loaded"))
        s_x_first = [sem(f"first_x_loaded{t}") for t in range(NT)]
        s_w_hi, s_gate_lo, s_up_lo, s_dn_hi, s_dn_lo = map(sem, ("w_hi", "gate_lo", "up_lo", "dn_hi", "dn_lo"))
        s_ln, s_norm, s_tr, s_hi, s_lo = sh.s_ln, sh.s_norm, sh.s_tr, sh.s_hi, sem("xT_lo")
        s_gate, s_up, s_silu, s_prod = map(sem, ("gate", "up", "silu_done", "product"))
        s_clip, s_round, s_over, s_under, s_floor, s_trunc = map(
            sem, ("clip", "round", "over_s", "under_s", "floor", "trunc"))
        s_down, s_down_read, s_res = map(sem, ("down", "down_read", "res_done"))

        src = x_src.rearrange("(b t p) c -> p b t c", p=P, t=NT)
        dst = x_dst.rearrange("(b t p) c -> p b t c", p=P, t=NT)
        gT = wgT.rearrange("(k p) i -> p k i", p=P)
        uT = wuT.rearrange("(k p) i -> p k i", p=P)
        TILES = NJ + NT
        FOUND = 0 if leads else 1
        STORED = base * (NT // 2) * 16

        def lo_done(b, k):
            return (b - FOUND) * NK + k + 1

        block = ctx.enter_context(nc.Block())

        def at(b):
            return bass.ds(b, 1)

        @block.sync
        def _(sp):
            def load_x(b):
                wait(sp, s_tr, (base + b) * NK)
                sp.dma_start(xa[:, :, :], src[:, at(b), :, :]).then_inc(s_x, 16)

            def load_raw(j):
                wait(sp, s_gate_lo, j - 1)
                wait(sp, s_up_lo, j - 1)
                load_raw_gate_up(sp, raw_gu, gT, uT, j, s_raw_gu)
                wait(sp, s_dn_lo, j - 1)
                load_raw_down(sp, raw_dn, wdT, j, s_raw_dn)

            def load_next_phase():
                sp.wait_ge(s_tr, NB * NK)
                for i in range(2):
                    sp.wait_ge(s_store[i], (NT // 2) * 16)
                sp.dma_start(xa[:, :, :], dst[:, 0, :, :]).then_inc(s_x, 16)
                for cut in (s_gate_lo, s_up_lo, s_dn_lo):
                    sp.wait_ge(cut, NJ)
                for k in range(2):
                    sp.dma_start(sh.raw_qkv(k), wqkvT[k * P:(k + 1) * P, :]).then_inc(sh.s_w[k], 16)

            def load_next_weights():
                sp.wait_ge(s_gate, NB * NJ)
                sp.wait_ge(s_up, NB * NJ)
                for k in range(2, NK):
                    sp.dma_start(sh.raw_qkv(k), wqkvT[k * P:(k + 1) * P, :]).then_inc(sh.s_w[k], 16)

            if leads:
                for t in range(0, NT, 2):
                    sp.dma_start(xa[:, t, :], src[:, 0, t, :]).then_inc(s_x_first[t], 16)
                load_raw(0)
                sp.dma_start(ident[:, :], ident_dram).then_inc(s_ident, 16)
                load_raw(1)

            def body(b, first, last):
                if first:
                    for j in range(2, NJ):
                        load_raw(j)
                        if j == 2:
                            load_x(1)
                elif not last:
                    load_x(b + 1)
                elif leads:
                    load_next_phase()
                for t in range(2):
                    wait(sp, s_store[t], STORED + b * (NT // 2) * 16)
                    sp.dma_start(res[:, t, :], src[:, at(b), t, :]).then_inc(s_res_in[t], 16)
                if last and leads:
                    load_next_weights()
                for t in range(NT):
                    i, used = t % 2, b * (NT // 2) + t // 2 + 1
                    sp.wait_ge(s_res, b * NT + t + 1)
                    sp.dma_start(dst[:, at(b), t, :], res[:, i, :]).then_inc(s_store[i], 16)
                    if t + 2 < NT:
                        sp.wait_ge(s_store[i], STORED + used * 16)
                        sp.dma_start(res[:, i, :], src[:, at(b), t + 2, :]).then_inc(s_res_in[i], 16)

            over_blocks(sp, body)
            if not leads:
                for i in range(2):
                    sp.wait_ge(s_store[i], STORED + NB * (NT // 2) * 16)

        @block.tensor
        def _(pe):
            def transpose_x(b, k):
                wait(pe, s_lo, lo_done(b, k - 2))
                pe.wait_ge(s_norm, (base + b + 1) * NT)
                for t in range(NT):
                    last = pe.transpose(ps[:, TR + k % 2, t * P:(t + 1) * P], xa[:, t, k * P:(k + 1) * P], ident[:, :])
                last.then_inc(s_tr, 1)

            def gate_up(b, j):
                n = b * NJ + j
                m = rows(j)
                for which, bank, free, done, cut in ((0, GATE, s_silu, s_gate, s_gate_lo), (1, UP, s_prod, s_up, s_up_lo)):
                    wait(pe, free, n - 1)
                    pe.wait_ge(cut, j + 1)
                    out = ps[0:m, bank + j % 2, :]
                    for k in range(NK):
                        cols = slice(j * P, j * P + m)
                        pe.matmul(out, w_gu[:, HI, which, k, cols], xT[:, HI, k, :], start=(k == 0), stop=False)
                        pe.matmul(out, w_gu[:, HI, which, k, cols], xT[:, LO, k, :], start=False, stop=False)
                        mm = pe.matmul(out, w_gu[:, LO, which, k, cols], xT[:, HI, k, :], start=False, stop=(k == NK - 1))
                    mm.then_inc(done, 1)

            def down(b, t, first):
                n = b * NT + t
                wait(pe, s_down_read, n - 1)
                out = ps[:, DOWN + t % 2, :]
                for j in range(NJ):
                    m = rows(j)
                    if t == 0 and j >= NJ - 3:
                        pe.wait_ge(s_trunc, b * TILES + j + 1)
                    if first and t == 0 and j >= NJ - 2:
                        pe.wait_ge(s_dn_lo, j + 1)
                    for part in (HI, LO):
                        mm = pe.matmul(out, inter[0:m, j, t * P:(t + 1) * P], w_dn[0:m, part, j, :],
                                       start=(j == 0 and part == HI), stop=(j == NJ - 1 and part == LO))
                mm.then_inc(s_down, 1)

            if leads:
                pe.wait_ge(s_ident, 16)
                for k in range(NK):
                    transpose_x(0, k)

            def body(b, first, last):
                wait(pe, s_lo, lo_done(b, NK - 1))
                for j in range(NJ):
                    gate_up(b, j)
                if first:
                    pe.wait_ge(s_dn_lo, NJ - 2)
                pe.wait_ge(s_trunc, b * TILES + NJ - 3)
                for t in range(NT):
                    if leads or not last:
                        transpose_x(b + 1, t)
                    down(b, t, first)

            over_blocks(pe, body)

        @block.scalar
        def _(act):
            def cut_hi(b, k):
                act.wait_ge(s_tr, (base + b) * NK + k + 1)
                act.activation(xT[:, HI, k, :], ps[:, TR + k % 2, :], ACT.Copy).then_inc(s_hi, 1)

            def cut_weights(j):
                m = rows(j)
                wait(act, s_raw_gu[j % 2], 32 * (j // 2 + 1 - FOUND))
                act.activation(w_gu[:, HI, :, :, j * P:j * P + m], raw_gu[:, j % 2, :, :, 0:m], ACT.Copy).then_inc(s_w_hi, 1)
                wait(act, s_raw_dn[j % 2], 16 * (j // 2 + 1 - FOUND))
                act.activation(w_dn[0:m, HI, j, :], raw_dn[0:m, j % 2, :], ACT.Copy).then_inc(s_dn_hi, 1)

            def scale(b, t):
                act.wait_ge(s_down, b * NT + t + 1)
                if t < 2:
                    act.wait_ge(s_prod, (b + 1) * NJ)
                else:
                    act.wait_ge(s_clip, b * TILES + NJ + t - 1)
                act.activation(silu[:, t % 2, :], ps[:, DOWN + t % 2, :], ACT.Copy, scale=128.0).then_inc(s_down_read, 1)

            if leads:
                for t in range(1, NT, 2):
                    act.dma_start(xa[:, t, :], src[:, 0, t, :]).then_inc(s_x_first[t], 16)
            cut_weights(0)
            if leads:
                for k in range(NK):
                    cut_hi(0, k)
            cut_weights(1)

            def body(b, first, last):
                for j in range(NJ):
                    n = b * NJ + j
                    m = rows(j)
                    act.wait_ge(s_gate, n + 1)
                    if j == 0 and not first:
                        act.wait_ge(s_clip, b * TILES)
                    wait(act, s_prod, n - 1)
                    act.activation(silu[0:m, j % 2, :], ps[0:m, GATE + j % 2, :], ACT.Silu, scale=1.0 / 128).then_inc(s_silu, 1)
                    if first and j + 2 < NJ:
                        cut_weights(j + 2)
                for k in range(NK):
                    if leads or not last:
                        cut_hi(b + 1, k)
                    if k:
                        scale(b, k - 1)
                    if leads and last:
                        if k == 0:
                            act.wait_ge(s_up, NB * NJ)
                        act.wait_ge(sh.s_w[k], 16)
                        act.activation(sh.w_qkv[:, HI, k, :], sh.raw_qkv(k), ACT.Copy).then_inc(sh.s_w_hi, 1)
                scale(b, NT - 1)

            over_blocks(act, body)

        @block.gpsimd
        def _(pool):
            def cut_weights(j):
                m = rows(j)
                pool.wait_ge(s_w_hi, j + 1)
                for i, done in enumerate((s_gate_lo, s_up_lo)):
                    pool.tensor_tensor(w_gu[:, LO, i, :, j * P:j * P + m], raw_gu[:, j % 2, i, :, 0:m],
                                       w_gu[:, HI, i, :, j * P:j * P + m].bitcast(F32), ALU.subtract).then_inc(done, 1)
                pool.wait_ge(s_dn_hi, j + 1)
                pool.tensor_tensor(w_dn[0:m, LO, j, :], raw_dn[0:m, j % 2, :], w_dn[0:m, HI, j, :].bitcast(F32),
                                   ALU.subtract).then_inc(s_dn_lo, 1)

            for j in range(NJ):
                cut_weights(j)
            if leads:
                for k in range(NK):
                    pool.wait_ge(sh.s_w_hi, k + 1)
                    pool.tensor_tensor(sh.w_qkv[:, LO, k, :], sh.raw_qkv(k), sh.w_qkv[:, HI, k, :].bitcast(F32),
                                       ALU.subtract).then_inc(sh.s_w_lo, 1)

        @block.vector
        def _(dve):
            def cut_lo(b, k):
                dve.wait_ge(s_hi, (base + b) * NK + k + 1)
                dve.tensor_tensor(xT[:, LO, k, :], ps[:, TR + k % 2, :], xT[:, HI, k, :].bitcast(F32),
                                  ALU.subtract).then_inc(s_lo, 1)

            def statistics(b, t):
                if isinstance(b, int) and b == 0:
                    dve.wait_ge(s_x_first[t], 16)
                else:
                    dve.wait_ge(s_x, (base + b) * 16)
                row_statistics(dve, xa, ln, t).then_inc(s_ln, 1)

            def normalise(b, t):
                if t == 0:
                    before = (base + b) * (NT + LN_STEPS) + NT
                    inverse_deviation(dve, ln, s_ln, before)
                    dve.wait_ge(s_ln, before + LN_STEPS)
                normalise_tile(dve, xa, ln, t).then_inc(s_norm, 1)

            def truncate(out, m, n):
                c, r = clipped[0:m, :], rounded[0:m, :]
                dve.wait_ge(s_clip, n + 1)
                dve.tensor_scalar(r, c, ROUND, -ROUND, ALU.add, ALU.add).then_inc(s_round, 1)
                dve.wait_ge(s_round, n + 1)
                dve.scalar_tensor_tensor(out=over[0:m, :], in0=c, scalar=0.0, in1=r,
                                         op0=ALU.max, op1=ALU.is_lt).then_inc(s_over, 1)
                dve.scalar_tensor_tensor(out=under[0:m, :], in0=c, scalar=0.0, in1=r,
                                         op0=ALU.min, op1=ALU.is_gt).then_inc(s_under, 1)
                dve.wait_ge(s_over, n + 1)
                dve.tensor_tensor(r, r, over[0:m, :], ALU.subtract).then_inc(s_floor, 1)
                dve.wait_ge(s_under, n + 1)
                dve.wait_ge(s_floor, n + 1)
                dve.tensor_tensor(out, r, under[0:m, :], ALU.add).then_inc(s_trunc, 1)

            def quantise_inner(b, j):
                n, m = b * TILES + j, rows(j)
                dve.wait_ge(s_silu, b * NJ + j + 1)
                dve.wait_ge(s_up, b * NJ + j + 1)
                dve.tensor_tensor(clipped[0:m, :], silu[0:m, j % 2, :], ps[0:m, UP + j % 2, :], ALU.mult).then_inc(s_prod, 1)
                dve.wait_ge(s_prod, b * NJ + j + 1)
                dve.tensor_scalar(clipped[0:m, :], clipped[0:m, :], -128.0, 127.0, ALU.max, ALU.min).then_inc(s_clip, 1)
                truncate(inter[0:m, j, :], m, n)

            def finish(b, t):
                n = b * TILES + NJ + t
                dve.wait_ge(s_down_read, b * NT + t + 1)
                dve.tensor_scalar(clipped[:, :], silu[:, t % 2, :], -128.0, 127.0, ALU.max, ALU.min).then_inc(s_clip, 1)
                truncate(over[:, :], P, n)
                dve.wait_ge(s_trunc, n + 1)
                dve.wait_ge(s_res_in[t % 2], (b * (NT // 2) + t // 2 + 1) * 16)
                dve.scalar_tensor_tensor(out=res[:, t % 2, :], in0=over[:, :], scalar=0.5, in1=res[:, t % 2, :],
                                         op0=ALU.mult, op1=ALU.add).then_inc(s_res, 1)

            if not leads:
                for i in range(2):
                    dve.wait_ge(s_store[i], STORED)
            if leads:
                for t in range(NT):
                    statistics(0, t)
                for t in range(NT):
                    normalise(0, t)
                for k in range(NK):
                    cut_lo(0, k)

            def body(b, first, last):
                for j in range(NJ):
                    quantise_inner(b, j)
                    start = 2 if first else 1
                    ahead = leads or not last
                    if ahead and start <= j < start + NT:
                        statistics(b + 1, j - start)
                    if ahead and start + NT <= j < start + 2 * NT:
                        normalise(b + 1, j - start - NT)
                for t in range(NT):
                    if leads or not last:
                        cut_lo(b + 1, t)
                    if t:
                        finish(b, t - 1)
                finish(b, NT - 1)

            over_blocks(dve, body)


UNITS = [(0, 0, 4), (1, 0, 2), (1, 2, 2)] + [(t, h, 1) for t in (2, 3) for h in range(GH)]
KEY_UNITS = [(NT - 1 - t, h, n) for t, h, n in sorted(UNITS, key=lambda u: (-u[0], u[1]))]
NU = len(UNITS)
PART_Q = (0, 0, 1, 0, 2, 1)
PART_K = (0, 1, 0, 2, 0, 1)
NS = len(PART_Q)
KROWS = NS * HD
SLOTS = 4


def step_lists():
    def maxima(d, g, us):
        return [(d, "max", g, u) for u in us]

    def both(d, kind, c):
        return [(d, kind, c, which) for which in range(2)]

    def bridge(d, done):
        out = [(d, "v", 0), *both(d, "tr", 0), (d, "v", 1), *both(d, "rest", 0), *both(d, "mid", 0), *both(d, "low", 0)]
        out += [(d, "stack", 0), *done["oT"], (d, "v", 2), *done["onorm"], (d, "stack", 1)]
        out += [(d, "v", 3), (d, "ascore", 0), *done["yt"][:1], (d, "asub", 0), (d, "aexp", 0), *done["yt"][1:2], *done["ylo"][:1]]
        out += done["yt"][2:3] + done["ylo"][1:2] + maxima(d, 0, range(0, 1)) + done["yt"][3:] + done["ylo"][2:3]
        out += maxima(d, 0, range(1, 3)) + done["ylo"][3:]
        out += both(d, "tr", 1) + [(d, "anorm", 0)] + both(d, "rest", 1)
        out += done["proj"][0] + maxima(d, 0, range(3, 5)) + both(d, "mid", 1) + maxima(d, 0, range(5, 6)) + both(d, "low", 1) + done["out"][0]
        out += [(d, "stack", 2)] + maxima(d, 0, range(6, 7)) + done["proj"][1] + maxima(d, 0, range(7, NU)) + done["out"][1]
        out += [(d, "neg", 0)] + maxima(d, 1, range(0, 2)) + done["proj"][2] + [(d, "mrow", 0)] + maxima(d, 1, range(2, 4))
        out += done["out"][2] + maxima(d, 1, range(4, 7)) + done["proj"][3] + maxima(d, 1, range(7, NU)) + done["out"][3]
        return out + [(d, "neg", 1), (d, "stack", 3)]

    nothing = {"oT": [], "onorm": [], "yt": [], "ylo": [], "proj": [[]] * NT, "out": [[]] * NT}
    finish = {
        "oT": [(0, "oT", G - 1)], "onorm": [(0, "onorm", G - 1)], "yt": [(0, "yt", k) for k in range(NK)], "ylo": [(0, "ylo", k) for k in range(NK)],
        "proj": [[(0, "proj", t)] for t in range(NT)], "out": [[(0, "out", t)] for t in range(NT)],
    }
    setup = []
    for i in range(NT):
        setup += [(0, "qk", i), (0, "rope", i)]
        if i == NT - 1:
            setup += [(0, "ak"), (0, "av")]
    setup += bridge(0, nothing)

    extra = {
        (0, 0): [(0, "amix", 0)], (0, 1): [(0, "mrow", 1)], (0, 3): [(0, "aout", 0)],
        (0, 4): [(0, "ascore", 1)], (0, 5): [(0, "asub", 1)], (0, 6): [(0, "aexp", 1), *both(0, "tr", 2)], (0, 7): both(0, "rest", 2),
        (0, 8): [(0, "anorm", 1)], (0, 9): both(0, "mid", 2), (0, 10): both(0, "low", 2),
        (1, 0): [(0, "amix", 1), (0, "stack", 4)], (1, 3): [(0, "aout", 1)], (1, 4): [(0, "ascore", 2)], (1, 5): [(0, "asub", 2)],
        (1, 6): [(0, "aexp", 2)], (1, 8): [(0, "anorm", 2)], (1, 10): [(0, "amix", 2)],
        (2, 0): [(0, "stack", 5)], (2, 3): [(0, "aout", 2)], (2, 7): both(0, "tr", 3), (2, 8): both(0, "rest", 3), (2, 10): both(0, "mid", 3),
        (3, 0): both(0, "low", 3) + [(0, "stack", 6)], (3, 4): [(0, "ascore", 3)], (3, 5): [(0, "asub", 3)], (3, 6): [(0, "aexp", 3)],
        (3, 8): [(0, "anorm", 3)], (4, 0): [(0, "stack", 7)], (4, 3): [(0, "amix", 3)], (4, 6): [(0, "aout", 3)],
    }
    ahead = {
        (0, 0): [(1, "load")], (3, 2): [(1, "stats", 0)], (3, 9): [(1, "stats", 1)], (4, 1): [(1, "stats", 2)], (4, 2): [(1, "stats", 3)],
        (4, 4): [(1, "rstd", 0)], (4, 7): [(1, "rstd", 1)], (4, 8): [(1, "rstd", 2)], (4, 9): [(1, "rstd", 3)],
        (4, 10): [(1, "normal", 0)], (5, 0): [(1, "normal", 1)], (5, 1): [(1, "normal", 2)], (5, 2): [(1, "normal", 3)],
        (5, 6): [(1, "xt", 0)], (5, 7): [(1, "xlo", 0)], (5, 8): [(1, "xt", 1)], (5, 9): [(1, "xlo", 1), (1, "xt", 2)], (5, 10): [(1, "xlo", 2), (1, "xt", 3)],
        (6, 0): [(1, "xlo", 3)],
        (6, 3): [(1, "qk", 0)], (6, 4): [(1, "rope", 0)], (6, 8): [(1, "qk", 1)], (6, 9): [(1, "rope", 1)],
        (7, 3): [(1, "qk", 2)], (7, 4): [(1, "rope", 2)], (7, 8): [(1, "qk", 3)], (7, 9): [(1, "rope", 3)],
    }

    def batch(last):
        out = []
        for g in range(G):
            for u in range(NU):
                out.append((0, "prob", g, u))
                if g + 2 < G:
                    out.append((0, "max", g + 2, u))
                if u == 2 and g:
                    out += [(0, "pv", g - 1, 2), (0, "pv", g - 1, 3)]
                if u == 3 and g and g + 1 < G:
                    out.append((0, "mrow", g + 1))
                if u == 5 and g:
                    out.append((0, "oT", g - 1))
                if u == 5:
                    out.append((0, "pv", g, 0))
                if u == 6 and g:
                    out.append((0, "onorm", g - 1))
                if u == 9:
                    out.append((0, "pv", g, 1))
                out += extra.get((g, u), [])
                out += [step for step in ahead.get((g, u), []) if not last or step[1] not in ("qk", "rope")]
            if g + 2 < G:
                out.append((0, "neg", g + 2))
        out += [(0, "pv", G - 1, 2), (0, "pv", G - 1, 3)]
        if not last:
            return out + bridge(1, finish)
        out += finish["oT"] + finish["onorm"]
        for k in range(NK):
            out += [(0, "yt", k), (0, "ylo", k)]
        for t in range(NT):
            out += [(0, "proj", t), (0, "out", t)]
        return out

    return setup, batch(False), batch(True)


SHARED = ("xt", "ak", "av", "tr", "ascore", "amix", "aout", "mrow", "oT", "yt")


def attention_phase(nc, sh, base, x_src, x_dst, wpT, wte, gating, consts, ffn_weights):
    with ExitStack() as ctx:
        def sb(name, shape, dt=F32):
            return ctx.enter_context(nc.sbuf_tensor(f"at_{name}", shape, dt))

        def sem(name):
            return ctx.enter_context(nc.semaphore(f"at_{name}"))

        w, wp, qk, parts, last_yT = sh.w_qkv, sh.w_proj, sh.qk, sh.parts, sh.last_yT
        xa, xT, res, ident, ln = sh.xa, sh.xT, sh.res, sh.ident, sh.ln
        y = sh.staging[:, 0:4 * C].rearrange("p (t c) -> p t c", t=NT)
        rest = sh.staging[:, 4 * C:6 * C].rearrange("p (w t) -> p w t", w=2)
        v = sb("v", [P, NT, H, HD + 1])
        stacks = sb("stacks", [KROWS + 3, SLOTS, GH, 2, T], BF16)
        q_stack, k_stack = (stacks[:, :, :, which, :] for which in range(2))
        probs = sb("probs", [P, 10 * T])
        o_cols = sb("o_cols", [P, T])
        o_part = sb("o_part", [P, NT, GH, HD])
        rsum = sb("rsum", [P, NT, GH])
        a_prob = sb("a_prob", [P, NT * 8, NA])
        a_max = sb("a_max", [P, NT * 8])
        a_sum = sb("a_sum", [P, NT * 8])
        a_T = sb("a_T", [8 * NA, T])
        ak = sb("ak", [P, 3, NK, 8 * NA], BF16)
        av = sb("av", [8 * NA, C])
        with nc.sbuf_tensor("at_aw", [P, 2, NK, 8 * NA], F32R) as aw:
            pass
        res_late = sb("res_late", [P, 2, C])
        cos = sb("cos", [P, NT, 64])
        sin = sb("sin", [P, NT, 64])
        ident_b = sb("ident_b", [P, P], BF16)
        neg_mask = sb("neg_mask", [P, P], BF16)
        ak_mask = sb("ak_mask", [P, 8])
        gate = sb("gate", [P, 1])
        top = sb("top", [P, NT, GH])
        top_rest = sb("top_rest", [P, NT, GH])
        top_parts = sb("top_parts", [P, NT, 3, GH], BF16)
        top_rows = sb("top_rows", [3 * GH, 2, T], BF16)
        ps = ctx.enter_context(nc.psum_tensor("at_ps", [P, 8, 512], F32))
        SMAX, SPROB, OUT, SH = 0, 3, 5, 6

        starts = [GH * sum(T - P * m for m in range(i)) for i in range(NT)]
        prob = [probs[:, starts[i]:starts[i] + GH * (T - P * i)].rearrange("p (h q) -> p h q", h=GH) for i in range(NT)]
        rope_b = res[:, :, :].rearrange("p i c -> p (i c)")
        raw_wp = probs[:, 0:NK * C].rearrange("p (k c) -> p k c", k=NK)
        raw_aw = rest[:, 0, 0:NK * 8 * NA].rearrange("p (k a) -> p k a", k=NK)
        ak_full = a_prob
        ak_rest = y[:, 0, 0:NK * 8 * NA]
        av_mask = y[0:8 * NA, 1, 0:P]

        s_const, s_masks = sem("const_loaded"), sem("masks")
        s_raw_aw, s_raw_wp = sem("raw_aw_loaded"), sem("raw_wp_loaded")
        s_wp_hi, s_wp_lo, s_aw_hi, s_aw_lo = map(sem, ("wp_hi", "wp_lo", "aw_hi", "aw_lo"))
        s_ak_mm, s_av_mm, s_ak, s_cast, s_zeroed = map(sem, ("ak_mm", "av_mm", "ak_steps", "ident_cast", "out_zeroed"))
        s_x, s_ln, s_norm, s_xt, s_xhi = sh.s_x, sh.s_ln, sh.s_norm, sh.s_tr, sh.s_hi
        s_qk, s_v, s_vcopy = map(sem, ("qk_mm", "v_mm", "v_copied"))
        s_rope, s_turned = sem("rope_terms"), sem("rope_summed")
        s_tr, s_hi, s_mid, s_parts = map(sem, ("qk_transposed", "part_hi", "part_mid", "parts_ready"))
        s_stack = [sem(f"stacked{i}") for i in range(SLOTS)]
        s_smm, s_max = sem("scores_for_max"), sem("unit_max")
        s_top, s_topT = map(sem, ("top_steps", "top_transposed"))
        s_toprow_in = [sem(f"top_row_in{i}") for i in range(2)]
        s_pmm, s_exp, s_causal, s_pv, s_ocopy = map(
            sem, ("scores_for_exp", "exp_done", "causal", "pv_tile", "out_copied"))
        s_oT, s_rsum, s_y = map(sem, ("out_transposed", "row_sum", "y_added"))
        s_amm, s_amax, s_aexp, s_asum, s_ascale, s_anorm = map(
            sem, ("a_scores", "a_max_done", "a_exp", "a_sum_done", "a_scale", "a_norm"))
        s_aT, s_aout = map(sem, ("a_transposed", "a_out"))
        s_yt, s_yhi = map(sem, ("y_transposed", "y_hi"))
        s_proj, s_res = sem("proj"), sem("res_done")
        s_res_in, s_store = [sem(f"res_loaded{t}") for t in range(NT)], sh.s_store
        s_staged = sem("next_weights_staged")
        STORED = base * (NT // 2) * 16
        s_pool_passed, s_sp_passed = sem("pool_passed"), sem("sp_passed")
        s_free = [sem(f"shared_bank_free{i}") for i in range(2)]

        src = x_src.rearrange("(b t p) c -> p b t c", p=P, t=NT)
        dst = x_dst.rearrange("(b t p) c -> p b t c", p=P, t=NT)
        gT, uT = (x.rearrange("(k p) i -> p k i", p=P) for x in ffn_weights[:2])
        wdT = ffn_weights[2]
        setup, middle, end = step_lists()
        order = {id(x): [s for s in x if s[1] in SHARED] for x in (setup, middle, end)}
        assert all(len(order[id(x)]) % 2 == 0 for x in (setup, middle))
        BEFORE, PER_BANK = len(order[id(setup)]) // 2, len(order[id(middle)]) // 2

        def uses_before(b, steps, step):
            start = 0 if steps is setup else BEFORE + b * PER_BANK
            return start + order[id(steps)].index(step) // 2

        def shared(steps, step):
            return ps[:, SH + order[id(steps)].index(step) % 2, :]

        def free(steps, step):
            return s_free[order[id(steps)].index(step) % 2]

        def read(b, steps, step):
            return free(steps, step), uses_before(b, steps, step) + 1

        def over_batches(eng, body):
            body(0, setup)
            body(0, middle)
            with eng.Fori(1, NB - 1) as b:
                body(b, middle)
            body(NB - 1, end)

        def at(b):
            return bass.ds(b, 1)

        def key_unit(g, u):
            i, h, n = KEY_UNITS[u]
            return i, h, n, T - P * i, SPROB + (g * NU + u) % 2

        def qk_bank(steps, t):
            return SPROB if steps is setup and t % 2 else SMAX

        def residual(t):
            return (res if t < 2 else res_late)[:, t % 2, :]

        def yT(steps):
            return last_yT if steps is end else xT

        block = ctx.enter_context(nc.Block())

        @block.sync
        def _(sp):
            sp.dma_start(raw_aw, wte.rearrange("(k p) a -> p k a", p=P)).then_inc(s_raw_aw, 16)
            for tile, name in ((cos, "cos"), (sin, "sin")):
                sp.dma_start(tile[:, :, :], consts[name].rearrange("(t p) c -> p t c", p=P)).then_inc(s_const, 16)
            sp.dma_start(ak_mask[:, :], consts["ak_mask"]).then_inc(s_const, 16)
            sp.dma_start(av_mask, consts["av_mask"]).then_inc(s_const, 16)
            sp.dma_start(raw_wp, wpT.rearrange("(k p) c -> p k c", p=P)).then_inc(s_raw_wp, 16)
            sp.dma_start(gate[:, :], gating.partition_broadcast(P)).then_inc(s_const, 16)

            def body(b0, steps):
                for step in steps:
                    ahead, kind, *a = step
                    b = b0 + ahead
                    if kind == "load":
                        sp.wait_ge(s_xt, (base + b) * NK)
                        if steps is end:
                            sp.dma_start(xa[:, :, :], dst[:, 0, :, :]).then_inc(s_x, 16)
                        else:
                            for i in range(2):
                                sp.wait_ge(s_store[i], STORED)
                            sp.dma_start(xa[:, :, :], src[:, at(b), :, :]).then_inc(s_x, 16)
                    if kind == "stack":
                        g, = a
                        c, half, slot = g // 2, g % 2, g % SLOTS
                        done = b * (G * NU) + (g - SLOTS + 1) * NU
                        sp.wait_ge(s_parts, 2 * (b * NK + c + 1))
                        sp.sem_inc(s_sp_passed, 1)
                        wait(sp, s_pmm, done)
                        own = slice(half * 64, half * 64 + 64)
                        for r in range(NS):
                            to = slice(r * HD, (r + 1) * HD)
                            of_q, of_k = PART_Q[r], 3 + PART_K[r]
                            sp.dma_start(stacks[to, slot, :, :, :],
                                         parts[own, :, :, :].rearrange("p w i t -> p (w i) t")[:, of_q:of_k + 1:of_k - of_q, :]
                                         ).then_inc(s_stack[slot], 16)
                    if kind == "yt" and a[0] == 0:
                        sp.wait_ge(s_turned, NB * NT if steps is end else (b + 2) * NT)
                        for i in range(2):
                            wait(sp, s_store[i], STORED + b * (NT // 2) * 16)
                        for t in range(NT):
                            sp.dma_start(residual(t), src[:, at(b), t, :]).then_inc(s_res_in[t], 16)
                    if kind == "out":
                        t, = a
                        if steps is end and t == 0:
                            sp.wait_ge(s_yt, NB * NK)
                            sp.wait_ge(s_y, NB * G)
                            for j in range(2):
                                load_raw_gate_up(sp, sh.raw_gate_up(), gT, uT, j, [s_staged] * 2)
                                load_raw_down(sp, sh.raw_down(), wdT, j, [s_staged] * 2)
                        sp.wait_ge(s_res, b * NT + t + 1)
                        sp.dma_start(dst[:, at(b), t, :], residual(t)).then_inc(s_store[t % 2], 16)

            over_batches(sp, body)
            sp.wait_ge(s_staged, 2 * 3 * 16)

        @block.tensor
        def _(pe):
            def three(out, lhsT, rhs, start, stop):
                pe.matmul(out, lhsT(HI), rhs(HI), start=start, stop=False)
                pe.matmul(out, lhsT(HI), rhs(LO), start=False, stop=False)
                return pe.matmul(out, lhsT(LO), rhs(HI), start=False, stop=stop)

            def body(b0, steps):
                def take(step):
                    wait(pe, free(steps, step), uses_before(b0, steps, step))
                    return shared(steps, step)

                for step in steps:
                    ahead, kind, *a = step
                    b = b0 + ahead
                    if kind == "xt":
                        k, = a
                        out = take(step)
                        pe.wait_ge(s_norm, (base + b + 1) * NT)
                        for t in range(NT):
                            mm = pe.transpose(out[:, t * P:(t + 1) * P], xa[:, t, k * P:(k + 1) * P], ident[:, :])
                        mm.then_inc(s_xt, 1)
                    if kind == "ak":
                        out = take(step)
                        pe.wait_ge(s_aw_lo, 1)
                        for c in range(NK):
                            for k in range(NK):
                                mm = three(out[:, c * NA:(c + 1) * NA], lambda part: w[:, part, k, C + c * P:C + (c + 1) * P],
                                           lambda part: aw[:, part, k, 0:NA], k == 0, k == NK - 1)
                        mm.then_inc(s_ak_mm, 1)
                    if kind == "av":
                        out = take(step)
                        for k in range(NK):
                            mm = three(out[0:8 * NA, :], lambda part: aw[:, part, k, :],
                                       lambda part: w[:, part, k, 2 * C:3 * C], k == 0, k == NK - 1)
                        mm.then_inc(s_av_mm, 1)
                    if kind == "qk":
                        t, = a
                        if t == 0:
                            if steps is not setup:
                                for k in (NK - 2, NK - 1):
                                    pe.wait_ge(*read(b0, steps, (ahead, "xt", k)))
                            wait(pe, s_max, b * G * NU)
                        elif steps is not setup or t >= 2:
                            pe.wait_ge(s_rope, (t - 1 if steps is setup else b * NT + t) * 3)
                        for part in range(2):
                            for k in range(NK):
                                mm = three(ps[:, qk_bank(steps, t) + part, :], lambda x: xT[:, x, k, t * P:(t + 1) * P],
                                           lambda x: w[:, x, k, part * C:(part + 1) * C], k == 0, k == NK - 1)
                        mm.then_inc(s_qk, 1)
                    if kind == "v":
                        t, = a
                        if steps is setup and t == 0:
                            pe.wait_ge(s_rope, NT * 3)
                        elif t == 0:
                            wait(pe, s_exp, b * G * NU)
                        if t >= 2:
                            pe.wait_ge(s_vcopy, b * NT + t - 1)
                        for k in range(NK):
                            mm = three(ps[:, SPROB + t % 2, :], lambda x: xT[:, x, k, t * P:(t + 1) * P],
                                       lambda x: w[:, x, k, 2 * C:3 * C], k == 0, k == NK - 1)
                        mm.then_inc(s_v, 1)
                    if kind == "tr":
                        c, which = a
                        out = take(step)
                        pe.wait_ge(s_turned, (b + 1) * NT)
                        for t in range(NT):
                            at_ = which * C + c * P
                            mm = pe.transpose(out[:, t * P:(t + 1) * P], qk[:, t, at_:at_ + P], ident[:, :])
                        mm.then_inc(s_tr, 1)
                    if kind == "ascore":
                        c, = a
                        out = take(step)
                        if steps is setup:
                            pe.wait_ge(s_ak, 4)
                        pe.wait_ge(s_parts, 2 * (b * NK + c + 1))
                        for t in range(NT):
                            for r in range(NS):
                                mm = pe.matmul(out[:, t * 8 * NA:(t + 1) * 8 * NA], parts[:, 0, PART_Q[r], t * P:(t + 1) * P],
                                               ak[:, PART_K[r], c, :], start=(r == 0), stop=(r == NS - 1))
                        mm.then_inc(s_amm, 1)
                    if kind == "amix":
                        c, = a
                        out = take(step)
                        pe.wait_ge(s_anorm, b * NK + c + 1)
                        for t in range(NT):
                            mm = pe.transpose(out[0:8 * NA, t * P:(t + 1) * P],
                                              a_prob[:, 8 * t:8 * t + 8, :].rearrange("p h a -> p (h a)"), ident[:, :])
                        mm.then_inc(s_aT, 1)
                    if kind == "aout":
                        c, = a
                        out = take(step)
                        pe.wait_ge(*read(b0, steps, (ahead, "amix", c)))
                        for t in range(NT):
                            mm = pe.matmul(out[:, t * P:(t + 1) * P], a_T[:, t * P:(t + 1) * P], av[:, c * P:(c + 1) * P],
                                           start=True, stop=True)
                        mm.then_inc(s_aout, 1)
                    if kind == "max":
                        g, u = a
                        t, h0, nh = UNITS[u]
                        n, slot = b * G + g, g % SLOTS
                        bank = SMAX + (g * NU + u) % 3
                        if steps is setup and g == 0 and u == 0:
                            pe.wait_ge(s_masks, 3)
                            pe.wait_ge(s_cast, 1)
                        if g == 0 and u == 0:
                            pe.wait_ge(s_rope, (b + 1) * NT * 3)
                        wait(pe, s_max, n * NU + u - 2)
                        if u == 0:
                            pe.wait_ge(s_stack[slot], (b * (G // SLOTS) + g // SLOTS + 1) * NS * 16)
                        m = P * (t + 1)
                        for h in range(h0, h0 + nh):
                            out = ps[:, bank, (h - h0) * m:(h - h0 + 1) * m]
                            pe.matmul(out, q_stack[0:KROWS, slot, h, t * P:(t + 1) * P], k_stack[0:KROWS, slot, h, 0:m],
                                      start=True, stop=False)
                            mm = pe.matmul(out[:, t * P:m], ident_b[:, :], neg_mask[:, :], start=False, stop=True)
                        mm.then_inc(s_smm, 1)
                    if kind == "mrow":
                        g, = a
                        out = take(step)
                        pe.wait_ge(s_top, (b * G + g + 1) * 4)
                        rows_ps = out[0:3 * GH, 0:T // 2].bitcast(BF16)
                        for t in range(NT):
                            mm = pe.transpose(rows_ps[:, t * P:(t + 1) * P],
                                              top_parts[:, t, :, :].rearrange("p s h -> p (s h)"), ident_b[:, :])
                        mm.then_inc(s_topT, 1)
                    if kind == "prob":
                        g, u = a
                        i, h0, nh, m, bank = key_unit(g, u)
                        n, slot = b * G + g, g % SLOTS
                        if g == 0 and u == 0:
                            pe.wait_ge(s_vcopy, (b + 1) * NT)
                            if isinstance(b, int) and b == 0:
                                pe.wait_ge(s_masks, 4)
                        if g == 0 and u < 2:
                            wait(pe, s_res, b * NT - 1 + u)
                        wait(pe, s_exp, n * NU + u - 1)
                        if u == 0:
                            pe.wait_ge(s_toprow_in[g % 2], (b * (G // 2) + g // 2 + 1) * 16)
                        for h in range(h0, h0 + nh):
                            mm = pe.matmul(ps[:, bank, (h - h0) * m:(h - h0 + 1) * m],
                                           k_stack[:, slot, h, i * P:(i + 1) * P], q_stack[:, slot, h, i * P:T],
                                           start=True, stop=True)
                        mm.then_inc(s_pmm, 1)
                    if kind == "pv":
                        g, i = a
                        n = b * G + g
                        pe.wait_ge(s_causal, n * NT + i + 1)
                        if i == 0:
                            wait(pe, s_ocopy, n)
                            if isinstance(b, int) and b == 0 and g == 0:
                                pe.wait_ge(s_zeroed, 1)
                        for h in range(GH):
                            mm = pe.matmul(ps[32 * h:32 * h + HD + 1, OUT, i * P:T], v[:, i, g * GH + h, :], prob[i][:, h, :],
                                           start=(i == 0), stop=(i == NT - 1))
                        mm.then_inc(s_pv, 1)
                    if kind == "oT":
                        g, = a
                        out = take(step)
                        pe.wait_ge(s_ocopy, b * G + g + 1)
                        for t in range(NT):
                            mm = pe.transpose(out[:, t * P:(t + 1) * P], o_cols[:, t * P:(t + 1) * P], ident[:, :])
                        mm.then_inc(s_oT, 1)
                    if kind == "yt":
                        k, = a
                        out = take(step)
                        pe.wait_ge(s_y, b * G + 2 * k + 2)
                        for t in range(NT):
                            mm = pe.transpose(out[:, t * P:(t + 1) * P], y[:, t, k * P:(k + 1) * P], ident[:, :])
                        mm.then_inc(s_yt, 1)
                    if kind == "proj":
                        t, = a
                        if isinstance(b, int) and b == 0 and t == 0:
                            pe.wait_ge(s_wp_lo, 1)
                        if t == 0:
                            for k in (NK - 2, NK - 1):
                                pe.wait_ge(*read(b0, steps, (0, "yt", k)))
                            if steps is end:
                                pe.wait_ge(s_exp, NB * G * NU)
                        if t < 2 and steps is not end:
                            pe.wait_ge(s_vcopy, (b + 1) * NT + t + 3)
                        if t >= 2:
                            pe.wait_ge(s_res, b * NT + t - 1)
                        for k in range(NK):
                            mm = three(ps[:, SPROB + t % 2, :], lambda x: yT(steps)[:, x, k, t * P:(t + 1) * P],
                                       lambda x: wp[:, x, k, :], k == 0, k == NK - 1)
                        mm.then_inc(s_proj, 1)

            over_batches(pe, body)

        @block.scalar
        def _(act):
            act.wait_ge(s_raw_aw, 16)
            act.activation(aw[:, HI, :, :], raw_aw, ACT.Copy).then_inc(s_aw_hi, 1)

            def body(b0, steps):
                for step in steps:
                    ahead, kind, *a = step
                    b = b0 + ahead
                    if kind == "xt":
                        k, = a
                        act.wait_ge(s_xt, (base + b) * NK + k + 1)
                        act.activation(xT[:, HI, k, :], shared(steps, step), ACT.Copy).then_inc(s_xhi, 1)
                    if kind == "ak":
                        act.wait_ge(s_raw_wp, 16)
                        act.activation(wp[:, HI, :, :], raw_wp, ACT.Copy).then_inc(s_wp_hi, 1)
                    if kind == "v":
                        t, = a
                        act.wait_ge(s_v, b * NT + t + 1)
                        act.activation(v[:, t, :, 0:HD], ps[:, SPROB + t % 2, :].rearrange("p (h d) -> p h d", h=H), ACT.Copy).then_inc(s_vcopy, 1)
                    if kind == "tr":
                        c, which = a
                        n = 2 * (b * NK + c) + which
                        act.wait_ge(s_tr, n + 1)
                        if which == 0:
                            last_b, last = (b, 2 * c) if c else (b - 1, G)
                            for g in (last - 2, last - 1):
                                wait(act, s_stack[g % SLOTS], (last_b * (G // SLOTS) + g // SLOTS + 1) * NS * 16)
                            wait(act, s_amm, b * NK + c)
                        act.activation(parts[:, which, 0, :], shared(steps, step), ACT.Copy).then_inc(s_hi, 1)
                    if kind == "mid":
                        c, which = a
                        act.wait_ge(*read(b0, steps, (ahead, "tr", c, which)))
                        act.activation(parts[:, which, 1, :], rest[:, which, :], ACT.Copy).then_inc(s_mid, 1)
                    if kind == "amix":
                        c, = a
                        act.wait_ge(s_aT, b * NK + c + 1)
                        act.activation(a_T[:, :], shared(steps, step)[0:8 * NA, :], ACT.Copy).then_inc(free(steps, step), 1)
                    if kind == "aexp":
                        c, = a
                        act.wait_ge(*read(b0, steps, (ahead, "ascore", c)))
                        act.activation(a_prob[:, :, :], a_prob[:, :, :], ACT.Exp, scale=float(1.0 / np.sqrt(np.float32(C)))).then_inc(s_aexp, 1)
                    if kind == "aout":
                        c, = a
                        act.wait_ge(s_aout, b * NK + c + 1)
                        act.activation(y[:, :, c * P:(c + 1) * P], shared(steps, step).rearrange("p (t c) -> p t c", t=NT), ACT.Copy).then_inc(free(steps, step), 1)
                    if kind == "mrow":
                        g, = a
                        n = b * G + g
                        act.wait_ge(s_topT, n + 1)
                        wait(act, s_toprow_in[g % 2], (b * (G // 2) + g // 2) * 16)
                        act.activation(top_rows[:, g % 2, :], shared(steps, step)[0:3 * GH, 0:T // 2].bitcast(BF16), ACT.Copy).then_inc(free(steps, step), 1)
                        act.wait_ge(*read(b0, steps, step))
                        act.dma_start(q_stack[KROWS:KROWS + 3, g % SLOTS, :, :], top_rows[:, g % 2, :]).then_inc(s_toprow_in[g % 2], 16)
                    if kind == "prob":
                        g, u = a
                        i, h0, nh, m, bank = key_unit(g, u)
                        n = b * G + g
                        if isinstance(b, int) and b == 0 and g == 0 and u == 0:
                            act.wait_ge(s_wp_lo, 1)
                        act.wait_ge(s_pmm, n * NU + u + 1)
                        wait(act, s_pv, (n - 1) * NT + i + 1)
                        act.activation(prob[i][:, h0:h0 + nh, :], ps[:, bank, 0:nh * m].rearrange("p (h q) -> p h q", h=nh),
                                       ACT.Exp, scale=HD ** -0.5).then_inc(s_exp, 1)
                    if kind == "pv" and a[1] == NT - 1:
                        g = a[0]
                        n = b * G + g
                        act.wait_ge(s_pv, (n + 1) * NT)
                        wait(act, s_oT, n)
                        act.activation(o_cols[:, :], ps[:, OUT, :], ACT.Copy).then_inc(s_ocopy, 1)
                    if kind == "yt":
                        k, = a
                        act.wait_ge(s_yt, b * NK + k + 1)
                        act.activation(yT(steps)[:, HI, k, :], shared(steps, step), ACT.Copy).then_inc(s_yhi, 1)

            over_batches(act, body)

        @block.gpsimd
        def _(pool):
            pool.memset(v[:, :, :, HD:HD + 1], 1.0).then_inc(s_masks, 1)
            pool.wait_ge(s_masks, 1)
            pool.memset(neg_mask[:, :], 0.0).then_inc(s_masks, 1)
            pool.wait_ge(s_masks, 2)
            pool.affine_select(neg_mask[:, :], neg_mask[:, :], pattern=[[-1, P]], compare_op=ALU.is_ge,
                               fill=-3e38, base=0, channel_multiplier=1).then_inc(s_masks, 1)
            pool.wait_ge(s_masks, 3)
            pool.wait_ge(s_aw_hi, 1)
            pool.tensor_tensor(aw[:, LO, :, :], raw_aw, aw[:, HI, :, :].bitcast(F32), ALU.subtract).then_inc(s_aw_lo, 1)
            pool.wait_ge(s_aw_lo, 1)
            pool.memset(k_stack[KROWS:KROWS + 3, :, :, :], 1.0).then_inc(s_masks, 1)
            pool.wait_ge(s_masks, 4)
            pool.wait_ge(s_wp_hi, 1)
            pool.tensor_tensor(wp[:, LO, :, :], raw_wp, wp[:, HI, :, :].bitcast(F32), ALU.subtract).then_inc(s_wp_lo, 1)

            def body(b0, steps):
                for step in steps:
                    ahead, kind, *a = step
                    b = b0 + ahead
                    if kind == "prob":
                        g, u = a
                        i = KEY_UNITS[u][0]
                        if u == NU - 1 or KEY_UNITS[u + 1][0] != i:
                            n = b * G + g
                            pool.wait_ge(s_exp, n * NU + u + 1)
                            pool.sem_inc(s_pool_passed, 1)
                            own = prob[i][:, :, 0:P]
                            pool.affine_select(own, own, pattern=[[0, GH], [1, P]], compare_op=ALU.is_ge, fill=0.0,
                                               base=0, channel_multiplier=-1).then_inc(s_causal, 1)

            over_batches(pool, body)

        @block.vector
        def _(dve):
            dve.memset(ps[:, OUT, :], 0.0).then_inc(s_zeroed, 1)

            def wide(x):
                return x[:, :].rearrange("p (h o) -> p h o", o=1).broadcast_to([P, NT * 8, NA])

            def adapter_keys(out):
                dve.wait_ge(s_ak_mm, 1)
                for c in range(NK):
                    ins = dve.tensor_tensor(
                        ak_full[:, 8 * c:8 * c + 8, :],
                        out[:, c * NA:(c + 1) * NA].rearrange("p (o a) -> p o a", o=1).broadcast_to([P, 8, NA]),
                        ak_mask[:, :].rearrange("p (h o) -> p h o", o=1).broadcast_to([P, 8, NA]), ALU.mult)
                return ins

            def cut_adapter_keys():
                flat = ak_full[:, :, :].rearrange("p h a -> p (h a)")

                def ak_part(i):
                    return ak[:, i, :, :].rearrange("p c a -> p (c a)")

                dve.tensor_copy(ak_part(0), flat).then_inc(s_ak, 1)
                dve.wait_ge(s_ak, 1)
                dve.tensor_tensor(ak_rest, flat, ak_part(0), ALU.subtract).then_inc(s_ak, 1)
                dve.wait_ge(s_ak, 2)
                dve.tensor_copy(ak_part(1), ak_rest).then_inc(s_ak, 1)
                dve.wait_ge(s_ak, 3)
                dve.tensor_tensor(ak_part(2), ak_rest, ak_part(1), ALU.subtract).then_inc(s_ak, 1)

            def body(b0, steps):
                for step in steps:
                    ahead, kind, *a = step
                    b = b0 + ahead
                    if kind == "stats":
                        if a[0] == 0:
                            dve.wait_ge(s_x, (base + b) * 16)
                        row_statistics(dve, xa, ln, a[0]).then_inc(s_ln, 1)
                    if kind == "rstd":
                        inverse_deviation(dve, ln, s_ln, (base + b) * (NT + LN_STEPS) + NT, a)
                    if kind == "normal":
                        dve.wait_ge(s_ln, (base + b + 1) * (NT + LN_STEPS))
                        normalise_tile(dve, xa, ln, a[0]).then_inc(s_norm, 1)
                    if kind == "ak":
                        dve.wait_ge(s_const, 5 * 16)
                        adapter_keys(shared(steps, step)).then_inc(free(steps, step), 1)
                        dve.wait_ge(*read(b0, steps, step))
                        cut_adapter_keys()
                    if kind == "av":
                        dve.tensor_copy(ident_b[:, :], ident[:, :]).then_inc(s_cast, 1)
                        dve.wait_ge(s_av_mm, 1)
                        dve.tensor_tensor(av[:, :].rearrange("p (c d) -> p c d", c=NK), shared(steps, step)[0:8 * NA, :].rearrange("p (c d) -> p c d", c=NK),
                                          av_mask.rearrange("p (o d) -> p o d", o=1).broadcast_to([8 * NA, NK, P]),
                                          ALU.mult).then_inc(free(steps, step), 1)
                    if kind == "xlo":
                        k, = a
                        xt = (ahead, "xt", k)
                        dve.wait_ge(s_xhi, (base + b) * NK + k + 1)
                        dve.tensor_tensor(xT[:, LO, k, :], shared(steps, xt), xT[:, HI, k, :].bitcast(F32),
                                          ALU.subtract).then_inc(free(steps, xt), 1)
                    if kind == "rope":
                        t, = a
                        n = b * NT + t
                        dve.wait_ge(s_qk, n + 1)
                        if t == 0:
                            for i in range(2):
                                dve.wait_ge(s_store[i], STORED + (0 if steps is setup else (b - 1) * (NT // 2) * 16))
                        if steps is setup:
                            dve.wait_ge(s_const, 5 * 16)
                        wait(dve, s_turned, n)
                        bank = qk_bank(steps, t)
                        both = ps[:, bank:bank + 2, :].rearrange("p w (g c) -> p (w g) c", c=64)
                        ra, rb = (x.rearrange("p (g c) -> p g c", c=64) for x in (qk[:, t, :], rope_b))

                        def table(x, lo, hi):
                            return x[:, t, lo:hi].rearrange("p (o c) -> p o c", o=1).broadcast_to([P, 2 * G, hi - lo])

                        dve.tensor_tensor(ra, both, table(cos, 0, 64), ALU.mult).then_inc(s_rope, 1)
                        dve.tensor_tensor(rb[:, :, 0:32], both[:, :, 32:64], table(sin, 0, 32), ALU.mult).then_inc(s_rope, 1)
                        dve.tensor_tensor(rb[:, :, 32:64], both[:, :, 0:32], table(sin, 32, 64), ALU.mult).then_inc(s_rope, 1)
                        dve.wait_ge(s_rope, (n + 1) * 3)
                        dve.tensor_tensor(qk[:, t, :], qk[:, t, :], rope_b, ALU.add).then_inc(s_turned, 1)
                    if kind == "rest":
                        c, which = a
                        n = 2 * (b * NK + c) + which
                        tr = (ahead, "tr", c, which)
                        dve.wait_ge(s_hi, n + 1)
                        dve.tensor_tensor(rest[:, which, :], shared(steps, tr), parts[:, which, 0, :], ALU.subtract).then_inc(free(steps, tr), 1)
                    if kind == "low":
                        c, which = a
                        n = 2 * (b * NK + c) + which
                        dve.wait_ge(s_mid, n + 1)
                        dve.tensor_tensor(parts[:, which, 2, :], rest[:, which, :], parts[:, which, 1, :], ALU.subtract).then_inc(s_parts, 1)
                    if kind == "max":
                        g, u = a
                        t, h0, nh = UNITS[u]
                        n, m = b * G + g, P * (t + 1)
                        bank = SMAX + (g * NU + u) % 3
                        dve.wait_ge(s_smm, n * NU + u + 1)
                        dve.tensor_reduce(top[:, t, h0:h0 + nh], ps[:, bank, 0:nh * m].rearrange("p (h k) -> p h k", h=nh),
                                          AX, ALU.max).then_inc(s_max, 1)
                    if kind == "neg":
                        g, = a
                        n = b * G + g
                        dve.wait_ge(s_max, (n + 1) * NU)
                        wait(dve, s_topT, n)
                        hi, mid, lo = (top_parts[:, :, i, :] for i in range(3))
                        dve.tensor_scalar(hi, top[:, :, :], -1.0, None, ALU.mult).then_inc(s_top, 1)
                        dve.wait_ge(s_top, 4 * n + 1)
                        dve.scalar_tensor_tensor(out=top_rest[:, :, :], in0=top[:, :, :], scalar=-1.0, in1=hi,
                                                 op0=ALU.mult, op1=ALU.subtract).then_inc(s_top, 1)
                        dve.wait_ge(s_top, 4 * n + 2)
                        dve.tensor_copy(mid, top_rest[:, :, :]).then_inc(s_top, 1)
                        dve.wait_ge(s_top, 4 * n + 3)
                        dve.tensor_tensor(lo, top_rest[:, :, :], mid, ALU.subtract).then_inc(s_top, 1)
                    if kind == "asub":
                        c, = a
                        n = b * NK + c
                        ascore = (ahead, "ascore", c)
                        s = shared(steps, ascore)[:, 0:NT * 8 * NA].rearrange("p (h a) -> p h a", a=NA)

                        dve.wait_ge(s_amm, n + 1)
                        wait(dve, s_aT, n)
                        dve.tensor_reduce(a_max[:, :], s, AX, ALU.max).then_inc(s_amax, 1)
                        dve.wait_ge(s_amax, n + 1)
                        dve.tensor_tensor(a_prob[:, :, :], s, wide(a_max), ALU.subtract).then_inc(free(steps, ascore), 1)
                    if kind == "anorm":
                        n = b * NK + a[0]
                        dve.wait_ge(s_aexp, n + 1)
                        dve.tensor_reduce(a_sum[:, :], a_prob[:, :, :], AX, ALU.add).then_inc(s_asum, 1)
                        dve.wait_ge(s_asum, n + 1)
                        dve.reciprocal(a_sum[:, :], a_sum[:, :]).then_inc(s_ascale, 1)
                        dve.wait_ge(s_ascale, 2 * n + 1)
                        dve.tensor_scalar(a_sum[:, :], a_sum[:, :], gate[:, 0:1], None, ALU.mult).then_inc(s_ascale, 1)
                        dve.wait_ge(s_ascale, 2 * n + 2)
                        dve.tensor_tensor(a_prob[:, :, :], a_prob[:, :, :], wide(a_sum), ALU.mult).then_inc(s_anorm, 1)
                    if kind == "onorm":
                        g, = a
                        n = b * G + g
                        oT = (ahead, "oT", g)
                        s = shared(steps, oT).rearrange("p (t h c) -> p t h c", t=NT, h=GH)
                        dve.wait_ge(s_oT, n + 1)
                        dve.reciprocal(rsum[:, :, :], s[:, :, :, HD]).then_inc(s_rsum, 1)
                        dve.wait_ge(s_rsum, n + 1)
                        dve.tensor_tensor(o_part[:, :, :, :], s[:, :, :, 0:HD],
                                          rsum[:, :, :].rearrange("p t (h o) -> p t h o", o=1).broadcast_to([P, NT, GH, HD]),
                                          ALU.mult).then_inc(free(steps, oT), 1)
                        dve.wait_ge(*read(b0, steps, oT))
                        own = y[:, :, g * GH * HD:(g + 1) * GH * HD]
                        dve.wait_ge(*read(b0, steps, (ahead, "aout", g // 2)))
                        dve.tensor_tensor(own, own, o_part[:, :, :, :].rearrange("p t h d -> p t (h d)"), ALU.add).then_inc(s_y, 1)
                    if kind == "ylo":
                        k, = a
                        yt = (ahead, "yt", k)
                        dve.wait_ge(s_yhi, b * NK + k + 1)
                        dve.tensor_tensor(yT(steps)[:, LO, k, :], shared(steps, yt), yT(steps)[:, HI, k, :].bitcast(F32),
                                          ALU.subtract).then_inc(free(steps, yt), 1)
                    if kind == "out":
                        t, = a
                        n = b * NT + t
                        dve.wait_ge(s_proj, n + 1)
                        dve.wait_ge(s_res_in[t], (b + 1) * 16)
                        dve.tensor_tensor(residual(t), ps[:, SPROB + t % 2, :], residual(t), ALU.add).then_inc(s_res, 1)

            over_batches(dve, body)


def macaron(nc, x, w_qkvT, w_projT, wte, gating, w_gateT, w_upT, w_downT, cos, sin, ident, ak_mask, av_mask, out):
    h1 = nc.dram_tensor("h1", [NB * T, C], F32).ap()
    h2 = nc.dram_tensor("h2", [NB * T, C], F32).ap()
    consts = {"cos": cos, "sin": sin, "ak_mask": ak_mask, "av_mask": av_mask}
    ffn_weights = (w_gateT, w_upT, w_downT)
    with ExitStack() as ctx:
        sh = Shared(nc, ctx)
        ffn_phase(nc, sh, "f1", 0, x, h1, *ffn_weights, ident, wqkvT=w_qkvT)
        attention_phase(nc, sh, NB, h1, h2, w_projT, wte, gating, consts, ffn_weights)
        ffn_phase(nc, sh, "f2", 2 * NB, h2, out, *ffn_weights, ident)


def shape_constants():
    theta = np.float32(1.0) / np.power(np.float32(10000.0), np.arange(0, HD, 2, dtype=np.float32) / np.float32(HD))
    angle = np.outer(np.arange(T, dtype=np.float32), theta.astype(np.float32)).astype(np.float32)
    cos, sin = np.cos(angle), np.sin(angle)
    head_of_row = np.arange(P) // 64 * GH + np.arange(P) % GH
    head_of_pair = np.arange(8 * NA) // NA
    return {
        "cos": np.repeat(np.concatenate([cos, cos], 1), GH, axis=1),
        "sin": np.repeat(np.concatenate([-sin, sin], 1), GH, axis=1),
        "ident": np.eye(P, dtype=np.float32),
        "ak_mask": (head_of_row[:, None] == np.arange(8)).astype(np.float32),
        "av_mask": (head_of_pair[:, None] == np.arange(P) // HD).astype(np.float32),
    }


_NAMES = ["x", "w_qkvT", "w_projT", "wte", "gating", "w_gateT", "w_upT", "w_downT", "cos", "sin", "ident", "ak_mask", "av_mask"]


def lay_out(x, w_attn, w_proj, adapter_wte, gating, w_gate, w_up, w_down):
    qk = w_attn[:2 * C].reshape(2, G, GH, HD, C).transpose(0, 1, 3, 2, 4).reshape(2 * C, C)
    arrays = {
        "x": x.reshape(NB * T, C), "w_qkvT": np.concatenate([qk, w_attn[2 * C:]]).T, "w_projT": w_proj.T,
        "wte": np.tile(adapter_wte.T, (1, 8)), "gating": gating, "w_gateT": w_gate.T, "w_upT": w_up.T, "w_downT": w_down.T,
    }
    arrays.update(shape_constants())
    return {name: np.ascontiguousarray(arrays[name]) for name in _NAMES}


def kernel(L0_attn_x, L0_attn_w_attn, L0_attn_w_proj, L0_attn_adapter_wte, L0_attn_gating,
           L0_ffn_w_gate, L0_ffn_w_up, L0_ffn_w_down):
    import concourse.bacc as _bacc
    from concourse import mybir as _mybir
    from concourse.bass_utils import run_bass_kernel_spmd as _run

    arrays = lay_out(*(np.asarray(a) for a in (
        L0_attn_x, L0_attn_w_attn, L0_attn_w_proj, L0_attn_adapter_wte, L0_attn_gating,
        L0_ffn_w_gate, L0_ffn_w_up, L0_ffn_w_down)))
    nc = _bacc.Bacc("TRN2", target_bir_lowering=False, num_devices=1)
    args = [nc.dram_tensor(f"in_{n}", arrays[n].shape, _mybir.dt.from_np(arrays[n].dtype), kind="ExternalInput").ap()
            for n in _NAMES]
    out = nc.dram_tensor("out_y", [NB * T, C], _mybir.dt.float32, kind="ExternalOutput").ap()
    macaron(nc, *args, out)
    r = _run(nc, [{f"in_{n}": arrays[n] for n in _NAMES}], core_ids=[0])
    return r.results[0]["out_y"].reshape(NB, T, C)
```
